# Optimizing a Trainium2 kernel written in Bass

```python
import numpy as np
import jax
import jax.numpy as jnp

def _softmax(x, axis=-1):
    return jax.nn.softmax(x, axis=axis)

def _gelu(x):
    return jax.nn.gelu(x, approximate=True)

def _silu(x):
    return jax.nn.silu(x)

def _sigmoid(x):
    return jax.nn.sigmoid(x)

def _layernorm(x, axis=-1, eps=1e-05):
    m = jnp.mean(x, axis=axis, keepdims=True)
    v = jnp.var(x, axis=axis, keepdims=True)
    return (x - m) / jnp.sqrt(v + eps)

def _scatter_add(tgt, idx, src, axis=0):
    return tgt.at[idx].add(src)

def _segment_sum(src, seg, n):
    return jax.ops.segment_sum(src, seg, n)
kernel_name = 'mk_gnn_preln_d4_gnn_r64_870516'

def setup_inputs(seed: int=0):
    np.random.seed(seed)
    _w = jnp.asarray

    def _rec_inputs():
        import jax
        import jax.numpy as jnp
        _gk = jax.random.key(seed)
        x = -0.0003713 + 1 * jax.random.normal(jax.random.fold_in(_gk, 1), (50000, 256), jnp.float32)
        src = jax.random.randint(jax.random.fold_in(_gk, 2), (25000,), 0, 50000, jnp.int32)
        dst = jnp.minimum((50000 * jax.random.uniform(jax.random.fold_in(_gk, 3), (25000,)) ** 2.0).astype(jnp.int32), 49999)
        _o = jnp.argsort(dst, stable=True)
        src = src[_o]
        dst = dst[_o]
        edge_weight = jax.random.uniform(jax.random.fold_in(_gk, 13), (25000,), jnp.float32, 0.0, 0.999998)
        return (x, src, dst, edge_weight)
    x, src, dst, edge_weight = _rec_inputs()

    def _L0_gnn_setup():
        import jax, jax.numpy as jnp
        import numpy as np
        N = 50000
        E = 12500
        D = 256
        H1, C1 = (4, 64)
        H2, C2 = (4, 64)
        NEG_SLOPE = 0.2

        def _gat_layer(x, src, dst, W, a_src, a_dst, b, n, h, c):
            feat = (x @ W).reshape(n, h, c)
            al_s = jnp.einsum('nhc,hc->nh', feat, a_src)
            al_d = jnp.einsum('nhc,hc->nh', feat, a_dst)
            e = al_s[src] + al_d[dst]
            e = jnp.where(e > 0, e, NEG_SLOPE * e)
            m = jax.ops.segment_max(e, dst, num_segments=n)
            ee = jnp.exp(e - m[dst])
            s = jax.ops.segment_sum(ee, dst, num_segments=n)
            alpha = ee / (s[dst] + 1e-16)
            out = jax.ops.segment_sum(alpha[:, :, None] * feat[src], dst, num_segments=n)
            return out.reshape(n, h * c) + b
        key = jax.random.key(seed)
        ks = jax.random.split(key, 10)

        def glorot(k, shape, fan):
            return jax.random.normal(k, shape, jnp.float32) * (1.0 / np.sqrt(fan))
        x = jax.random.normal(ks[0], (N, D), jnp.float32)
        edge_index = jax.random.randint(ks[1], (2, E), 0, N, dtype=jnp.int32)
        W1 = glorot(ks[2], (D, H1 * C1), D)
        a_src1 = glorot(ks[3], (H1, C1), C1)
        a_dst1 = glorot(ks[4], (H1, C1), C1)
        b1 = jnp.zeros((H1 * C1,), jnp.float32)
        W2 = glorot(ks[5], (H1 * C1, H2 * C2), H1 * C1)
        a_src2 = glorot(ks[6], (H2, C2), C2)
        a_dst2 = glorot(ks[7], (H2, C2), C2)
        b2 = jnp.zeros((H2 * C2,), jnp.float32)
        return {'x': x, 'edge_index': edge_index, 'W1': W1, 'a_src1': a_src1, 'a_dst1': a_dst1, 'b1': b1, 'W2': W2, 'a_src2': a_src2, 'a_dst2': a_dst2, 'b2': b2}
    _L0_gnn_all = _L0_gnn_setup()
    _L0_gnn_in = {k: v for k, v in _L0_gnn_all.items() if k in ('W1', 'a_src1', 'a_dst1', 'b1', 'W2', 'a_src2', 'a_dst2', 'b2')}
    del _L0_gnn_all

    def _L1_gnn_setup():
        import jax, jax.numpy as jnp
        import numpy as np
        N_NODES = 50000
        N_EDGES = 12500
        D_MODEL = 256
        H = 8
        D_K = 32
        key = jax.random.key(seed)
        kx, kq, kk, kv, ks, kd = jax.random.split(key, 6)
        scale = 1.0 / np.sqrt(D_MODEL)
        x = jax.random.normal(kx, (N_NODES, D_MODEL), dtype=jnp.float32)
        Wq = jax.random.normal(kq, (D_MODEL, H * D_K), dtype=jnp.float32) * scale
        Wk = jax.random.normal(kk, (D_MODEL, H * D_K), dtype=jnp.float32) * scale
        Wv = jax.random.normal(kv, (D_MODEL, H * D_K), dtype=jnp.float32) * scale
        src = jax.random.randint(ks, (N_EDGES,), 0, N_NODES, dtype=jnp.int32)
        dst = jax.random.randint(kd, (N_EDGES,), 0, N_NODES, dtype=jnp.int32)
        return {'x': x, 'Wq': Wq, 'Wk': Wk, 'Wv': Wv, 'src': src, 'dst': dst}
    _L1_gnn_all = _L1_gnn_setup()
    _L1_gnn_in = {k: v for k, v in _L1_gnn_all.items() if k in ('Wq', 'Wk', 'Wv')}
    del _L1_gnn_all

    def _L2_gnn_setup():
        import jax, jax.numpy as jnp
        import numpy as np
        N_NODES = 10000
        N_EDGES = 5000
        D_IN = 256
        D_OUT = 256
        MAX_NORM = 0.95

        def _expmap0(u):
            un = jnp.linalg.norm(u, axis=-1, keepdims=True)
            un_c = jnp.maximum(un, 1e-15)
            return jnp.tanh(un_c) * u / un_c
        key = jax.random.key(seed)
        ks = jax.random.split(key, 7)
        x = jax.random.normal(ks[0], (N_NODES, D_IN), dtype=jnp.float32)
        edge_index = jax.random.randint(ks[1], (2, N_EDGES), 0, N_NODES, dtype=jnp.int64)
        W = jax.random.normal(ks[2], (D_OUT, D_IN), dtype=jnp.float32) * (1.0 / np.sqrt(D_IN))
        b = jax.random.normal(ks[3], (D_OUT,), dtype=jnp.float32) * 0.02
        mag_w = jax.random.normal(ks[4], (1, D_IN), dtype=jnp.float32) * 0.02
        mag_b = jax.random.normal(ks[5], (1,), dtype=jnp.float32) * 0.02
        attn_w = jax.random.normal(ks[6], (1, 2 * D_OUT), dtype=jnp.float32) * (1.0 / np.sqrt(2 * D_OUT))
        return {'x': x, 'edge_index': edge_index, 'W': W, 'b': b, 'mag_w': mag_w, 'mag_b': mag_b, 'attn_w': attn_w}
    _L2_gnn_all = _L2_gnn_setup()
    _L2_gnn_in = {k: v for k, v in _L2_gnn_all.items() if k in ('W', 'b', 'mag_w', 'mag_b', 'attn_w')}
    del _L2_gnn_all

    def _L3_gnn_setup():
        import jax, jax.numpy as jnp
        import numpy as np
        N_NODES = 50000
        N_EDGES = 300000
        D = 256
        EPS = 1e-12

        def _gcn_layer(x, W, b, src, dst, norm, n_nodes):
            xt = x @ W
            msg = xt[src] * norm[:, None]
            agg = jax.ops.segment_sum(msg, dst, num_segments=n_nodes)
            return jax.nn.relu(agg + b)
        key = jax.random.key(seed)
        ks = jax.random.split(key, 10)
        h5_all = jax.random.normal(ks[0], (N_NODES, D), dtype=jnp.float32)
        edge_index = jax.random.randint(ks[1], (2, N_EDGES), 0, N_NODES, dtype=jnp.int64)
        edge_weight = jax.random.uniform(ks[2], (N_EDGES,), dtype=jnp.float32)
        s = 1.0 / np.sqrt(D)
        W6 = jax.random.normal(ks[3], (D, D), dtype=jnp.float32) * s
        b6 = jnp.zeros((D,), dtype=jnp.float32)
        W7 = jax.random.normal(ks[4], (D, D), dtype=jnp.float32) * s
        b7 = jnp.zeros((D,), dtype=jnp.float32)
        Wp = jax.random.normal(ks[5], (D, D), dtype=jnp.float32) * s
        bp = jnp.zeros((D,), dtype=jnp.float32)
        return {'h5_all': h5_all, 'edge_index': edge_index, 'edge_weight': edge_weight, 'W6': W6, 'b6': b6, 'W7': W7, 'b7': b7, 'Wp': Wp, 'bp': bp}
    _L3_gnn_all = _L3_gnn_setup()
    _L3_gnn_in = {k: v for k, v in _L3_gnn_all.items() if k in ('W6', 'b6', 'W7', 'b7', 'Wp', 'bp')}
    del _L3_gnn_all
    return {'x': x, 'src': src, 'dst': dst, 'edge_weight': edge_weight, 'L0_gnn_W1': _L0_gnn_in['W1'], 'L0_gnn_a_src1': _L0_gnn_in['a_src1'], 'L0_gnn_a_dst1': _L0_gnn_in['a_dst1'], 'L0_gnn_b1': _L0_gnn_in['b1'], 'L0_gnn_W2': _L0_gnn_in['W2'], 'L0_gnn_a_src2': _L0_gnn_in['a_src2'], 'L0_gnn_a_dst2': _L0_gnn_in['a_dst2'], 'L0_gnn_b2': _L0_gnn_in['b2'], 'L1_gnn_Wq': _L1_gnn_in['Wq'], 'L1_gnn_Wk': _L1_gnn_in['Wk'], 'L1_gnn_Wv': _L1_gnn_in['Wv'], 'L2_gnn_W': _L2_gnn_in['W'], 'L2_gnn_b': _L2_gnn_in['b'], 'L2_gnn_mag_w': _L2_gnn_in['mag_w'], 'L2_gnn_mag_b': _L2_gnn_in['mag_b'], 'L2_gnn_attn_w': _L2_gnn_in['attn_w'], 'L3_gnn_W6': _L3_gnn_in['W6'], 'L3_gnn_b6': _L3_gnn_in['b6'], 'L3_gnn_W7': _L3_gnn_in['W7'], 'L3_gnn_b7': _L3_gnn_in['b7'], 'L3_gnn_Wp': _L3_gnn_in['Wp'], 'L3_gnn_bp': _L3_gnn_in['bp']}

def reference(x, src, dst, edge_weight, L0_gnn_W1, L0_gnn_a_src1, L0_gnn_a_dst1, L0_gnn_b1, L0_gnn_W2, L0_gnn_a_src2, L0_gnn_a_dst2, L0_gnn_b2, L1_gnn_Wq, L1_gnn_Wk, L1_gnn_Wv, L2_gnn_W, L2_gnn_b, L2_gnn_mag_w, L2_gnn_mag_b, L2_gnn_attn_w, L3_gnn_W6, L3_gnn_b6, L3_gnn_W7, L3_gnn_b7, L3_gnn_Wp, L3_gnn_bp):
    import jax
    import jax.numpy as jnp

    def _L0_gnn_ref(x, edge_index, W1, a_src1, a_dst1, b1, W2, a_src2, a_dst2, b2):
        import jax, jax.numpy as jnp
        import numpy as np
        N = 50000
        E = 12500
        D = 256
        H1, C1 = (4, 64)
        H2, C2 = (4, 64)
        NEG_SLOPE = 0.2

        def _gat_layer(x, src, dst, W, a_src, a_dst, b, n, h, c):
            feat = (x @ W).reshape(n, h, c)
            al_s = jnp.einsum('nhc,hc->nh', feat, a_src)
            al_d = jnp.einsum('nhc,hc->nh', feat, a_dst)
            e = al_s[src] + al_d[dst]
            e = jnp.where(e > 0, e, NEG_SLOPE * e)
            m = jax.ops.segment_max(e, dst, num_segments=n)
            ee = jnp.exp(e - m[dst])
            s = jax.ops.segment_sum(ee, dst, num_segments=n)
            alpha = ee / (s[dst] + 1e-16)
            out = jax.ops.segment_sum(alpha[:, :, None] * feat[src], dst, num_segments=n)
            return out.reshape(n, h * c) + b
        loops = jnp.arange(N, dtype=edge_index.dtype)
        src = jnp.concatenate([edge_index[0], loops])
        dst = jnp.concatenate([edge_index[1], loops])
        h = _gat_layer(x, src, dst, W1, a_src1, a_dst1, b1, N, H1, C1)
        h = jax.nn.elu(h)
        out = _gat_layer(h, src, dst, W2, a_src2, a_dst2, b2, N, H2, C2)
        return out

    def _L1_gnn_ref(x, Wq, Wk, Wv, src, dst):
        import jax, jax.numpy as jnp
        import numpy as np
        N_NODES = 50000
        N_EDGES = 12500
        D_MODEL = 256
        H = 8
        D_K = 32
        q = (x @ Wq).reshape(N_NODES, H, D_K)
        k = (x @ Wk).reshape(N_NODES, H, D_K)
        v = (x @ Wv).reshape(N_NODES, H, D_K)
        score = jnp.sum(k[src] * q[dst], axis=-1, keepdims=True)
        score = jnp.exp(jnp.clip(score / np.sqrt(D_K), -5.0, 5.0))
        wv = jax.ops.segment_sum(v[src] * score, dst, num_segments=N_NODES)
        z = jax.ops.segment_sum(score, dst, num_segments=N_NODES)
        out = wv / (z + 1e-09)
        return out.reshape(N_NODES, H * D_K)

    def _L2_gnn_ref(x, edge_index, W, b, mag_w, mag_b, attn_w):
        import jax, jax.numpy as jnp
        import numpy as np
        N_NODES = 10000
        N_EDGES = 5000
        D_IN = 256
        D_OUT = 256
        MAX_NORM = 0.95

        def _expmap0(u):
            un = jnp.linalg.norm(u, axis=-1, keepdims=True)
            un_c = jnp.maximum(un, 1e-15)
            return jnp.tanh(un_c) * u / un_c
        N = x.shape[0]
        F_out = W.shape[0]
        h_raw = x @ W.T + b
        h_dir = h_raw / jnp.maximum(jnp.linalg.norm(h_raw, axis=-1, keepdims=True), 1e-12)
        h_mag = jax.nn.sigmoid(x @ mag_w.T + mag_b) * 1.5
        h = h_dir * h_mag
        src, tgt = (edge_index[0], edge_index[1])
        h_src = h[src]
        h_tgt = h[tgt]
        a_s, a_t = (attn_w[0, :F_out], attn_w[0, F_out:])
        scores = h_src @ a_s + h_tgt @ a_t
        mx = jnp.maximum(jax.ops.segment_max(scores, tgt, num_segments=N), -1000000000.0)
        ex = jnp.exp(scores - mx[tgt])
        se = jax.ops.segment_sum(ex, tgt, num_segments=N)
        attn_weights = ex / (se[tgt] + 1e-10)
        agg = jax.ops.segment_sum(h_src * attn_weights[:, None], tgt, num_segments=N)
        h_combined = h + agg
        h_poincare = _expmap0(h_combined)
        norms = jnp.linalg.norm(h_poincare, axis=1, keepdims=True)
        return jnp.where(norms > MAX_NORM, h_poincare * (MAX_NORM / (norms + 1e-08)), h_poincare)

    def _L3_gnn_ref(h5_all, edge_index, edge_weight, W6, b6, W7, b7, Wp, bp):
        import jax, jax.numpy as jnp
        import numpy as np
        N_NODES = 50000
        N_EDGES = 300000
        D = 256
        EPS = 1e-12

        def _gcn_layer(x, W, b, src, dst, norm, n_nodes):
            xt = x @ W
            msg = xt[src] * norm[:, None]
            agg = jax.ops.segment_sum(msg, dst, num_segments=n_nodes)
            return jax.nn.relu(agg + b)
        src, dst = (edge_index[0], edge_index[1])
        deg_out = jax.ops.segment_sum(edge_weight, src, num_segments=N_NODES)
        deg_in = jax.ops.segment_sum(edge_weight, dst, num_segments=N_NODES)
        norm = edge_weight * jax.lax.rsqrt(deg_out[src] * deg_in[dst] + EPS)
        h6 = _gcn_layer(h5_all, W6, b6, src, dst, norm, N_NODES)
        h7 = _gcn_layer(h6, W7, b7, src, dst, norm, N_NODES)
        out = h7 @ Wp + bp
        return out
    edge_index = jnp.stack([src, dst])
    h = jnp.maximum(_layernorm(x, axis=-1), 0.0)
    x = x + _L0_gnn_ref(h, edge_index, L0_gnn_W1, L0_gnn_a_src1, L0_gnn_a_dst1, L0_gnn_b1, L0_gnn_W2, L0_gnn_a_src2, L0_gnn_a_dst2, L0_gnn_b2)
    h = jnp.maximum(_layernorm(x, axis=-1), 0.0)
    x = x + _L1_gnn_ref(h, L1_gnn_Wq, L1_gnn_Wk, L1_gnn_Wv, src, dst)
    h = jnp.maximum(_layernorm(x, axis=-1), 0.0)
    x = x + _L2_gnn_ref(h, edge_index, L2_gnn_W, L2_gnn_b, L2_gnn_mag_w, L2_gnn_mag_b, L2_gnn_attn_w)
    h = jnp.maximum(_layernorm(x, axis=-1), 0.0)
    x = x + _L3_gnn_ref(h, edge_index, edge_weight, L3_gnn_W6, L3_gnn_b6, L3_gnn_W7, L3_gnn_b7, L3_gnn_Wp, L3_gnn_bp)
    return x

_drawn_inputs = setup_inputs


def setup_inputs(seed=0):
    import zlib

    import numpy as np

    out = dict(_drawn_inputs(seed))
    spreads = {'L0_gnn_b1': (0.0, 0.1),
     'L0_gnn_b2': (0.0, 0.1),
     'L3_gnn_b6': (0.0, 0.314),
     'L3_gnn_b7': (0.0, 0.1),
     'L3_gnn_bp': (0.0, 0.1)}
    factors = {'edge_weight': 2.7,
     'L0_gnn_a_dst1': 107.864,
     'L0_gnn_a_src2': 3.323,
     'L0_gnn_a_dst2': 67.936,
     'L2_gnn_b': 61.015,
     'L2_gnn_mag_w': 95.272,
     'L2_gnn_attn_w': 200.0,
     'L2_gnn_W': 3.56}
    for name, (base, spread) in spreads.items():
        noise = np.random.default_rng([zlib.crc32(name.encode()), seed]).standard_normal(out[name].shape)
        drawn = base * np.exp(spread * noise) if base else spread * noise
        out[name] = jnp.asarray(drawn.astype(out[name].dtype))
    for name, factor in factors.items():
        out[name] = (out[name] * factor).astype(out[name].dtype)
    return out
```

```python
import concourse.bass as bass
from concourse import mybir
from contextlib import ExitStack

F32 = mybir.dt.float32
I32 = mybir.dt.int32
ALU = mybir.AluOpType
ACT = mybir.ActivationFunctionType
AX = mybir.AxisListType

P = 128
D = 256
KB = D // P
UNROLL = 4
CH = 7
F1W = 272
F2W = 264
BIG = 1e30
RSQRT_SEED = 1597463007.0


def hold(eng, sem, value, passed):
    base = 0
    if type(sem) is Running:
        sem, base = sem.sem, sem.base
    if type(value) is int:
        if value > 0:
            eng.wait_ge(sem, base + value)
    else:
        eng.wait_ge(sem, value + base)
        eng.sem_inc(passed, 1)


class Running:

    def __init__(self, sem):
        self.sem, self.base = sem, 0


class At:

    def __init__(self, n, turn, s):
        self.n, self.turn, self.s = n, turn, s

    def back(self, lag):
        return At(self.n - lag, self.turn + (self.s - lag) // UNROLL, (self.s - lag) % UNROLL)

    def slot(self, k):
        return self.s % k

    def use(self, k):
        return self.turn * (UNROLL // k) + self.s // k

    def alive(self, count):
        return type(self.n) is not int or 0 <= self.n < count


def pipeline(eng, count, depth, body):
    lo = -(-max(depth, 1) // UNROLL) * UNROLL
    turns = (count - 1 - lo) // UNROLL
    if turns < 1:
        lo, turns = 0, 0
    for n in range(lo):
        body(At(n, n // UNROLL, n % UNROLL))
    if turns:
        with eng.Fori(0, turns) as k:
            for s in range(UNROLL):
                body(At(k * UNROLL + (lo + s), k + lo // UNROLL, s))
    for n in range(lo + turns * UNROLL, count + depth):
        body(At(n, n // UNROLL, n % UNROLL))


class Chain:

    def __init__(self, eng, sem):
        self.eng, self.sem, self.n = eng, sem, 0

    def restart(self):
        self.eng.drain()
        self.eng.sem_clear(self.sem)
        self.n = 0

    def __call__(self, ins):
        self.n += 1
        ins.then_inc(self.sem, 1)
        self.eng.wait_ge(self.sem, self.n)


def rsqrt(nc, link, y, v, a):
    link(nc.vector.tensor_scalar(a.bitcast(I32), v.bitcast(I32), 1, None, ALU.logical_shift_right))
    link(nc.vector.tensor_scalar(y.bitcast(I32), a.bitcast(I32), -1.0, RSQRT_SEED, ALU.mult, ALU.add))
    for _ in range(3):
        link(nc.vector.tensor_tensor(a, y, y, ALU.mult))
        link(nc.vector.scalar_tensor_tensor(a, a, -0.5, v, ALU.mult, ALU.mult))
        link(nc.vector.scalar_tensor_tensor(y, a, 1.5, y, ALU.add, ALU.mult))


def min_int(value, most):
    return min(value, most) if type(value) is int else value


def magnitude(nc, link, fac, e, r):
    link(nc.vector.tensor_scalar(fac, e, 1.0, None, ALU.add))
    link(nc.vector.reciprocal(fac, fac))
    link(nc.vector.scalar_tensor_tensor(fac, fac, 1.5, r, ALU.mult, ALU.mult))


def expmap_scale(nc, link, scale, th, un, unc, a, b):
    V = nc.vector
    link(V.reciprocal(a, unc))
    link(V.tensor_tensor(scale, th, a, ALU.mult))
    link(V.tensor_tensor(a, scale, un, ALU.mult))
    link(V.tensor_scalar(b, a, 1e-8, None, ALU.add))
    link(V.reciprocal(b, b))
    link(V.tensor_scalar(b, b, 0.95, -1.0, ALU.mult, ALU.add))
    link(V.scalar_tensor_tensor(b, a, 0.95, b, ALU.is_gt, ALU.mult))
    link(V.scalar_tensor_tensor(scale, b, 1.0, scale, ALU.add, ALU.mult))


def gnn_program(nc, x, src, dst, edge_weight, W1, a_src1, a_dst1, b1, W2, a_src2, a_dst2, b2,
                Wq, Wk, Wv, WL, bL, mag_w, mag_b, attn_w, W6, b6, W7, b7, Wp, bp, out):
    N, E = x.shape[0], src.shape[0]
    NC = -(-E // (P * CH))
    T = NC * CH
    EP = T * P
    HQ = 4
    CQ = NC * HQ
    CE = CH * P
    OOB = N + 4096
    U = -(-N // (2 * P))
    UPART = (N - (U - 1) * 2 * P) // 2
    NCOL = 2 * U
    assert CQ <= P and NCOL <= 512 and N % 4 == 0

    def dram(name, shape):
        return nc.dram_tensor(name, shape, F32, kind="Internal").ap()

    F1 = dram("F1", (N, F1W))
    F2 = dram("F2", (N, F2W))
    H2 = dram("H2", (N, D))
    HL = dram("HL", (N, F2W))
    X3 = dram("X3", (N, D))
    T7 = dram("T7", (N, D))
    FE2 = dram("FE2", (EP, F2W))
    XE1 = dram("XE1", (EP, D))
    XE2 = dram("XE2", (EP, D))
    HE2 = dram("HE2", (EP, D))
    XE3 = dram("XE3", (EP, D))
    DSTF = dram("DSTF", (T, P))

    ctx = ExitStack()
    with ctx:
        def sb(name, shape, dt=F32, on=ctx):
            return on.enter_context(nc.sbuf_tensor(name, shape, dt))

        ident = sb("ident", [P, P])
        last_row = sb("last_row", [P, 1])
        dst_row = sb("dst_row", [P, EP])
        dst_col = sb("dst_col", [P, T])
        carry_col = sb("carry_col", [P, T])
        ew = sb("ew", [P, T])
        norm = sb("norm", [P, T])
        index = sb("index", [P, T, 7], I32)
        w_edge = sb("w_edge", [P, T, HQ])
        w_self = sb("w_self", [P, T, HQ])
        w1 = sb("w1", [P, KB, F2W])
        w2 = sb("w2", [P, KB, F2W])
        wl = sb("wl", [P, KB, F2W])
        wq = sb("wq", [P, KB, D])
        wkv = sb("wkv", [P, KB, 2 * D])
        w6 = sb("w6", [P, KB, D])
        w7 = sb("w7", [P, KB, D])
        wp = sb("wp", [P, KB, D])
        rb1 = sb("rb1", [P, D])
        rb2 = sb("rb2", [P, D])
        rbl = sb("rbl", [P, F2W])
        rb6 = sb("rb6", [P, D])
        rb7 = sb("rb7", [P, D])
        rbp = sb("rbp", [P, D])
        gcn_const = sb("gcn_const", [P, D])
        t7_const = sb("t7_const", [P, 4, D])

        def running(name):
            return [Running(ctx.enter_context(nc.semaphore(f"{name}{i}"))) for i in range(4)]

        gathered_in = [running("gathered_a"), running("gathered_b")]
        scattered_out = running("scattered")

        class Phase:

            count = 0

            def __enter__(self):
                Phase.count += 1
                self.tag = f"_{Phase.count}"
                self.st = ExitStack()
                self.st.__enter__()
                self.sems = []
                self.passed = {e: self.sem("passed_" + e) for e in ("sp", "act", "pe", "dve", "pool")}
                return self

            def sem(self, name):
                s = self.st.enter_context(nc.semaphore(name + self.tag))
                self.sems.append(s)
                return s

            def slots(self, name, n):
                return [self.sem(f"{name}{k}") for k in range(n)]

            def sb(self, name, shape, dt=F32):
                return sb(name + self.tag, shape, dt, self.st)

            def ps(self, name, shape, dt=F32):
                return self.st.enter_context(nc.psum_tensor(name + self.tag, shape, dt))

            def __exit__(self, *err):
                if err[0] is None:
                    with nc.Block() as block:
                        @block.gpsimd
                        def _(pool):
                            for s in self.sems:
                                pool.sem_clear(s)
                return self.st.__exit__(*err)

        with Phase() as ph:
            NB = -(-T // P)
            raw = [ph.sb(f"raw{k}", [P, NB, P], I32) for k in range(3)]
            rows = [ph.sb(f"rows{k}", [P, NB, P]) for k in range(4)]
            src_col = ph.sb("src_col", [P, T])
            next_col = ph.sb("next_col", [P, T])
            tmp = ph.sb("tmp", [P, T])
            av = [ph.sb(f"av{k}", [P, D]) for k in range(6)]
            prod = ph.sb("prod", [P, KB, D])
            wraw = ph.sb("wraw", [P, KB, D])
            relu_b = ph.sb("relu_b", [P, D])
            relu_bt = ph.sb("relu_bt", [P, KB, P])
            ps_t = ph.ps("ps_t", [P, 512])
            ps_w = ph.ps("ps_w", [P, 4, P])
            s_pad, s_in, s_ids, s_id = ph.sem("s_pad"), ph.sem("s_in"), ph.sem("s_ids"), ph.sem("s_id")
            s_dr, s_drs = ph.sem("s_dr"), ph.sem("s_drs")
            s_v, s_pe, s_ch = ph.sem("s_v"), ph.sem("s_pe"), ph.sem("s_ch")
            with nc.Block() as block:
                def load_rows(eng, to, flat, n):
                    full, count = n // P, 0
                    for b in range(NB):
                        r = min(full - b * P, P)
                        if r > 0:
                            eng.dma_start(to[0:r, b, :], flat[b * P * P:b * P * P + r * P]
                                          .rearrange("(t p) -> t p", p=P)).then_inc(s_ids, 16)
                            count += 1
                    if n % P:
                        q = full % P
                        eng.dma_start(to[q:q + 1, full // P, 0:n % P],
                                      flat[full * P:n].rearrange("(a n) -> a n", a=1)).then_inc(s_ids, 16)
                        count += 1
                    return count

                counted = {}

                @block.sync
                def _(sp):
                    n = 0
                    for w, t in ((W1, w1), (W2, w2)):
                        sp.dma_start(t[:, :, 0:D], w.rearrange("(k p) n -> p k n", p=P)).then_inc(s_in, 16)
                        n += 1
                    for w, t in ((Wq, wq), (W6, w6), (W7, w7), (Wp, wp), (WL, wraw)):
                        sp.dma_start(t[:, :, :], w.rearrange("(k p) n -> p k n", p=P)).then_inc(s_in, 16)
                        n += 1
                    sp.dma_start(wkv[:, :, 0:D], Wk.rearrange("(k p) n -> p k n", p=P)).then_inc(s_in, 16)
                    sp.dma_start(wkv[:, :, D:2 * D], Wv.rearrange("(k p) n -> p k n", p=P)).then_inc(s_in, 16)
                    with nc.allow_non_contiguous_dma(reason="one column of 256 elements"):
                        sp.dma_start(wl[:, :, 258:259], mag_w.rearrange("a (k p) -> p k a", p=P)).then_inc(s_in, 16)
                    n += 3
                    for v, t in ((b1, rb1), (b2, rb2), (b6, rb6), (b7, rb7), (bp, rbp)):
                        sp.dma_start(t[:, :], v.partition_broadcast(P)).then_inc(s_in, 16)
                        n += 1
                    sp.dma_start(rbl[:, 0:D], bL.partition_broadcast(P)).then_inc(s_in, 16)
                    sp.dma_start(rbl[:, 258:259], mag_b.partition_broadcast(P)).then_inc(s_in, 16)
                    for v, t in zip((a_src1, a_dst1, a_src2, a_dst2), av):
                        sp.dma_start(t[:, :], v.rearrange("h c -> (h c)").partition_broadcast(P)).then_inc(s_in, 16)
                    sp.dma_start(av[4][:, :], attn_w[0, 0:D].partition_broadcast(P)).then_inc(s_in, 16)
                    sp.dma_start(av[5][:, :], attn_w[0, D:2 * D].partition_broadcast(P)).then_inc(s_in, 16)
                    counted["in"] = 16 * (n + 8)
                    sp.wait_ge(s_pad, 8)
                    c = load_rows(sp, raw[0], src, E)
                    c += load_rows(sp, raw[1], dst, E)
                    c += load_rows(sp, raw[2], dst[1:E], E - 1)
                    c += load_rows(sp, rows[3], edge_weight, E)
                    counted["ids"] = 16 * c
                    sp.wait_ge(s_drs, 1)
                    for b in range(NB):
                        r = min(T - b * P, P)
                        sp.dma_start(DSTF[b * P:b * P + r, :], rows[1][0:r, b, :]).then_inc(s_dr, 16)
                    sp.wait_ge(s_dr, 16 * NB)
                    sp.dma_start(dst_row[:, :], DSTF.rearrange("t p -> (t p)").partition_broadcast(P))\
                      .then_inc(s_dr, 16)
                    sp.wait_ge(s_dr, 16 * NB + 16)

                @block.gpsimd
                def _(pool):
                    nc.gpsimd.memset(raw[0][:, :, :], 0).then_inc(s_pad, 1)
                    nc.gpsimd.memset(raw[1][:, :, :], OOB).then_inc(s_pad, 1)
                    nc.gpsimd.memset(raw[2][:, :, :], -1).then_inc(s_pad, 1)
                    nc.gpsimd.memset(rows[3][:, :, :], 0.0).then_inc(s_pad, 1)
                    nc.gpsimd.memset(w1[:, :, D:F2W], 0.0).then_inc(s_pad, 1)
                    nc.gpsimd.memset(w2[:, :, D:F2W], 0.0).then_inc(s_pad, 1)
                    nc.gpsimd.memset(wl[:, :, 259:F2W], 0.0).then_inc(s_pad, 1)
                    nc.gpsimd.memset(rbl[:, 259:F2W], 0.0).then_inc(s_pad, 1)
                    nc.gpsimd.memset(ident[:, :], 0.0).then_inc(s_id, 1)
                    nc.gpsimd.memset(last_row[:, :], 0.0).then_inc(s_id, 1)
                    pool.wait_ge(s_id, 2)
                    nc.gpsimd.affine_select(out=ident[:, :], in_=ident[:, :], compare_op=ALU.not_equal, fill=1.0,
                                            base=0, pattern=[[-1, P]], channel_multiplier=1).then_inc(s_id, 1)
                    nc.gpsimd.affine_select(out=last_row[:, :], in_=last_row[:, :], compare_op=ALU.not_equal,
                                            fill=1.0, base=-(P - 1), pattern=[[0, 1]], channel_multiplier=1)\
                        .then_inc(s_id, 1)
                    pool.wait_ge(s_id, 4)

                @block.tensor
                def _(pe):
                    pe.wait_ge(s_id, 4)
                    for k in (0, 1, 2, 3):
                        pe.wait_ge(s_v, k + 1)
                        for b in range(NB):
                            last = nc.tensor.transpose(ps_t[:, b * P:(b + 1) * P], rows[k][:, b, :], ident[:, :])
                        last.then_inc(s_pe, 1)
                    pe.wait_ge(s_v, 5)
                    pe.wait_ge(s_in, counted["in"])
                    for i in range(KB):
                        for o in range(KB):
                            last = nc.tensor.transpose(ps_w[:, i * KB + o, :], wraw[:, o, i * P:(i + 1) * P],
                                                       ident[:, :])
                    last.then_inc(s_pe, 1)
                    for k, w in ((0, w7), (1, wp)):
                        pe.wait_ge(s_v, 6 + 2 * k)
                        for j in range(KB):
                            last = nc.tensor.transpose(ps_t[:, j * P:(j + 1) * P], relu_b[:, j * P:(j + 1) * P],
                                                       ident[:, :])
                        last.then_inc(s_pe, 1)
                        pe.wait_ge(s_v, 7 + 2 * k)
                        for j in range(KB):
                            last = nc.tensor.matmul(ps_t[:, 256:512], relu_bt[:, j, :], w[:, j, :],
                                                    start=(j == 0), stop=(j == KB - 1))
                        last.then_inc(s_pe, 1)

                @block.vector
                def _(dve):
                    link = Chain(dve, s_ch)
                    V = nc.vector
                    dve.wait_ge(s_ids, counted["ids"])
                    for k in range(3):
                        link(V.tensor_copy(rows[k][:, :, :], raw[k][:, :, :]))
                    dve.sem_inc(s_drs, 1)
                    dve.sem_inc(s_v, 1)
                    cols = (src_col, dst_col, next_col, ew)
                    for k in range(4):
                        dve.wait_ge(s_pe, k + 1)
                        link(V.tensor_copy(cols[k][:, :], ps_t[:, 0:T]))
                        dve.sem_inc(s_v, 1)
                    dve.wait_ge(s_in, counted["in"])
                    dve.wait_ge(s_pe, 5)
                    dve.wait_ge(s_pad, 8)
                    dve.wait_ge(s_id, 4)
                    for i in range(KB):
                        link(V.tensor_copy(wl[:, i, 0:D], ps_w[:, i * KB:(i + 1) * KB, :]
                                           .rearrange("p a b -> p (a b)")))
                    link(V.tensor_scalar(relu_b[:, :], rb6[:, :], 0.0, None, ALU.max))
                    dve.sem_inc(s_v, 1)
                    dve.wait_ge(s_pe, 6)
                    link(V.tensor_copy(relu_bt[:, :, :].rearrange("p a b -> p (a b)"), ps_t[:, 0:D]))
                    dve.sem_inc(s_v, 1)
                    dve.wait_ge(s_pe, 7)
                    for r in range(4):
                        link(V.tensor_copy(t7_const[:, r, :], ps_t[:, 256:512]))
                    link(V.tensor_scalar(relu_b[:, :], rb7[:, :], 0.0, None, ALU.max))
                    dve.sem_inc(s_v, 1)
                    dve.wait_ge(s_pe, 8)
                    link(V.tensor_copy(relu_bt[:, :, :].rearrange("p a b -> p (a b)"), ps_t[:, 0:D]))
                    dve.sem_inc(s_v, 1)
                    dve.wait_ge(s_pe, 9)
                    link(V.tensor_tensor(gcn_const[:, :], ps_t[:, 256:512], rbp[:, :], ALU.add))
                    for w, a, b in ((w1, av[0], av[1]), (w2, av[2], av[3])):
                        for off, vec in ((D, a), (D + 4, b)):
                            for k in range(KB):
                                link(V.tensor_tensor(prod[:, k, :], w[:, k, 0:D], vec[:, :], ALU.mult))
                                link(V.tensor_reduce(w[:, k, off:off + 4],
                                                     prod[:, k, :].rearrange("p (h c) -> p h c", h=4),
                                                     axis=AX.X, op=ALU.add))
                    for off, vec in ((D, av[4]), (D + 1, av[5])):
                        for k in range(KB):
                            link(V.tensor_tensor(prod[:, k, :], wl[:, k, 0:D], vec[:, :], ALU.mult))
                            link(V.tensor_reduce(wl[:, k, off:off + 1], prod[:, k, :], axis=AX.X, op=ALU.add))
                        link(V.tensor_tensor(prod[:, 0, :], rbl[:, 0:D], vec[:, :], ALU.mult))
                        link(V.tensor_reduce(rbl[:, off:off + 1], prod[:, 0, :], axis=AX.X, op=ALU.add))
                    link(V.tensor_copy(index[:, :, 0], src_col[:, :]))
                    link(V.tensor_scalar(index[:, :, 3], src_col[:, :], 17.0, 16.0, ALU.mult, ALU.add))
                    link(V.tensor_scalar(index[:, :, 5], src_col[:, :], 33.0, 32.0, ALU.mult, ALU.add))
                    link(V.tensor_scalar(tmp[:, :], dst_col[:, :], float(N - 1), None, ALU.min))
                    link(V.tensor_copy(index[:, :, 1], tmp[:, :]))
                    link(V.tensor_scalar(index[:, :, 4], tmp[:, :], 17.0, 16.0, ALU.mult, ALU.add))
                    link(V.tensor_scalar(index[:, :, 6], tmp[:, :], 33.0, 32.0, ALU.mult, ALU.add))
                    link(V.tensor_tensor(tmp[:, :], dst_col[:, :], next_col[:, :], ALU.is_equal))
                    link(V.scalar_tensor_tensor(index[:, :, 2], tmp[:, :], float(OOB), dst_col[:, :],
                                                ALU.mult, ALU.add))
                    link(V.memset(carry_col[:, :], -1.0))
                    link(V.tensor_scalar(tmp[:, 1:T], dst_col[:, 0:T - 1], 1.0, last_row[:, 0:1],
                                         ALU.add, ALU.mult))
                    link(V.tensor_scalar(carry_col[:, 1:T], tmp[:, 1:T], -1.0, None, ALU.add))

        deg_stack = ExitStack()
        deg = sb("deg", [P, NCOL, 2], on=deg_stack)
        with Phase() as ph:
            iota_i = ph.sb("iota_i", [P, NCOL if NCOL > P else P], I32)
            iota_f = ph.sb("iota_f", [P, NCOL if NCOL > P else P])
            ids = ph.sb("ids", [P, T], I32)
            bits = ph.sb("bits", [P, T], I32)
            high = ph.sb("high", [P, T], I32)
            lo_f = [ph.sb(f"lo_f{k}", [P, T]) for k in range(2)]
            hi_f = [ph.sb(f"hi_f{k}", [P, T]) for k in range(2)]
            hot_lo = ph.sb("hot_lo", [P, 2, 2, P])
            hot_hi = ph.sb("hot_hi", [P, 2, 2, NCOL])
            ps_deg = [ph.ps(f"ps_deg{k}", [P, NCOL]) for k in range(2)]
            s_iota, s_ch = ph.sem("s_iota"), ph.sem("s_ch")
            hots_ready, hots_used = ph.sem("hots_ready"), ph.sem("hots_used")
            with nc.Block() as block:
                @block.gpsimd
                def _(pool):
                    nc.gpsimd.iota(iota_i[:, :], [[1, iota_i.shape[1]]], base=0, channel_multiplier=0)\
                        .then_inc(s_iota, 1)

                @block.vector
                def _(dve):
                    link = Chain(dve, s_ch)
                    V = nc.vector
                    dve.wait_ge(s_iota, 1)
                    link(V.tensor_copy(iota_f[:, :], iota_i[:, :]))
                    for k, nodes in ((0, 0), (1, 1)):
                        link(V.tensor_scalar(ids[:, :], index[:, :, nodes], 1, 127,
                                             ALU.logical_shift_right, ALU.bitwise_and))
                        link(V.tensor_copy(lo_f[k][:, :], ids[:, :]))
                        link(V.tensor_scalar(ids[:, :], index[:, :, nodes], 8, 1,
                                             ALU.logical_shift_right, ALU.logical_shift_left))
                        link(V.tensor_scalar(bits[:, :], index[:, :, nodes], 1, None, ALU.bitwise_and))
                        link(V.tensor_tensor(high[:, :], ids[:, :], bits[:, :], ALU.bitwise_or))
                        link(V.tensor_copy(hi_f[k][:, :], high[:, :]))

                    def tile(at):
                        if at.alive(T):
                            hold(dve, hots_used, at.n - 1, ph.passed["dve"])
                            col = bass.ds(at.n, 1)
                            for k in range(2):
                                V.tensor_scalar(hot_lo[:, at.slot(2), k, :], iota_f[:, 0:P], lo_f[k][:, col],
                                                ew[:, col], ALU.is_equal, ALU.mult)
                                last = V.tensor_scalar(hot_hi[:, at.slot(2), k, :], iota_f[:, 0:NCOL],
                                                       hi_f[k][:, col], None, ALU.is_equal)
                            last.then_inc(hots_ready, 1)
                    pipeline(dve, T, 0, tile)
                    dve.wait_ge(hots_used, T)
                    for k in range(2):
                        link(V.tensor_copy(deg[:, :, k], ps_deg[k][:, :]))

                @block.tensor
                def _(pe):
                    def tile(at):
                        hold(pe, hots_ready, at.n + 1, ph.passed["pe"])
                        first = type(at.n) is int and at.n == 0
                        end = type(at.n) is int and at.n == T - 1
                        for k in range(2):
                            last = nc.tensor.matmul(ps_deg[k][:, :], hot_lo[:, at.slot(2), k, :], hot_hi[:, at.slot(2), k, :],
                                                    start=first, stop=end)
                        last.then_inc(hots_used, 1)
                    pipeline(pe, T, 0, tile)

        with Phase() as ph:
            xin = ph.sb("xin", [P, 2, 2, D])
            xb = ph.sb("xb", [P, 4, 2, D])
            h1 = ph.sb("h1", [P, 2, 2, D])
            h2 = ph.sb("h2", [P, 2, 2, D])
            f1o = ph.sb("f1o", [P, 2, 2, F1W])
            f2o = ph.sb("f2o", [P, 2, 2, F2W])
            z = ph.sb("z", [P, 2, D])
            zm = ph.sb("zm", [P, 2, D])
            g = ph.sb("g", [P, 2, 2, D])
            t1 = ph.sb("t1", [P, 4, P])
            t2 = ph.sb("t2", [P, 4, P])
            t3 = ph.sb("t3", [P, 4, P])
            hr = ph.sb("hr", [P, 2, F2W])
            sq = ph.sb("sq", [P, 2, D])
            ho = ph.sb("ho", [P, 2, 2, F2W])
            x3o = ph.sb("x3o", [P, 2, 2, D])
            oo = ph.sb("oo", [P, 2, 2, D])
            st = ph.sb("st", [P, 4, 6])
            mean, dm = ph.sb("mean", [P, 4]), ph.sb("dm", [P, 4])
            var, ra = ph.sb("var", [P, 6]), ph.sb("ra", [P, 6])
            rt, nm = ph.sb("rt", [P, 2, 6]), ph.sb("nm", [P, 2, 4])
            n2, em, th = ph.sb("n2", [P, 2]), ph.sb("em", [P, 2]), ph.sb("th", [P, 2])
            fac, un, unc = ph.sb("fac", [P, 2]), ph.sb("un", [P, 2]), ph.sb("unc", [P, 2])
            ga, gb, gc = ph.sb("ga", [P, 2]), ph.sb("gb", [P, 2]), ph.sb("gc", [P, 2])
            warm = ph.sb("warm", [P, 1])
            tp = [ph.ps(f"tp{k}", [P, 4, P]) for k in range(3)]
            mm_ac = ph.ps("mm_ac", [P, 2, 512])
            mm_b = ph.ps("mm_b", [P, 2, 512])
            x_in = ph.slots("x_in", 2)
            f1_out, f2_out, h2_out = ph.slots("f1_out", 2), ph.slots("f2_out", 2), ph.slots("h2_out", 2)
            hl_out, x3_out, o_out = ph.slots("hl_out", 2), ph.slots("x3_out", 2), ph.slots("o_out", 2)
            s = {k: ph.sem(k) for k in (
                "s_ch", "xb", "deg", "stats", "h1", "h2", "zm", "exp", "g", "tp0", "tp1", "tp2", "t1", "t2", "t3",
                "mm1", "mm2", "mm3", "f1", "f2", "hr", "sq", "x1", "unc", "tanh", "x3", "ho", "oo", "warm",
                "pad")}
            link_sem = s["s_ch"]

            def rows_of(table, at):
                if type(at.n) is not int:
                    return table[bass.ds(at.n * (2 * P), 2 * P), :].rearrange("(p r) w -> p (r w)", r=2), P
                np_ = UPART if at.n == U - 1 else P
                return table[at.n * 2 * P:at.n * 2 * P + 2 * np_, :].rearrange("(p r) w -> p (r w)", r=2), np_

            def flat(t, slot, np_):
                return t[0:np_, slot, :, :].rearrange("p r w -> p (r w)")

            def both(row, w):
                return row[:, 0:w].unsqueeze(1).to_broadcast([P, 2, w])

            with nc.Block() as block:
                @block.sync
                def _(sp):
                    ps = ph.passed["sp"]

                    def unit(at):
                        if at.alive(U):
                            hold(sp, s["stats"], at.n - 1, ps)
                            hold(sp, s["h1"], at.n - 1, ps)
                            hold(sp, s["xb"], at.n - 1, ps)
                            view, np_ = rows_of(x, at)
                            sp.dma_start(flat(xin, at.slot(2), np_), view).then_inc(x_in[at.slot(2)], 16)
                        j = at.back(1)
                        if j.alive(U):
                            view, np_ = rows_of(F1, j)
                            hold(sp, s["f1"], j.n + 1, ps)
                            hold(sp, s["deg"], j.n + 1, ps)
                            sp.dma_start(view, flat(f1o, j.slot(2), np_)).then_inc(f1_out[j.slot(2)], 16)
                        j = at.back(2)
                        if j.alive(U):
                            view, np_ = rows_of(F2, j)
                            hold(sp, s["f2"], j.n + 1, ps)
                            sp.dma_start(view, flat(f2o, j.slot(2), np_)).then_inc(f2_out[j.slot(2)], 16)
                        j = at.back(3)
                        if j.alive(U):
                            view, np_ = rows_of(H2, j)
                            hold(sp, s["h2"], j.n + 1, ps)
                            sp.dma_start(view, flat(h2, j.slot(2), np_)).then_inc(h2_out[j.slot(2)], 16)
                        j = at.back(4)
                        if j.alive(U):
                            view, np_ = rows_of(HL, j)
                            hold(sp, s["ho"], j.n + 1, ps)
                            sp.dma_start(view, flat(ho, j.slot(2), np_)).then_inc(hl_out[j.slot(2)], 16)
                            view, np_ = rows_of(X3, j)
                            hold(sp, s["x3"], j.n + 1, ps)
                            sp.dma_start(view, flat(x3o, j.slot(2), np_)).then_inc(x3_out[j.slot(2)], 16)
                            view, np_ = rows_of(out, j)
                            hold(sp, s["oo"], j.n + 1, ps)
                            sp.dma_start(view, flat(oo, j.slot(2), np_)).then_inc(o_out[j.slot(2)], 16)
                    pipeline(sp, U, 4, unit)
                    for group in (f1_out, f2_out, h2_out, hl_out, x3_out, o_out):
                        for k in range(2):
                            sp.wait_ge(group[k], 16 * ((U + 1 - k) // 2))

                @block.gpsimd
                def _(pool):
                    pp = ph.passed["pool"]
                    nc.gpsimd.memset(f1o[:, :, :, :], 0.0)
                    nc.gpsimd.memset(warm[:, :], 0.0).then_inc(s["pad"], 1)
                    pool.wait_ge(s["pad"], 1)

                    def unit(at):
                        if at.alive(U):
                            hold(pool, x_in[at.slot(2)], 16 * (at.use(2) + 1), pp)
                            hold(pool, s["x3"], at.n - 3, pp)
                            nc.gpsimd.tensor_tensor(xb[:, at.slot(4), :, :], xin[:, at.slot(2), :, :],
                                                    both(rb2, D), ALU.add).then_inc(s["xb"], 1)
                            hold(pool, f1_out[at.slot(2)], 16 * at.use(2), pp)
                            nc.gpsimd.tensor_copy(f1o[:, at.slot(2), :, 264:266], deg[:, bass.ds(at.n * 2, 2), :])\
                                .then_inc(s["deg"], 1)
                        j = at.back(3)
                        if j.alive(U):
                            hold(pool, s["x3"], j.n + 1, pp)
                            hold(pool, o_out[j.slot(2)], 16 * j.use(2), pp)
                            nc.gpsimd.tensor_tensor(oo[:, j.slot(2), :, :], x3o[:, j.slot(2), :, :],
                                                    both(gcn_const, D), ALU.add).then_inc(s["oo"], 1)
                    pipeline(pool, U, 3, unit)

                @block.tensor
                def _(pe):
                    pp = ph.passed["pe"]

                    def turn_rows(rows_t, bank, sem):
                        for r in range(2):
                            for k in range(KB):
                                last = nc.tensor.transpose(bank[:, 2 * r + k, :], rows_t[:, r, k * P:(k + 1) * P],
                                                           ident[:, :])
                        last.then_inc(sem, 1)

                    def product(acc, lhs, w, sem):
                        for r in range(2):
                            for k in range(KB):
                                last = nc.tensor.matmul(acc[:, r, 0:F2W], lhs[:, 2 * r + k, :], w[:, k, :],
                                                        start=(k == 0), stop=(k == KB - 1))
                        last.then_inc(sem, 1)

                    def unit(at):
                        a, b, c = at, at.back(1), at.back(2)
                        if c.alive(U):
                            hold(pe, s["h2"], c.n + 1, pp)
                            hold(pe, s["t3"], c.n, pp)
                            turn_rows(h2[:, c.slot(2), :, :], tp[2], s["tp2"])
                        if a.alive(U):
                            hold(pe, s["h1"], a.n + 1, pp)
                            hold(pe, s["t1"], a.n, pp)
                            turn_rows(h1[:, a.slot(2), :, :], tp[0], s["tp0"])
                            hold(pe, s["t1"], a.n + 1, pp)
                            hold(pe, s["f1"], a.n, pp)
                            hold(pe, s["hr"], a.n - 2, pp)
                            product(mm_ac, t1, w1, s["mm1"])
                        if b.alive(U):
                            hold(pe, s["g"], b.n + 1, pp)
                            hold(pe, s["t2"], b.n, pp)
                            turn_rows(g[:, b.slot(2), :, :], tp[1], s["tp1"])
                            hold(pe, s["t2"], b.n + 1, pp)
                            hold(pe, s["f2"], b.n, pp)
                            product(mm_b, t2, w2, s["mm2"])
                        if c.alive(U):
                            hold(pe, s["t3"], c.n + 1, pp)
                            hold(pe, s["hr"], c.n, pp)
                            if a.alive(U):
                                hold(pe, s["f1"], a.n + 1, pp)
                            product(mm_ac, t3, wl, s["mm3"])
                    pipeline(pe, U, 2, unit)

                @block.scalar
                def _(act):
                    pa = ph.passed["act"]
                    act.wait_ge(s["pad"], 1)
                    nc.scalar.activation(warm[:, :], warm[:, :], ACT.Exp).then_inc(s["warm"], 1)
                    act.wait_ge(s["warm"], 1)

                    def unit(at):
                        a, b, c, d = at, at.back(1), at.back(2), at.back(3)
                        if b.alive(U):
                            hold(act, s["zm"], b.n + 1, pa)
                            nc.scalar.activation(zm[:, :, :], zm[:, :, :], ACT.Exp).then_inc(s["exp"], 1)
                        if d.alive(U):
                            hold(act, s["hr"], d.n + 1, pa)
                            nc.scalar.activation(em[:, :], em[:, :], ACT.Exp, scale=-1.0)
                            for r in range(2):
                                last = nc.scalar.activation(sq[:, r, :], hr[:, r, 0:D], ACT.Square,
                                                            accum_out=n2[:, r:r + 1])
                            last.then_inc(s["sq"], 1)
                        if a.alive(U) or c.alive(U):
                            hold(act, s["stats"], at.n + 1, pa)
                        if c.alive(U):
                            hold(act, h2_out[c.slot(2)], 16 * c.use(2), pa)
                            for r in range(2):
                                last = nc.scalar.activation(h2[:, c.slot(2), r, :], xb[:, c.slot(4), r, :], ACT.Relu,
                                                            bias=nm[:, at.slot(2), 2 + r:3 + r],
                                                            scale=rt[:, at.slot(2), 2 + r:3 + r])
                            last.then_inc(s["h2"], 1)
                        if a.alive(U):
                            hold(act, s["tp0"], a.n - 1, pa)
                            for r in range(2):
                                last = nc.scalar.activation(h1[:, a.slot(2), r, :], xin[:, a.slot(2), r, :], ACT.Relu,
                                                            bias=nm[:, at.slot(2), r:r + 1],
                                                            scale=rt[:, at.slot(2), r:r + 1])
                            last.then_inc(s["h1"], 1)
                        if c.alive(U):
                            hold(act, s["tp2"], c.n + 1, pa)
                            hold(act, s["mm3"], c.n, pa)
                            nc.scalar.activation(t3[:, :, :], tp[2][:, :, :], ACT.Copy).then_inc(s["t3"], 1)
                        if a.alive(U):
                            hold(act, s["tp0"], a.n + 1, pa)
                            hold(act, s["mm1"], a.n, pa)
                            nc.scalar.activation(t1[:, :, :], tp[0][:, :, :], ACT.Copy).then_inc(s["t1"], 1)
                        if d.alive(U):
                            hold(act, s["unc"], d.n + 1, pa)
                            nc.scalar.activation(th[:, :], unc[:, :], ACT.Tanh).then_inc(s["tanh"], 1)
                        if a.alive(U):
                            hold(act, s["mm1"], a.n + 1, pa)
                            hold(act, f1_out[a.slot(2)], 16 * a.use(2), pa)
                            hold(act, s["zm"], a.n - 1, pa)
                            nc.scalar.activation(f1o[:, a.slot(2), :, 0:F2W], mm_ac[:, :, 0:F2W], ACT.Copy)\
                                .then_inc(s["f1"], 1)
                        if b.alive(U):
                            hold(act, s["tp1"], b.n + 1, pa)
                            hold(act, s["mm2"], b.n, pa)
                            nc.scalar.activation(t2[:, :, :], tp[1][:, :, :], ACT.Copy).then_inc(s["t2"], 1)
                            hold(act, s["mm2"], b.n + 1, pa)
                            hold(act, f2_out[b.slot(2)], 16 * b.use(2), pa)
                            hold(act, s["x1"], b.n - 1, pa)
                            nc.scalar.activation(f2o[:, b.slot(2), :, :], mm_b[:, :, 0:F2W], ACT.Copy)\
                                .then_inc(s["f2"], 1)
                    pipeline(act, U, 3, unit)

                @block.vector
                def _(dve):
                    pv = ph.passed["dve"]
                    V = nc.vector
                    link = Chain(dve, link_sem)
                    link(V.memset(st[:, :, :], 1.0))
                    link(V.memset(var[:, :], 1.0))

                    def unit(at):
                        a, b, c, d = at, at.back(1), at.back(2), at.back(3)
                        link.restart()
                        if b.alive(U):
                            hold(dve, s["f1"], b.n + 1, pv)
                            link(V.tensor_tensor(z[:, :, :], f1o[:, b.slot(2), :, 0:D], both(rb1, D), ALU.add))
                            V.tensor_scalar(zm[:, :, :], z[:, :, :], 0.0, None, ALU.min).then_inc(s["zm"], 1)
                        if d.alive(U):
                            hold(dve, s["mm3"], d.n + 1, pv)
                            link(V.tensor_tensor(hr[:, :, :], mm_ac[:, :, 0:F2W], both(rbl, F2W), ALU.add))
                            V.tensor_scalar(em[:, :], hr[:, :, 258], -87.0, None, ALU.max).then_inc(s["hr"], 1)
                        if c.alive(U):
                            hold(dve, s["f2"], c.n + 1, pv)
                            hold(dve, s["xb"], c.n + 1, pv)
                            V.tensor_tensor(xb[:, c.slot(4), :, :], xb[:, c.slot(4), :, :],
                                            f2o[:, c.slot(2), :, 0:D], ALU.add).then_inc(s["x1"], 1)
                            hold(dve, s["x1"], c.n + 1, pv)
                            for r in range(2):
                                last = V.bn_stats(st[:, 2 + r, :], xb[:, c.slot(4), r, :])
                        if a.alive(U):
                            hold(dve, x_in[a.slot(2)], 16 * (a.use(2) + 1), pv)
                            for r in range(2):
                                last = V.bn_stats(st[:, r, :], xin[:, a.slot(2), r, :])
                        if a.alive(U) or c.alive(U):
                            link(last)
                            V.tensor_tensor(dm[:, :], st[:, :, 1], st[:, :, 4], ALU.subtract)
                            V.tensor_tensor(mean[:, :], st[:, :, 1], st[:, :, 4], ALU.add)
                            link(V.tensor_tensor(var[:, 0:4], st[:, :, 2], st[:, :, 5], ALU.add))
                            link(V.tensor_tensor(dm[:, :], dm[:, :], dm[:, :], ALU.mult))
                            link(V.scalar_tensor_tensor(var[:, 0:4], dm[:, :], D / 4.0, var[:, 0:4],
                                                        ALU.mult, ALU.add))
                            link(V.tensor_scalar(var[:, 0:4], var[:, 0:4], 1.0 / D, 1e-5, ALU.mult, ALU.add))
                        if d.alive(U):
                            hold(dve, s["sq"], d.n + 1, pv)
                            link(V.tensor_scalar(var[:, 4:6], n2[:, :], 1e-24, None, ALU.max))
                        hold(dve, s["h1"], min_int(a.n - 1, U), pv)
                        hold(dve, s["h2"], c.n - 1, pv)
                        rsq = rt[:, at.slot(2), :]
                        rsqrt(nc, link, rsq, var[:, :], ra[:, :])
                        if a.alive(U) or c.alive(U):
                            V.scalar_tensor_tensor(nm[:, at.slot(2), :], mean[:, :], -0.5, rsq[:, 0:4],
                                                   ALU.mult, ALU.mult).then_inc(s["stats"], 1)
                        if b.alive(U):
                            hold(dve, s["exp"], b.n + 1, pv)
                            hold(dve, s["tp1"], b.n - 1, pv)
                            V.scalar_tensor_tensor(g[:, b.slot(2), :, :], zm[:, :, :], -1.0, z[:, :, :],
                                                   ALU.add, ALU.max).then_inc(s["g"], 1)
                        if d.alive(U):
                            magnitude(nc, link, fac[:, :], em[:, :], rsq[:, 4:6])
                            link(V.tensor_tensor(un[:, :], n2[:, :], rsq[:, 4:6], ALU.mult))
                            link(V.tensor_tensor(un[:, :], un[:, :], fac[:, :], ALU.mult))
                            link(V.tensor_scalar(unc[:, :], un[:, :], 1e-15, None, ALU.max))
                            dve.sem_inc(s["unc"], 1)
                            hold(dve, hl_out[d.slot(2)], 16 * d.use(2), pv)
                            for r in range(2):
                                last = V.tensor_scalar(ho[:, d.slot(2), r, :], hr[:, r, :], fac[:, r:r + 1], None,
                                                       ALU.mult)
                            last.then_inc(s["ho"], 1)
                            hold(dve, s["tanh"], d.n + 1, pv)
                            expmap_scale(nc, link, ga[:, :], th[:, :], un[:, :], unc[:, :], gb[:, :], gc[:, :])
                            link(V.tensor_tensor(ga[:, :], ga[:, :], fac[:, :], ALU.mult))
                            hold(dve, x3_out[d.slot(2)], 16 * d.use(2), pv)
                            hold(dve, s["oo"], d.n - 1, pv)
                            for r in range(2):
                                last = V.scalar_tensor_tensor(x3o[:, d.slot(2), r, :], hr[:, r, 0:D], ga[:, r:r + 1],
                                                              xb[:, d.slot(4), r, :], ALU.mult, ALU.add)
                            last.then_inc(s["x3"], 1)
                    pipeline(dve, U, 3, unit)
        deg_stack.close()

        def tile_of(row, at):
            return row[:, bass.ds(at.n * P, P)]

        def softmax_weights(table, piece, width, col_src, col_dst, scores, first=False):
            gathered = ExitStack()
            raw_s = sb(f"raw_s{Phase.count}", [P, T, width], on=gathered)
            raw_d = sb(f"raw_d{Phase.count}", [P, T, width], on=gathered)
            with Phase() as ph:
                got = ph.sb("got", [P, 2, CH, 2, width])
                ix = ph.sb("ix", [P, 2, CH, 7], I32)
                got_in, taken, ix_ready = gathered_in[0][0:2], ph.sem("taken"), ph.sem("ix_ready")
                view = table.rearrange("n (q w) -> (n q) w", w=width)
                with nc.Block() as block:
                    @block.gpsimd
                    def _(pool):
                        pp = ph.passed["pool"]
                        bound = pool.to_reg(N * piece - 1)

                        def chunk(at):
                            sl = at.slot(2)
                            hold(pool, taken, at.n - 1, pp)
                            nc.gpsimd.tensor_copy(ix[:, sl, :, :], index[:, bass.ds(at.n * CH, CH), :])\
                                .then_inc(ix_ready, 1)
                            hold(pool, ix_ready, at.n + 1, pp)
                            for r in range(CH):
                                for k, col in ((0, col_src), (1, col_dst)):
                                    nc.gpsimd.indirect_dma_start(
                                        out=got[:, sl, r, k, :], out_offset=None, in_=view,
                                        in_offset=bass.IndirectOffsetOnAxis(ap=ix[:, sl, r, col:col + 1], axis=0),
                                        bounds_check=bound, oob_is_err=False).then_inc(got_in[sl].sem, 16)
                        pipeline(pool, NC, 0, chunk)

                    @block.vector
                    def _(dve):
                        def chunk(at):
                            sl = at.slot(2)
                            hold(dve, got_in[sl], 32 * CH * (at.use(2) + 1), ph.passed["dve"])
                            nc.vector.tensor_copy(raw_s[:, bass.ds(at.n * CH, CH), :], got[:, sl, :, 0, :])
                            nc.vector.tensor_copy(raw_d[:, bass.ds(at.n * CH, CH), :], got[:, sl, :, 1, :])\
                                .then_inc(taken, 1)
                        pipeline(dve, NC, 0, chunk)
                for k in range(2):
                    got_in[k].base += 32 * CH * ((NC + 1 - k) // 2)

            def by_chunk(a):
                return a.rearrange("p (c r) h -> p r c h", r=CH)

            with Phase() as ph:
                logit = ph.sb("logit", [P, CH, P])
                own = ph.sb("own", [P, CH, P])
                key = ph.sb("key", [P, CH, P])
                lt = ph.sb("lt", [P, CE])
                kt = ph.sb("kt", [P, CE])
                fwd = ph.sb("fwd", [P, CE])
                bwd = ph.sb("bwd", [P, CE])
                pen_s = ph.sb("pen_s", [P, CE])
                pen_l = ph.sb("pen_l", [P, CE])
                diag = ph.sb("diag", [P, 4, P])
                ones = ph.sb("ones", [P, P])
                xr = ph.sb("xr", [P, 4, P])
                eq = ph.sb("eq", [P, 4, P])
                mx = ph.sb("mx", [P, 4])
                both_mx = ph.sb("both_mx", [P, 2])
                ps_l = ph.ps("ps_l", [P, 1024])
                ps_k = ph.ps("ps_k", [P, 1024])
                ps_x = ph.ps("ps_x", [P, 4, P])
                s_ch, s_v, s_pe, s_a = ph.sem("s_ch"), ph.sem("s_v"), ph.sem("s_pe"), ph.sem("s_a")
                with nc.Block() as block:
                    @block.tensor
                    def _(pe):
                        pe.wait_ge(s_v, 1)
                        for r in range(CH):
                            nc.tensor.transpose(ps_l[:, r * P:(r + 1) * P], logit[:, r, :], ident[:, :])
                            last = nc.tensor.transpose(ps_k[:, r * P:(r + 1) * P], key[:, r, :], ident[:, :])
                        last.then_inc(s_pe, 1)
                        pe.wait_ge(s_v, 2)
                        nc.tensor.matmul(ps_x[:, :, :], ones[:, :], diag[:, :, :], start=True, stop=True)\
                            .then_inc(s_pe, 1)
                        pe.wait_ge(s_v, 3)
                        for r in range(CH):
                            last = nc.tensor.transpose(ps_l[:, r * P:(r + 1) * P], bwd[:, r * P:(r + 1) * P],
                                                       ident[:, :])
                        last.then_inc(s_pe, 1)

                    @block.scalar
                    def _(act):
                        act.wait_ge(s_v, 4)
                        nc.scalar.activation(w_edge[:, :, :], w_edge[:, :, :], ACT.Exp)
                        nc.scalar.activation(w_self[:, :, :], w_self[:, :, :], ACT.Exp).then_inc(s_a, 1)
                        act.wait_ge(s_a, 1)

                    @block.vector
                    def _(dve):
                        link = Chain(dve, s_ch)
                        V = nc.vector
                        link(V.memset(logit[:, :, :], -BIG))
                        link(V.memset(own[:, :, :], 0.0))
                        link(V.memset(key[:, :, :], -1.0))
                        link(V.memset(ones[:, :], 1.0))

                        def heads(a):
                            return a[:, :, 0:CQ].rearrange("p r (c h) -> p r c h", h=HQ)
                        dst_rc = dst_col[:, :].rearrange("p (c r) -> p r c", r=CH)
                        for h in range(HQ):
                            link(V.tensor_scalar(heads(key)[:, :, :, h], dst_rc, float(HQ), float(h),
                                                 ALU.mult, ALU.add))
                        if scores == "gat":
                            link(V.tensor_tensor(heads(logit), by_chunk(raw_s[:, :, 0:HQ]),
                                                 by_chunk(raw_d[:, :, HQ:2 * HQ]), ALU.add))
                            link(V.tensor_tensor(heads(own), by_chunk(raw_d[:, :, 0:HQ]),
                                                 by_chunk(raw_d[:, :, HQ:2 * HQ]), ALU.add))
                            for a in (logit, own):
                                link(V.scalar_tensor_tensor(a[:, :, 0:CQ], a[:, :, 0:CQ], 0.2, a[:, :, 0:CQ],
                                                            ALU.mult, ALU.max))
                        else:
                            for h in range(HQ):
                                link(V.tensor_tensor(heads(logit)[:, :, :, h],
                                                     raw_s[:, :, 0].rearrange("p (c r) -> p r c", r=CH),
                                                     raw_d[:, :, 1].rearrange("p (c r) -> p r c", r=CH), ALU.add))
                        if first:
                            link(V.tensor_tensor(norm[:, :], raw_s[:, :, 8], raw_d[:, :, 9], ALU.mult))
                            link(V.tensor_scalar(norm[:, :], norm[:, :], 1e-12, None, ALU.add))
                            rsqrt(nc, link, fwd[:, 0:T], norm[:, :], bwd[:, 0:T])
                            link(V.tensor_tensor(norm[:, :], fwd[:, 0:T], ew[:, :], ALU.mult))
                        dve.sem_inc(s_v, 1)
                        dve.wait_ge(s_pe, 1)
                        link(V.tensor_copy(lt[:, :], ps_l[:, 0:CE]))
                        link(V.tensor_copy(kt[:, :], ps_k[:, 0:CE]))
                        link(V.memset(pen_s[:, 0:1], 0.0))
                        link(V.memset(pen_l[:, CE - 1:CE], 0.0))
                        link(V.tensor_tensor(fwd[:, 1:CE], kt[:, 1:CE], kt[:, 0:CE - 1], ALU.is_equal))
                        link(V.tensor_scalar(pen_s[:, 1:CE], fwd[:, 1:CE], -1.0, BIG, ALU.add, ALU.mult))
                        link(V.tensor_copy(pen_l[:, 0:CE - 1], pen_s[:, 1:CE]))
                        link(V.tensor_tensor_scan(fwd[:, :], pen_s[:, :], lt[:, :], -BIG, ALU.add, ALU.max))
                        link(V.tensor_tensor_scan(bwd[:, ::-1], pen_l[:, ::-1], fwd[:, ::-1], -BIG,
                                                  ALU.add, ALU.max))
                        ends = (bwd[:, 0:1], bwd[:, CE - 1:CE], kt[:, 0:1], kt[:, CE - 1:CE])
                        for k, e in enumerate(ends):
                            link(V.tensor_scalar(diag[:, k, :], ident[:, :], e, None, ALU.mult))
                        dve.sem_inc(s_v, 1)
                        dve.wait_ge(s_pe, 2)
                        link(V.tensor_copy(xr[:, :, :], ps_x[:, :, :]))
                        for k in range(2):
                            for m in range(2):
                                link(V.tensor_scalar(eq[:, 2 * k + m, :], xr[:, 2 + m, :], ends[2 + k], -1.0,
                                                     ALU.is_equal, ALU.add))
                                link(V.scalar_tensor_tensor(eq[:, 2 * k + m, :], eq[:, 2 * k + m, :], BIG,
                                                            xr[:, m, :], ALU.mult, ALU.add))
                        link(V.tensor_reduce(both_mx[:, :], eq[:, :, :].rearrange("p (k m) q -> p k (m q)", k=2),
                                             axis=AX.X, op=ALU.max))
                        for k in range(2):
                            link(V.tensor_scalar(lt[:, :], kt[:, :], ends[2 + k], -1.0, ALU.is_equal, ALU.add))
                            link(V.tensor_scalar(lt[:, :], lt[:, :], BIG, both_mx[:, k:k + 1], ALU.mult, ALU.add))
                            link(V.tensor_tensor(bwd[:, :], bwd[:, :], lt[:, :], ALU.max))
                        dve.sem_inc(s_v, 1)
                        dve.wait_ge(s_pe, 3)
                        top = fwd[:, :].rearrange("p (r q) -> p r q", r=CH)
                        link(V.tensor_copy(fwd[:, :], ps_l[:, 0:CE]))
                        if scores == "gat":
                            link(V.tensor_tensor(top[:, :, 0:CQ], top[:, :, 0:CQ], own[:, :, 0:CQ], ALU.max))
                        else:
                            link(V.tensor_scalar(fwd[:, :], fwd[:, :], -1e9, None, ALU.max))
                        for a, w in ((logit, w_edge), (own, w_self)):
                            link(V.tensor_tensor(a[:, :, 0:CQ], a[:, :, 0:CQ], top[:, :, 0:CQ], ALU.subtract))
                            link(V.tensor_copy(by_chunk(w[:, :, :]), heads(a)))
                        dve.sem_inc(s_v, 1)
            gathered.close()

        class EdgePass(Phase):

            def __init__(self, width, columns, gathers, scatter, lag):
                self.width, self.columns, self.lag = width, columns, lag
                self.gathers, self.scatter = gathers, scatter

            def __enter__(self):
                Phase.__enter__(self)
                self.sel = self.sb("sel", [P, 2, P])
                self.carry = self.sb("carry", [P, 2, P])
                self.msg = self.sb("msg", [P, 2, self.columns])
                self.rows = self.sb("rows", [P, 2, self.columns])
                self.ix = self.sb("ix", [P, 4, 4], I32)
                self.ix_put = self.sb("ix_put", [P, 4, 1], I32)
                self.got = [self.sb(f"got{k}", [P, 4, t.shape[1]]) for k, (t, c) in enumerate(self.gathers)]
                self.put = self.sb("put", [P, 2, self.scatter.shape[1]])
                self.warm = self.sb("warm", [P, 1])
                self.acc = [self.ps(f"acc{k}", [P, 512]) for k in range(2)]
                self.got_in = [gathered_in[k] for k in range(len(self.gathers))]
                self.put_out = scattered_out
                self.done = {k: self.sem(k) for k in ("ix", "msg", "acc", "rows", "used", "put", "start", "ix_put",
                                                      "warm", "ch")}
                return self

            def step(self, *names):
                for k in names:
                    self.done[k] = self.sem(k)

            def start_pool(self, pool):
                nc.gpsimd.memset(self.rows[:, :, :], 0.0)
                nc.gpsimd.memset(self.put[:, :, :], 0.0)
                nc.gpsimd.memset(self.warm[:, :], 0.0).then_inc(self.done["start"], 1)
                pool.wait_ge(self.done["start"], 1)

            def start_act(self, act):
                act.wait_ge(self.done["start"], 1)
                nc.scalar.activation(self.warm[:, :], self.warm[:, :], ACT.Exp).then_inc(self.done["warm"], 1)
                act.wait_ge(self.done["warm"], 1)

            def gather(self, pool, at, bound):
                hold(pool, self.done["msg"], at.n - 3, self.passed["pool"])
                hold(pool, self.done["used"], at.n - 3, self.passed["pool"])
                self.gather_free(pool, at, bound)

            def gather_free(self, pool, at, bound):
                d, pp, sl = self.done, self.passed["pool"], at.slot(4)
                if self.lag < 4:
                    hold(pool, self.put_out[sl], 16 * at.use(4), pp)
                nc.gpsimd.tensor_copy(self.ix[:, sl, :], index[:, bass.ds(at.n, 1), 0:4]).then_inc(d["ix"], 1)
                hold(pool, d["ix"], at.n + 1, pp)
                for (table, col), buf, sem in zip(self.gathers, self.got, self.got_in):
                    nc.gpsimd.indirect_dma_start(
                        out=buf[:, sl, :], out_offset=None, in_=table,
                        in_offset=bass.IndirectOffsetOnAxis(ap=self.ix[:, sl, col:col + 1], axis=0),
                        bounds_check=bound, oob_is_err=False).then_inc(sem[sl].sem, 16)

            def scatter_rows(self, pool, at, bound):
                d, pp, sl = self.done, self.passed["pool"], at.slot(4)
                ix = self.ix[:, sl, 2:3]
                if self.lag >= 4:
                    ix = self.ix_put[:, sl, :]
                    hold(pool, self.put_out[sl], 16 * at.use(4), pp)
                    nc.gpsimd.tensor_copy(ix, index[:, bass.ds(at.n, 1), 2]).then_inc(d["ix_put"], 1)
                    hold(pool, d["ix_put"], at.n + 1, pp)
                hold(pool, d["put"], at.n + 1, pp)
                nc.gpsimd.indirect_dma_start(
                    out=self.scatter, in_=self.put[:, at.slot(2), :], in_offset=None,
                    out_offset=bass.IndirectOffsetOnAxis(ap=ix, axis=0),
                    bounds_check=bound, oob_is_err=False).then_inc(self.put_out[at.slot(4)].sem, 16)

            def free_put(self, eng, at, passed):
                if type(at.n) is int and at.n < 2:
                    return
                j = at.back(2)
                hold(eng, self.put_out[j.slot(4)], 16 * (j.use(4) + 1), passed)

            def end_pool(self, pool):
                for k in range(4):
                    hold(pool, self.put_out[k], 16 * ((T + 3 - k) // 4), None)

            def __exit__(self, *err):
                for group in (*self.got_in, self.put_out):
                    for k in range(4):
                        group[k].base += 16 * ((T + 3 - k) // 4)
                return Phase.__exit__(self, *err)

            def select(self, dve, at):
                V, sl, col = nc.vector, at.slot(2), bass.ds(at.n, 1)
                V.tensor_scalar(self.sel[:, sl, :], tile_of(dst_row, at), dst_col[:, col], None, ALU.is_equal)
                V.tensor_scalar(self.carry[:, sl, :], tile_of(dst_row, at), carry_col[:, col], None,
                                ALU.is_equal).then_inc(self.done["msg"], 1)

            def accumulate(self, pe, at):
                d, pp, sl = self.done, self.passed["pe"], at.slot(2)
                hold(pe, d["msg"], at.n + 1, pp)
                hold(pe, d["rows"], at.n - 1, pp)
                acc = self.acc[sl][:, 0:self.width]
                nc.tensor.matmul(acc, self.sel[:, sl, :], self.msg[:, sl, 0:self.width], start=True, stop=False)
                hold(pe, d["rows"], at.n, pp)
                if type(at.n) is int and at.n == 0:
                    pe.wait_ge(d["start"], 1)
                nc.tensor.matmul(acc, self.carry[:, sl, :], self.rows[:, 1 - sl, 0:self.width], start=False,
                                 stop=True).then_inc(d["acc"], 1)

            def take_rows(self, act, at):
                hold(act, self.done["used"], at.n - 1, self.passed["act"])
                self.take_rows_free(act, at)

            def take_rows_free(self, act, at):
                d, pa = self.done, self.passed["act"]
                hold(act, d["acc"], at.n + 1, pa)
                nc.scalar.activation(self.rows[:, at.slot(2), 0:self.width], self.acc[at.slot(2)][:, 0:self.width],
                                     ACT.Copy).then_inc(d["rows"], 1)

        def turn(nc, rows2, bank):
            for k in range(KB):
                last = nc.tensor.transpose(bank[:, k, :], rows2[:, k * P:(k + 1) * P], ident[:, :])
            return last

        def product(acc, lhs, w):
            for k in range(KB):
                last = nc.tensor.matmul(acc, lhs[:, k, :], w[:, k, :], start=(k == 0), stop=(k == KB - 1))
            return last

        def head_view(a):
            return a.rearrange("p (h c) -> p h c", h=HQ)

        def per_head(w, at, c):
            return w[:, bass.ds(at.n, 1), :].rearrange("p a h -> p (a h)").unsqueeze(2).to_broadcast([P, HQ, c])

        def edge_rows(table, at):
            return table[bass.ds(at.n * P, P), :]

        def gat_message(dve, ph, at):
            pv = ph.passed["dve"]
            hold(dve, ph.got_in[0][at.slot(4)], 16 * (at.use(4) + 1), pv)
            hold(dve, ph.done["acc"], at.n - 1, pv)
            nc.vector.tensor_tensor(head_view(ph.msg[:, at.slot(2), 0:D]), head_view(ph.got[0][:, at.slot(4), 0:D]),
                                    per_head(w_edge, at, D // HQ), ALU.mult)
            nc.vector.tensor_copy(ph.msg[:, at.slot(2), D:D + HQ], w_edge[:, bass.ds(at.n, 1), :])
            ph.select(dve, at)

        def gat_output(link, ph, at, o, own, den):
            V, rows = nc.vector, ph.rows[:, at.slot(2), :]
            V.tensor_tensor(head_view(o), head_view(own), per_head(w_self, at, D // HQ), ALU.mult)
            link(V.scalar_tensor_tensor(den, rows[:, D:D + HQ], 1e-16,
                                        w_self[:, bass.ds(at.n, 1), :].rearrange("p a h -> p (a h)"),
                                        ALU.add, ALU.add))
            V.reciprocal(den, den)
            link(V.tensor_tensor(o, o, rows[:, 0:D], ALU.add))
            link(V.tensor_tensor(head_view(o), head_view(o), den.unsqueeze(2).to_broadcast([P, HQ, D // HQ]),
                                 ALU.mult))

        def layernorm_stats(link, st, mean, dm, var):
            V = nc.vector
            V.tensor_tensor(dm, st[:, 1:2], st[:, 4:5], ALU.subtract)
            V.tensor_tensor(mean, st[:, 1:2], st[:, 4:5], ALU.add)
            link(V.tensor_tensor(var, st[:, 2:3], st[:, 5:6], ALU.add))
            link(V.tensor_tensor(dm, dm, dm, ALU.mult))
            link(V.scalar_tensor_tensor(var, dm, D / 4.0, var, ALU.mult, ALU.add))
            link(V.tensor_scalar(var, var, 1.0 / D, 1e-5, ALU.mult, ALU.add))

        softmax_weights(F1, 17, 16, 3, 4, "gat", first=True)
        with EdgePass(D + HQ, D + HQ, [(F1, 0), (F1, 1)], F2, 2) as ph:
            ph.step("zm", "exp", "g", "tp", "gt", "mm", "fe")
            d = ph.done
            o = ph.sb("o", [P, D])
            zm = ph.sb("zm", [P, D])
            den = ph.sb("den", [P, HQ])
            g = ph.sb("g", [P, D])
            gt = ph.sb("gt", [P, KB, P])
            tp = ph.ps("tp", [P, KB, P])
            mm = ph.ps("mm", [P, 512])
            fe_out = ph.slots("fe_out", 2)
            t7_out = ph.sem("t7_out")
            with nc.Block() as block:
                @block.gpsimd
                def _(pool):
                    ph.start_pool(pool)
                    bound = pool.to_reg(N - 1)

                    def tile(at):
                        if at.alive(T):
                            ph.gather(pool, at, bound)
                        if at.back(ph.lag).alive(T):
                            ph.scatter_rows(pool, at.back(ph.lag), bound)
                    pipeline(pool, T, ph.lag, tile)
                    ph.end_pool(pool)

                @block.sync
                def _(sp):
                    full = N // (4 * P)
                    rest = N - full * 4 * P
                    with sp.Fori(0, full) as k:
                        sp.dma_start(T7[bass.ds(k * (4 * P), 4 * P), :].rearrange("(p r) w -> p (r w)", r=4),
                                     t7_const[:, :, :].rearrange("p r w -> p (r w)")).then_inc(t7_out, 16)
                    if rest:
                        sp.dma_start(T7[full * 4 * P:N, :].rearrange("(p r) w -> p (r w)", r=4),
                                     t7_const[0:rest // 4, :, :].rearrange("p r w -> p (r w)")).then_inc(t7_out, 16)

                    def tile(at):
                        if at.back(1).alive(T):
                            j = at.back(1)
                            hold(sp, d["put"], j.n + 1, ph.passed["sp"])
                            sp.dma_start(edge_rows(FE2, j), ph.put[:, j.slot(2), :]).then_inc(fe_out[j.slot(2)], 16)
                    pipeline(sp, T, 1, tile)
                    for k in range(2):
                        sp.wait_ge(fe_out[k], 16 * ((T + 1 - k) // 2))
                    sp.wait_ge(t7_out, 16 * (full + (1 if rest else 0)))

                @block.vector
                def _(dve):
                    link = Chain(dve, d["ch"])
                    pv = ph.passed["dve"]
                    V = nc.vector

                    def tile(at):
                        link.restart()
                        b = at.back(1)
                        if b.alive(T):
                            hold(dve, d["rows"], b.n + 1, pv)
                            hold(dve, ph.got_in[1][b.slot(4)], 16 * (b.use(4) + 1), pv)
                            gat_output(link, ph, b, o[:, :], ph.got[1][:, b.slot(4), 0:D], den[:, :])
                            link(V.tensor_tensor(o[:, :], o[:, :], rb1[:, :], ALU.add))
                            V.tensor_scalar(zm[:, :], o[:, :], 0.0, None, ALU.min).then_inc(d["zm"], 1)
                            dve.sem_inc(d["used"], 1)
                        if at.alive(T):
                            gat_message(dve, ph, at)
                        if b.alive(T):
                            hold(dve, d["exp"], b.n + 1, pv)
                            hold(dve, d["tp"], b.n, pv)
                            V.scalar_tensor_tensor(g[:, :], zm[:, :], -1.0, o[:, :], ALU.add, ALU.max)\
                                .then_inc(d["g"], 1)
                            hold(dve, d["g"], b.n + 1, pv)
                    pipeline(dve, T, 1, tile)

                @block.tensor
                def _(pe):
                    pp = ph.passed["pe"]

                    def tile(at):
                        if at.alive(T):
                            ph.accumulate(pe, at)
                        b = at.back(1)
                        if b.alive(T):
                            hold(pe, d["g"], b.n + 1, pp)
                            hold(pe, d["gt"], b.n, pp)
                            turn(nc, g[:, :], tp).then_inc(d["tp"], 1)
                            hold(pe, d["gt"], b.n + 1, pp)
                            hold(pe, d["put"], b.n, pp)
                            product(mm[:, 0:F2W], gt, w2).then_inc(d["mm"], 1)
                    pipeline(pe, T, 1, tile)

                @block.scalar
                def _(act):
                    pa = ph.passed["act"]
                    ph.start_act(act)

                    def tile(at):
                        b = at.back(1)
                        if b.alive(T):
                            hold(act, d["zm"], b.n + 1, pa)
                            nc.scalar.activation(zm[:, :], zm[:, :], ACT.Exp).then_inc(d["exp"], 1)
                        if at.alive(T):
                            ph.take_rows(act, at)
                        if b.alive(T):
                            hold(act, d["tp"], b.n + 1, pa)
                            hold(act, d["mm"], b.n, pa)
                            nc.scalar.activation(gt[:, :, :], tp[:, :, :], ACT.Copy).then_inc(d["gt"], 1)
                            hold(act, d["mm"], b.n + 1, pa)
                            ph.free_put(act, b, pa)
                            hold(act, fe_out[b.slot(2)], 16 * b.use(2), pa)
                            nc.scalar.activation(ph.put[:, b.slot(2), :], mm[:, 0:F2W], ACT.Copy)\
                                .then_inc(d["put"], 1)
                    pipeline(act, T, 1, tile)

        softmax_weights(F2, 33, 8, 5, 6, "gat")
        with EdgePass(D + HQ, D + HQ, [(F2, 0), (x, 1)], H2, 2) as ph:
            ph.step("x1", "stats")
            d = ph.done
            fe = ph.sb("fe", [P, 4, F2W])
            o = ph.sb("o", [P, D])
            x1 = ph.sb("x1", [P, 2, D])
            den = ph.sb("den", [P, HQ])
            st, mean, dm = ph.sb("st", [P, 6]), ph.sb("mean", [P, 1]), ph.sb("dm", [P, 1])
            var, ra = ph.sb("var", [P, 1]), ph.sb("ra", [P, 1])
            rt, nm = ph.sb("rt", [P, 2]), ph.sb("nm", [P, 2])
            fe_in, x1_out = ph.slots("fe_in", 4), ph.slots("x1_out", 2)
            with nc.Block() as block:
                @block.gpsimd
                def _(pool):
                    ph.start_pool(pool)
                    bound = pool.to_reg(N - 1)

                    def tile(at):
                        if at.alive(T):
                            ph.gather(pool, at, bound)
                        if at.back(ph.lag).alive(T):
                            ph.scatter_rows(pool, at.back(ph.lag), bound)
                    pipeline(pool, T, ph.lag, tile)
                    ph.end_pool(pool)

                @block.sync
                def _(sp):
                    def tile(at):
                        if at.alive(T):
                            hold(sp, d["used"], at.n - 3, ph.passed["sp"])
                            sp.dma_start(fe[:, at.slot(4), :], edge_rows(FE2, at)).then_inc(fe_in[at.slot(4)], 16)
                        j = at.back(3)
                        if j.alive(T):
                            hold(sp, d["x1"], j.n + 1, ph.passed["sp"])
                            sp.dma_start(edge_rows(XE1, j), x1[:, j.slot(2), :]).then_inc(x1_out[j.slot(2)], 16)
                    pipeline(sp, T, 3, tile)
                    for k in range(2):
                        sp.wait_ge(x1_out[k], 16 * ((T + 1 - k) // 2))

                @block.vector
                def _(dve):
                    link = Chain(dve, d["ch"])
                    pv = ph.passed["dve"]
                    V = nc.vector

                    def tile(at):
                        link.restart()
                        if at.alive(T):
                            gat_message(dve, ph, at)
                        b = at.back(1)
                        if b.alive(T):
                            hold(dve, d["rows"], b.n + 1, pv)
                            hold(dve, fe_in[b.slot(4)], 16 * (b.use(4) + 1), pv)
                            hold(dve, ph.got_in[1][b.slot(4)], 16 * (b.use(4) + 1), pv)
                            gat_output(link, ph, b, o[:, :], fe[:, b.slot(4), 0:D], den[:, :])
                            link(V.tensor_tensor(o[:, :], o[:, :], rb2[:, :], ALU.add))
                            hold(dve, x1_out[b.slot(2)], 16 * b.use(2), pv)
                            hold(dve, d["put"], b.n - 1, pv)
                            V.tensor_tensor(x1[:, b.slot(2), :], o[:, :], ph.got[1][:, b.slot(4), :], ALU.add)\
                                .then_inc(d["x1"], 1)
                            hold(dve, d["x1"], b.n + 1, pv)
                            dve.sem_inc(d["used"], 1)
                            link(V.bn_stats(st[:, :], x1[:, b.slot(2), :]))
                            layernorm_stats(link, st, mean[:, :], dm[:, :], var[:, :])
                            rsq = rt[:, b.slot(2):b.slot(2) + 1]
                            rsqrt(nc, link, rsq, var[:, :], ra[:, :])
                            V.scalar_tensor_tensor(nm[:, b.slot(2):b.slot(2) + 1], mean[:, :], -0.5, rsq,
                                                   ALU.mult, ALU.mult).then_inc(d["stats"], 1)
                    pipeline(dve, T, 1, tile)

                @block.tensor
                def _(pe):
                    pipeline(pe, T, 0, lambda at: ph.accumulate(pe, at))

                @block.scalar
                def _(act):
                    pa = ph.passed["act"]
                    ph.start_act(act)

                    def tile(at):
                        if at.alive(T):
                            ph.take_rows(act, at)
                        b = at.back(1)
                        if b.alive(T):
                            hold(act, d["stats"], b.n + 1, pa)
                            ph.free_put(act, b, pa)
                            sl = b.slot(2)
                            nc.scalar.activation(ph.put[:, sl, :], x1[:, sl, :], ACT.Relu, bias=nm[:, sl:sl + 1],
                                                 scale=rt[:, sl:sl + 1]).then_inc(d["put"], 1)
                    pipeline(act, T, 1, tile)

        NH = 8
        with EdgePass(D + NH, D + NH, [(H2, 0), (H2, 1)], HL, 5) as ph:
            ph.step("tp", "ht", "kv", "q", "score", "exp", "qm", "x2", "stats", "h", "tp3", "h3", "mm", "hr", "sq", "xl")
            d = ph.done
            xe = ph.sb("xe", [P, 4, D])
            ht = ph.sb("ht", [P, 4, P])
            qs = ph.sb("qs", [P, 2, D])
            pr = ph.sb("pr", [P, D])
            sc = ph.sb("sc", [P, 2, NH])
            o = ph.sb("o", [P, D])
            x2 = ph.sb("x2", [P, 2, D])
            den = ph.sb("den", [P, NH])
            h = ph.sb("h", [P, D])
            h3 = ph.sb("h3", [P, KB, P])
            hr = ph.sb("hr", [P, F2W])
            sq = ph.sb("sq", [P, D])
            em, n2, fac = ph.sb("em", [P, 1]), ph.sb("n2", [P, 1]), ph.sb("fac", [P, 1])
            st, mean, dm = ph.sb("st", [P, 6]), ph.sb("mean", [P, 1]), ph.sb("dm", [P, 1])
            var, ra = ph.sb("var", [P, 2]), ph.sb("ra", [P, 2])
            rt, nm = ph.sb("rt", [P, 2, 2]), ph.sb("nm", [P, 2])
            tp = ph.ps("tp", [P, 4, P])
            kv = [ph.ps(f"kv{k}", [P, 2 * D]) for k in range(2)]
            qp = ph.ps("qp", [P, D])
            tp3 = ph.ps("tp3", [P, KB, P])
            mm = ph.ps("mm", [P, 512])
            xe_in, x2_out, he_out = ph.slots("xe_in", 4), ph.slots("x2_out", 2), ph.slots("he_out", 2)
            with nc.Block() as block:
                @block.gpsimd
                def _(pool):
                    ph.start_pool(pool)
                    bound = pool.to_reg(N - 1)

                    def tile(at):
                        if at.alive(T):
                            hold(pool, d["tp"], at.n - 3, ph.passed["pool"])
                            ph.gather_free(pool, at, bound)
                        if at.back(ph.lag).alive(T):
                            ph.scatter_rows(pool, at.back(ph.lag), bound)
                    pipeline(pool, T, ph.lag, tile)
                    ph.end_pool(pool)

                @block.sync
                def _(sp):
                    ps = ph.passed["sp"]

                    def tile(at):
                        if at.alive(T):
                            hold(sp, d["xl"], at.n - 3, ps)
                            sp.dma_start(xe[:, at.slot(4), :], edge_rows(XE1, at)).then_inc(xe_in[at.slot(4)], 16)
                        j = at.back(3)
                        if j.alive(T):
                            hold(sp, d["x2"], j.n + 1, ps)
                            sp.dma_start(edge_rows(XE2, j), x2[:, j.slot(2), :]).then_inc(x2_out[j.slot(2)], 16)
                        j = at.back(4)
                        if j.alive(T):
                            hold(sp, d["put"], j.n + 1, ps)
                            sp.dma_start(edge_rows(HE2, j), ph.put[:, j.slot(2), 0:D]).then_inc(he_out[j.slot(2)], 16)
                    pipeline(sp, T, 4, tile)
                    for k in range(2):
                        sp.wait_ge(x2_out[k], 16 * ((T + 1 - k) // 2))
                        sp.wait_ge(he_out[k], 16 * ((T + 1 - k) // 2))

                @block.tensor
                def _(pe):
                    pp = ph.passed["pe"]

                    def tile(at):
                        if at.alive(T):
                            for k in range(2):
                                hold(pe, ph.got_in[k][at.slot(4)], 16 * (at.use(4) + 1), pp)
                            hold(pe, d["ht"], at.n, pp)
                            turn(nc, ph.got[0][:, at.slot(4), :], tp[:, 0:2, :])
                            turn(nc, ph.got[1][:, at.slot(4), :], tp[:, 2:4, :]).then_inc(d["tp"], 1)
                        c = at.back(2)
                        if c.alive(T):
                            ph.accumulate(pe, c)
                        e = at.back(3)
                        if e.alive(T):
                            hold(pe, d["h"], e.n + 1, pp)
                            hold(pe, d["h3"], e.n, pp)
                            turn(nc, h[:, :], tp3).then_inc(d["tp3"], 1)
                        if at.alive(T):
                            hold(pe, d["ht"], at.n + 1, pp)
                            hold(pe, d["msg"], at.n - 1, pp)
                            product(kv[at.slot(2)][:, :], ht[:, 0:2, :], wkv).then_inc(d["kv"], 1)
                            hold(pe, d["q"], at.n, pp)
                            product(qp[:, :], ht[:, 2:4, :], wq).then_inc(d["qm"], 1)
                        if e.alive(T):
                            hold(pe, d["h3"], e.n + 1, pp)
                            hold(pe, d["hr"], e.n, pp)
                            product(mm[:, 0:F2W], h3, wl).then_inc(d["mm"], 1)
                    pipeline(pe, T, 3, tile)

                @block.vector
                def _(dve):
                    link = Chain(dve, d["ch"])
                    pv = ph.passed["dve"]
                    V = nc.vector
                    link(V.memset(var[:, :], 1.0))

                    def tile(at):
                        link.restart()
                        b, c, e, f = at.back(1), at.back(2), at.back(3), at.back(4)
                        if b.alive(T):
                            hold(dve, d["kv"], b.n + 1, pv)
                            hold(dve, d["q"], b.n + 1, pv)
                            link(V.tensor_tensor(pr[:, :], kv[b.slot(2)][:, 0:D], qs[:, b.slot(2), :], ALU.mult))
                            score = sc[:, b.slot(2), :]
                            hold(dve, d["exp"], b.n - 1, pv)
                            link(V.tensor_reduce(score, pr[:, :].rearrange("p (h c) -> p h c", h=NH),
                                                 axis=AX.X, op=ALU.add))
                            link(V.tensor_scalar(score, score, float((D // NH) ** -0.5), 5.0, ALU.mult, ALU.min))
                            V.tensor_scalar(score, score, -5.0, None, ALU.max).then_inc(d["score"], 1)
                        if f.alive(T):
                            hold(dve, d["mm"], f.n + 1, pv)
                            link(V.tensor_tensor(hr[:, :], mm[:, 0:F2W], rbl[:, :], ALU.add))
                            V.tensor_scalar(em[:, :], hr[:, 258:259], -87.0, None, ALU.max).then_inc(d["hr"], 1)
                        if e.alive(T):
                            hold(dve, d["rows"], e.n + 1, pv)
                            hold(dve, xe_in[e.slot(4)], 16 * (e.use(4) + 1), pv)
                            rows = ph.rows[:, e.slot(2), :]
                            link(V.tensor_scalar(den[:, :], rows[:, D:D + NH], 1e-9, None, ALU.add))
                            link(V.reciprocal(den[:, :], den[:, :]))
                            link(V.tensor_tensor(o[:, :].rearrange("p (h c) -> p h c", h=NH),
                                                 rows[:, 0:D].rearrange("p (h c) -> p h c", h=NH),
                                                 den[:, :].unsqueeze(2).to_broadcast([P, NH, D // NH]), ALU.mult))
                            dve.sem_inc(d["used"], 1)
                            hold(dve, x2_out[e.slot(2)], 16 * e.use(2), pv)
                            hold(dve, d["h"], e.n - 1, pv)
                            V.tensor_tensor(x2[:, e.slot(2), :], o[:, :], xe[:, e.slot(4), :], ALU.add)\
                                .then_inc(d["x2"], 1)
                            hold(dve, d["x2"], e.n + 1, pv)
                            dve.sem_inc(d["xl"], 1)
                            link(V.bn_stats(st[:, :], x2[:, e.slot(2), :]))
                            layernorm_stats(link, st, mean[:, :], dm[:, :], var[:, 0:1])
                        if c.alive(T):
                            hold(dve, d["exp"], c.n + 1, pv)
                            hold(dve, d["acc"], c.n - 1, pv)
                            V.tensor_tensor(ph.msg[:, c.slot(2), 0:D].rearrange("p (h c) -> p h c", h=NH),
                                            kv[c.slot(2)][:, D:2 * D].rearrange("p (h c) -> p h c", h=NH),
                                            sc[:, c.slot(2), :].unsqueeze(2).to_broadcast([P, NH, D // NH]), ALU.mult)
                            V.tensor_copy(ph.msg[:, c.slot(2), D:D + NH], sc[:, c.slot(2), :])
                            ph.select(dve, c)
                        if f.alive(T):
                            hold(dve, d["sq"], f.n + 1, pv)
                            link(V.tensor_scalar(var[:, 1:2], n2[:, :], 1e-24, None, ALU.max))
                        if e.alive(T) or f.alive(T):
                            rsq = rt[:, e.slot(2), :]
                            rsqrt(nc, link, rsq, var[:, :], ra[:, :])
                        if e.alive(T):
                            V.scalar_tensor_tensor(nm[:, e.slot(2):e.slot(2) + 1], mean[:, :], -0.5, rsq[:, 0:1],
                                                   ALU.mult, ALU.mult).then_inc(d["stats"], 1)
                        if f.alive(T):
                            magnitude(nc, link, fac[:, :], em[:, :], rsq[:, 1:2])
                            ph.free_put(dve, f, pv)
                            hold(dve, he_out[f.slot(2)], 16 * f.use(2), pv)
                            V.tensor_scalar(ph.put[:, f.slot(2), :], hr[:, :], fac[:, 0:1], None, ALU.mult)\
                                .then_inc(d["put"], 1)
                            hold(dve, d["put"], f.n + 1, pv)
                    pipeline(dve, T, 4, tile)

                @block.scalar
                def _(act):
                    pa = ph.passed["act"]
                    ph.start_act(act)

                    def tile(at):
                        b, c, e, f = at.back(1), at.back(2), at.back(3), at.back(4)
                        if b.alive(T):
                            hold(act, d["score"], b.n + 1, pa)
                            nc.scalar.activation(sc[:, b.slot(2), :], sc[:, b.slot(2), :], ACT.Exp)\
                                .then_inc(d["exp"], 1)
                        if f.alive(T):
                            hold(act, d["hr"], f.n + 1, pa)
                            nc.scalar.activation(em[:, :], em[:, :], ACT.Exp, scale=-1.0)
                            nc.scalar.activation(sq[:, :], hr[:, 0:D], ACT.Square, accum_out=n2[:, :])\
                                .then_inc(d["sq"], 1)
                        if at.alive(T):
                            hold(act, d["tp"], at.n + 1, pa)
                            hold(act, d["qm"], at.n, pa)
                            nc.scalar.activation(ht[:, :, :], tp[:, :, :], ACT.Copy).then_inc(d["ht"], 1)
                        if c.alive(T):
                            ph.take_rows(act, c)
                        if e.alive(T):
                            hold(act, d["stats"], e.n + 1, pa)
                            hold(act, d["tp3"], e.n, pa)
                            sl = e.slot(2)
                            nc.scalar.activation(h[:, :], x2[:, sl, :], ACT.Relu, bias=nm[:, sl:sl + 1],
                                                 scale=rt[:, sl, 0:1]).then_inc(d["h"], 1)
                            hold(act, d["tp3"], e.n + 1, pa)
                            hold(act, d["mm"], e.n, pa)
                            nc.scalar.activation(h3[:, :, :], tp3[:, :, :], ACT.Copy).then_inc(d["h3"], 1)
                        if at.alive(T):
                            hold(act, d["qm"], at.n + 1, pa)
                            hold(act, d["score"], at.n - 1, pa)
                            nc.scalar.activation(qs[:, at.slot(2), :], qp[:, :], ACT.Copy).then_inc(d["q"], 1)
                    pipeline(act, T, 4, tile)

        softmax_weights(HL, 33, 8, 5, 6, "hyperbolic")
        with EdgePass(D + 2, D + 2, [(HL, 0)], X3, 2) as ph:
            ph.step("hc", "sq", "unc", "tanh")
            d = ph.done
            xe = ph.sb("xe", [P, 4, D])
            he = ph.sb("he", [P, 4, D])
            hc = ph.sb("hc", [P, D])
            sq = ph.sb("sq", [P, D])
            den, n2, th = ph.sb("den", [P, 1]), ph.sb("n2", [P, 1]), ph.sb("th", [P, 1])
            var, ra, rt = ph.sb("var", [P, 1]), ph.sb("ra", [P, 1]), ph.sb("rt", [P, 1])
            un, unc = ph.sb("un", [P, 1]), ph.sb("unc", [P, 1])
            ga, gb, gc = ph.sb("ga", [P, 1]), ph.sb("gb", [P, 1]), ph.sb("gc", [P, 1])
            e_in, x3_out = ph.slots("e_in", 4), ph.slots("x3_out", 2)
            with nc.Block() as block:
                @block.gpsimd
                def _(pool):
                    ph.start_pool(pool)
                    bound = pool.to_reg(N - 1)

                    def tile(at):
                        if at.alive(T):
                            ph.gather(pool, at, bound)
                        if at.back(ph.lag).alive(T):
                            ph.scatter_rows(pool, at.back(ph.lag), bound)
                    pipeline(pool, T, ph.lag, tile)
                    ph.end_pool(pool)

                @block.sync
                def _(sp):
                    ps = ph.passed["sp"]

                    def tile(at):
                        if at.alive(T):
                            hold(sp, d["put"], at.n - 3, ps)
                            sp.dma_start(xe[:, at.slot(4), :], edge_rows(XE2, at)).then_inc(e_in[at.slot(4)], 16)
                            sp.dma_start(he[:, at.slot(4), :], edge_rows(HE2, at)).then_inc(e_in[at.slot(4)], 16)
                        j = at.back(2)
                        if j.alive(T):
                            hold(sp, d["put"], j.n + 1, ps)
                            sp.dma_start(edge_rows(XE3, j), ph.put[:, j.slot(2), :]).then_inc(x3_out[j.slot(2)], 16)
                    pipeline(sp, T, 2, tile)
                    for k in range(2):
                        sp.wait_ge(x3_out[k], 16 * ((T + 1 - k) // 2))

                @block.vector
                def _(dve):
                    link = Chain(dve, d["ch"])
                    pv = ph.passed["dve"]
                    V = nc.vector

                    def tile(at):
                        link.restart()
                        b = at.back(1)
                        if b.alive(T):
                            hold(dve, d["rows"], b.n + 1, pv)
                            hold(dve, e_in[b.slot(4)], 32 * (b.use(4) + 1), pv)
                            link(V.tensor_scalar(den[:, :], ph.rows[:, b.slot(2), D:D + 1], 1e-10, None, ALU.add))
                            link(V.reciprocal(den[:, :], den[:, :]))
                            V.scalar_tensor_tensor(hc[:, :], ph.rows[:, b.slot(2), 0:D], den[:, 0:1],
                                                   he[:, b.slot(4), :], ALU.mult, ALU.add).then_inc(d["hc"], 1)
                        if at.alive(T):
                            hold(dve, ph.got_in[0][at.slot(4)], 16 * (at.use(4) + 1), pv)
                            hold(dve, d["acc"], at.n - 1, pv)
                            w = w_edge[:, bass.ds(at.n, 1), :].rearrange("p a h -> p (a h)")
                            V.tensor_scalar(ph.msg[:, at.slot(2), 0:D], ph.got[0][:, at.slot(4), 0:D], w[:, 0:1],
                                            None, ALU.mult)
                            V.tensor_copy(ph.msg[:, at.slot(2), D:D + 2], w[:, 0:2])
                            ph.select(dve, at)
                        if b.alive(T):
                            hold(dve, d["hc"], b.n + 1, pv)
                            dve.sem_inc(d["used"], 1)
                            hold(dve, d["sq"], b.n + 1, pv)
                            link(V.tensor_scalar(var[:, :], n2[:, :], 1e-36, None, ALU.max))
                            rsqrt(nc, link, rt[:, :], var[:, :], ra[:, :])
                            link(V.tensor_tensor(un[:, :], n2[:, :], rt[:, :], ALU.mult))
                            V.tensor_scalar(unc[:, :], un[:, :], 1e-15, None, ALU.max).then_inc(d["unc"], 1)
                            hold(dve, d["tanh"], b.n + 1, pv)
                            hold(dve, d["unc"], b.n + 1, pv)
                            expmap_scale(nc, link, ga[:, :], th[:, :], un[:, :], unc[:, :], gb[:, :], gc[:, :])
                            ph.free_put(dve, b, pv)
                            hold(dve, x3_out[b.slot(2)], 16 * b.use(2), pv)
                            V.scalar_tensor_tensor(ph.put[:, b.slot(2), :], hc[:, :], ga[:, 0:1],
                                                   xe[:, b.slot(4), :], ALU.mult, ALU.add).then_inc(d["put"], 1)
                            hold(dve, d["put"], b.n + 1, pv)
                    pipeline(dve, T, 1, tile)

                @block.tensor
                def _(pe):
                    pipeline(pe, T, 0, lambda at: ph.accumulate(pe, at))

                @block.scalar
                def _(act):
                    pa = ph.passed["act"]
                    ph.start_act(act)

                    def tile(at):
                        b = at.back(1)
                        if b.alive(T):
                            hold(act, d["hc"], b.n + 1, pa)
                            nc.scalar.activation(sq[:, :], hc[:, :], ACT.Square, accum_out=n2[:, :])\
                                .then_inc(d["sq"], 1)
                        if at.alive(T):
                            ph.take_rows(act, at)
                        if b.alive(T):
                            hold(act, d["unc"], b.n + 1, pa)
                            nc.scalar.activation(th[:, :], unc[:, :], ACT.Tanh).then_inc(d["tanh"], 1)
                    pipeline(act, T, 1, tile)

        with EdgePass(D, D, [(X3, 0)], T7, 4) as ph:
            ph.step("stats", "h", "tp", "at", "m6", "z", "tpz", "zt", "m7")
            d = ph.done
            h = ph.sb("h", [P, 2, D])
            rowt = ph.sb("rowt", [P, KB, P])
            z = ph.sb("z", [P, D])
            zt = ph.sb("zt", [P, KB, P])
            st, mean, dm = ph.sb("st", [P, 6]), ph.sb("mean", [P, 1]), ph.sb("dm", [P, 1])
            var, ra = ph.sb("var", [P, 1]), ph.sb("ra", [P, 1])
            rt, nm = ph.sb("rt", [P, 2]), ph.sb("nm", [P, 2])
            tp = ph.ps("tp", [P, KB, P])
            tpz = ph.ps("tpz", [P, KB, P])
            m6 = ph.ps("m6", [P, D])
            m7 = ph.ps("m7", [P, D])
            with nc.Block() as block:
                @block.gpsimd
                def _(pool):
                    ph.start_pool(pool)
                    bound = pool.to_reg(N - 1)

                    def tile(at):
                        if at.alive(T):
                            hold(pool, d["h"], at.n - 3, ph.passed["pool"])
                            ph.gather_free(pool, at, bound)
                        if at.back(ph.lag).alive(T):
                            ph.scatter_rows(pool, at.back(ph.lag), bound)
                    pipeline(pool, T, ph.lag, tile)
                    ph.end_pool(pool)

                @block.vector
                def _(dve):
                    link = Chain(dve, d["ch"])
                    pv = ph.passed["dve"]
                    V = nc.vector

                    def tile(at):
                        link.restart()
                        if at.alive(T):
                            sl = at.slot(2)
                            hold(dve, ph.got_in[0][at.slot(4)], 16 * (at.use(4) + 1), pv)
                            hold(dve, d["h"], at.n - 1, pv)
                            link(V.bn_stats(st[:, :], ph.got[0][:, at.slot(4), :]))
                            layernorm_stats(link, st, mean[:, :], dm[:, :], var[:, :])
                            rsqrt(nc, link, rt[:, sl:sl + 1], var[:, :], ra[:, :])
                            V.scalar_tensor_tensor(nm[:, sl:sl + 1], mean[:, :], -0.5, rt[:, sl:sl + 1],
                                                   ALU.mult, ALU.mult).then_inc(d["stats"], 1)
                        b = at.back(1)
                        if b.alive(T):
                            hold(dve, d["h"], b.n + 1, pv)
                            hold(dve, d["acc"], b.n - 1, pv)
                            V.tensor_scalar(ph.msg[:, b.slot(2), :], h[:, b.slot(2), :], norm[:, bass.ds(b.n, 1)],
                                            None, ALU.mult)
                            ph.select(dve, b)
                        c = at.back(2)
                        if c.alive(T):
                            hold(dve, d["m6"], c.n + 1, pv)
                            hold(dve, d["tpz"], c.n, pv)
                            V.tensor_tensor(z[:, :], m6[:, :], rb6[:, :], ALU.add).then_inc(d["z"], 1)
                    pipeline(dve, T, 2, tile)

                @block.tensor
                def _(pe):
                    pp = ph.passed["pe"]

                    def tile(at):
                        b, c = at.back(1), at.back(2)
                        if b.alive(T):
                            ph.accumulate(pe, b)
                        if c.alive(T):
                            hold(pe, d["rows"], c.n + 1, pp)
                            hold(pe, d["at"], c.n, pp)
                            turn(nc, ph.rows[:, c.slot(2), :], tp).then_inc(d["tp"], 1)
                            hold(pe, d["at"], c.n + 1, pp)
                            hold(pe, d["z"], c.n, pp)
                            product(m6[:, :], rowt, w6).then_inc(d["m6"], 1)
                            hold(pe, d["z"], c.n + 1, pp)
                            hold(pe, d["zt"], c.n, pp)
                            turn(nc, z[:, :], tpz).then_inc(d["tpz"], 1)
                            hold(pe, d["zt"], c.n + 1, pp)
                            hold(pe, d["put"], c.n, pp)
                            product(m7[:, :], zt, w7).then_inc(d["m7"], 1)
                    pipeline(pe, T, 2, tile)

                @block.scalar
                def _(act):
                    pa = ph.passed["act"]
                    ph.start_act(act)

                    def tile(at):
                        b, c = at.back(1), at.back(2)
                        if at.alive(T):
                            sl = at.slot(2)
                            hold(act, d["stats"], at.n + 1, pa)
                            hold(act, d["msg"], at.n - 1, pa)
                            nc.scalar.activation(h[:, sl, :], ph.got[0][:, at.slot(4), :], ACT.Relu,
                                                 bias=nm[:, sl:sl + 1], scale=rt[:, sl:sl + 1]).then_inc(d["h"], 1)
                        if b.alive(T):
                            hold(act, d["tp"], b.n - 1, pa)
                            ph.take_rows_free(act, b)
                        if c.alive(T):
                            hold(act, d["tp"], c.n + 1, pa)
                            hold(act, d["m6"], c.n, pa)
                            nc.scalar.activation(rowt[:, :, :], tp[:, :, :], ACT.Copy).then_inc(d["at"], 1)
                            hold(act, d["tpz"], c.n + 1, pa)
                            hold(act, d["m7"], c.n, pa)
                            nc.scalar.activation(zt[:, :, :], tpz[:, :, :], ACT.Relu).then_inc(d["zt"], 1)
                            hold(act, d["m7"], c.n + 1, pa)
                            ph.free_put(act, c, pa)
                            nc.scalar.activation(ph.put[:, c.slot(2), :], m7[:, :], ACT.Copy).then_inc(d["put"], 1)
                    pipeline(act, T, 2, tile)

        with EdgePass(D, D, [(T7, 0)], out, 3) as ph:
            ph.step("y", "tp", "yt", "mm", "xb")
            d = ph.done
            xe = ph.sb("xe", [P, 4, D])
            y = ph.sb("y", [P, D])
            yt = ph.sb("yt", [P, KB, P])
            xb = ph.sb("xb", [P, D])
            tp = ph.ps("tp", [P, KB, P])
            mm = ph.ps("mm", [P, D])
            e_in = ph.slots("e_in", 4)
            with nc.Block() as block:
                @block.gpsimd
                def _(pool):
                    ph.start_pool(pool)
                    bound = pool.to_reg(N - 1)

                    def tile(at):
                        if at.alive(T):
                            hold(pool, d["msg"], at.n - 3, ph.passed["pool"])
                            ph.gather_free(pool, at, bound)
                        if at.back(ph.lag).alive(T):
                            ph.scatter_rows(pool, at.back(ph.lag), bound)
                    pipeline(pool, T, ph.lag, tile)
                    ph.end_pool(pool)

                @block.sync
                def _(sp):
                    def tile(at):
                        hold(sp, d["put"], at.n - 3, ph.passed["sp"])
                        sp.dma_start(xe[:, at.slot(4), :], edge_rows(XE3, at)).then_inc(e_in[at.slot(4)], 16)
                    pipeline(sp, T, 0, tile)

                @block.vector
                def _(dve):
                    pv = ph.passed["dve"]
                    V = nc.vector

                    def tile(at):
                        b, c = at.back(1), at.back(2)
                        if b.alive(T):
                            hold(dve, d["rows"], b.n + 1, pv)
                            hold(dve, d["tp"], b.n, pv)
                            V.tensor_tensor(y[:, :], ph.rows[:, b.slot(2), :], rb7[:, :], ALU.add)\
                                .then_inc(d["y"], 1)
                        if at.alive(T):
                            hold(dve, ph.got_in[0][at.slot(4)], 16 * (at.use(4) + 1), pv)
                            hold(dve, d["acc"], at.n - 1, pv)
                            V.tensor_scalar(ph.msg[:, at.slot(2), :], ph.got[0][:, at.slot(4), :],
                                            norm[:, bass.ds(at.n, 1)], None, ALU.mult)
                            ph.select(dve, at)
                        if c.alive(T):
                            hold(dve, e_in[c.slot(4)], 16 * (c.use(4) + 1), pv)
                            hold(dve, d["put"], c.n, pv)
                            V.tensor_tensor(xb[:, :], xe[:, c.slot(4), :], rbp[:, :], ALU.add).then_inc(d["xb"], 1)
                            hold(dve, d["xb"], c.n + 1, pv)
                            hold(dve, d["mm"], c.n + 1, pv)
                            ph.free_put(dve, c, pv)
                            V.tensor_tensor(ph.put[:, c.slot(2), :], mm[:, :], xb[:, :], ALU.add)\
                                .then_inc(d["put"], 1)
                    pipeline(dve, T, 2, tile)

                @block.tensor
                def _(pe):
                    pp = ph.passed["pe"]

                    def tile(at):
                        if at.alive(T):
                            ph.accumulate(pe, at)
                        b = at.back(1)
                        if b.alive(T):
                            hold(pe, d["y"], b.n + 1, pp)
                            hold(pe, d["yt"], b.n, pp)
                            turn(nc, y[:, :], tp).then_inc(d["tp"], 1)
                            hold(pe, d["yt"], b.n + 1, pp)
                            hold(pe, d["put"], b.n, pp)
                            product(mm[:, :], yt, wp).then_inc(d["mm"], 1)
                    pipeline(pe, T, 1, tile)

                @block.scalar
                def _(act):
                    pa = ph.passed["act"]
                    ph.start_act(act)

                    def tile(at):
                        if at.alive(T):
                            hold(act, d["y"], at.n - 1, pa)
                            ph.take_rows_free(act, at)
                        b = at.back(1)
                        if b.alive(T):
                            hold(act, d["tp"], b.n + 1, pa)
                            hold(act, d["mm"], b.n, pa)
                            nc.scalar.activation(yt[:, :, :], tp[:, :, :], ACT.Relu).then_inc(d["yt"], 1)
                    pipeline(act, T, 1, tile)


NAMES = ['x', 'src', 'dst', 'edge_weight', 'L0_gnn_W1', 'L0_gnn_a_src1', 'L0_gnn_a_dst1', 'L0_gnn_b1', 'L0_gnn_W2',
         'L0_gnn_a_src2', 'L0_gnn_a_dst2', 'L0_gnn_b2', 'L1_gnn_Wq', 'L1_gnn_Wk', 'L1_gnn_Wv', 'L2_gnn_W',
         'L2_gnn_b', 'L2_gnn_mag_w', 'L2_gnn_mag_b', 'L2_gnn_attn_w', 'L3_gnn_W6', 'L3_gnn_b6', 'L3_gnn_W7',
         'L3_gnn_b7', 'L3_gnn_Wp', 'L3_gnn_bp']


def kernel(**inputs):
    import numpy as np
    import concourse.bacc as bacc
    from concourse.bass_utils import run_bass_kernel_spmd

    nc = bacc.Bacc("TRN2", target_bir_lowering=False, num_devices=1)
    arrays, args = {}, []
    for name in NAMES:
        a = np.ascontiguousarray(inputs[name])
        arrays[f"in_{name}_dram"] = a
        args.append(nc.dram_tensor(f"in_{name}_dram", a.shape, mybir.dt.from_np(a.dtype), kind="ExternalInput").ap())
    shape = tuple(inputs["x"].shape)
    args.append(nc.dram_tensor("out_0_dram", shape, F32, kind="ExternalOutput").ap())
    gnn_program(nc, *args)
    r = run_bass_kernel_spmd(nc, [arrays], core_ids=[0])
    return r.results[0]["out_0_dram"]
```

```python
import concourse.bass as bass
from concourse import mybir
from contextlib import ExitStack

F32 = mybir.dt.float32
I32 = mybir.dt.int32
ALU = mybir.AluOpType
ACT = mybir.ActivationFunctionType
AX = mybir.AxisListType

P = 128
D = 256
KB = D // P
UNROLL = 2
G = 4
CH = 7
F1W = 272
F2W = 264
BIG = 1e30
RSQRT_SEED = 1597463007.0


def hold(eng, sem, value, passed):
    base = 0
    if type(sem) is Running:
        sem, base = sem.sem, sem.base
    if type(value) is int:
        if value > 0:
            eng.wait_ge(sem, base + value)
    else:
        eng.wait_ge(sem, value + base)
        eng.sem_inc(passed, 1)


class Running:

    def __init__(self, sem):
        self.sem, self.base = sem, 0


class At:

    def __init__(self, n, turn, s):
        self.n, self.turn, self.s = n, turn, s

    def back(self, lag):
        return At(self.n - lag, self.turn + (self.s - lag) // UNROLL, (self.s - lag) % UNROLL)

    @property
    def slot(self):
        return self.s

    @property
    def use(self):
        return self.turn

    def alive(self, count):
        return type(self.n) is not int or 0 <= self.n < count


def pipeline(eng, count, depth, body):
    lo = -(-(depth + 2) // UNROLL) * UNROLL
    turns = (count - 1 - lo) // UNROLL
    if turns < 1:
        lo, turns = 0, 0
    for n in range(lo):
        body(At(n, n // UNROLL, n % UNROLL))
    if turns:
        with eng.Fori(0, turns) as k:
            for s in range(UNROLL):
                body(At(k * UNROLL + (lo + s), k + lo // UNROLL, s))
    for n in range(lo + turns * UNROLL, count + depth):
        body(At(n, n // UNROLL, n % UNROLL))


class Chain:

    def __init__(self, eng, sem):
        self.eng, self.sem, self.n = eng, sem, 0

    def restart(self):
        self.eng.drain()
        self.eng.sem_clear(self.sem)
        self.n = 0

    def go(self, ins):
        self.n += 1
        ins.then_inc(self.sem, 1)
        return self.n

    def need(self, n):
        self.eng.wait_ge(self.sem, n)

    def __call__(self, ins):
        self.need(self.go(ins))


def take(steps, count=None):
    while count is None or count > 0:
        if next(steps, "end") == "end":
            return
        if count is not None:
            count -= 1


def rsqrt(nc, link, y, v, a):
    V = nc.vector
    n = link.go(V.tensor_scalar(a.bitcast(I32), v.bitcast(I32), 1, None, ALU.logical_shift_right))
    yield
    link.need(n)
    n = link.go(V.tensor_scalar(y.bitcast(I32), a.bitcast(I32), -1.0, RSQRT_SEED, ALU.mult, ALU.add))
    yield
    for _ in range(3):
        link.need(n)
        n = link.go(V.tensor_tensor(a, y, y, ALU.mult))
        yield
        link.need(n)
        n = link.go(V.scalar_tensor_tensor(a, a, -0.5, v, ALU.mult, ALU.mult))
        yield
        link.need(n)
        n = link.go(V.scalar_tensor_tensor(y, a, 1.5, y, ALU.add, ALU.mult))
        yield
    link.need(n)


def min_int(value, most):
    return min(value, most) if type(value) is int else value


def magnitude(nc, link, fac, e, r, un, unc, n2):
    V = nc.vector
    n = link.go(V.tensor_scalar(fac, e, 1.0, None, ALU.add))
    yield
    if un is not None:
        V.tensor_tensor(un, n2, r, ALU.mult)
    link.need(n)
    n = link.go(V.reciprocal(fac, fac))
    yield
    link.need(n)
    n = link.go(V.scalar_tensor_tensor(fac, fac, 1.5, r, ALU.mult, ALU.mult))
    yield
    link.need(n)
    if un is not None:
        n = link.go(V.tensor_tensor(un, un, fac, ALU.mult))
        yield
        link.need(n)
        n = link.go(V.tensor_scalar(unc, un, 1e-15, None, ALU.max))
        yield
        link.need(n)


def expmap_scale(nc, link, scale, th, un, unc, a, b):
    V = nc.vector
    for op in (lambda: V.reciprocal(a, unc),
               lambda: V.tensor_tensor(scale, th, a, ALU.mult),
               lambda: V.tensor_tensor(a, scale, un, ALU.mult),
               lambda: V.tensor_scalar(b, a, 1e-8, None, ALU.add),
               lambda: V.reciprocal(b, b),
               lambda: V.tensor_scalar(b, b, 0.95, -1.0, ALU.mult, ALU.add),
               lambda: V.scalar_tensor_tensor(b, a, 0.95, b, ALU.is_gt, ALU.mult),
               lambda: V.scalar_tensor_tensor(scale, b, 1.0, scale, ALU.add, ALU.mult)):
        n = link.go(op())
        yield
        link.need(n)


def layernorm_stats(nc, link, st, mean, dm, var):
    V = nc.vector
    V.tensor_tensor(dm, st[:, :, 1], st[:, :, 4], ALU.subtract)
    V.tensor_tensor(mean, st[:, :, 1], st[:, :, 4], ALU.add)
    n = link.go(V.tensor_tensor(var, st[:, :, 2], st[:, :, 5], ALU.add))
    yield
    for op in (lambda: V.tensor_tensor(dm, dm, dm, ALU.mult),
               lambda: V.scalar_tensor_tensor(var, dm, D / 4.0, var, ALU.mult, ALU.add),
               lambda: V.tensor_scalar(var, var, 1.0 / D, 1e-5, ALU.mult, ALU.add)):
        link.need(n)
        n = link.go(op())
        yield
    link.need(n)


def gnn_program(nc, x, src, dst, edge_weight, W1, a_src1, a_dst1, b1, W2, a_src2, a_dst2, b2,
                Wq, Wk, Wv, WL, bL, mag_w, mag_b, attn_w, W6, b6, W7, b7, Wp, bp, out):
    N, E = x.shape[0], src.shape[0]
    NC = -(-E // (P * CH))
    T = NC * CH
    EP = T * P
    HQ = 4
    CQ = NC * HQ
    CE = CH * P
    OOB = N + 4096
    NG = T // G
    U = -(-N // (G * P))
    UPART = (N - (U - 1) * G * P) // G
    NCOL = G * U
    assert CQ <= P and NCOL <= 512 and N % G == 0 and T % G == 0

    def dram(name, shape):
        return nc.dram_tensor(name, shape, F32, kind="Internal").ap()

    F1 = dram("F1", (N, F1W))
    F2 = dram("F2", (N, F2W))
    H2 = dram("H2", (N, D))
    HL = dram("HL", (N, F2W))
    X3 = dram("X3", (N, D))
    T7 = dram("T7", (N, D))
    FE2 = dram("FE2", (EP, F2W))
    XE1 = dram("XE1", (EP, D))
    XE2 = dram("XE2", (EP, D))
    HE2 = dram("HE2", (EP, D))
    XE3 = dram("XE3", (EP, D))
    DSTF = dram("DSTF", (T, P))
    CONT = dram("CONT", (T, P))

    ctx = ExitStack()
    with ctx:
        def sb(name, shape, dt=F32, on=ctx):
            return on.enter_context(nc.sbuf_tensor(name, shape, dt))

        ident = sb("ident", [P, P])
        last_row = sb("last_row", [P, P])
        dst_col = sb("dst_col", [P, T])
        ew = sb("ew", [P, T])
        norm = sb("norm", [P, T])
        index = sb("index", [P, T, 7], I32)
        w_edge = sb("w_edge", [P, T, HQ])
        w_self = sb("w_self", [P, T, HQ])
        w1 = sb("w1", [P, KB, F2W])
        w2 = sb("w2", [P, KB, F2W])
        wl = sb("wl", [P, KB, F2W])
        wq = sb("wq", [P, KB, D])
        wkv = sb("wkv", [P, KB, 2 * D])
        w6 = sb("w6", [P, KB, D])
        w7 = sb("w7", [P, KB, D])
        wp = sb("wp", [P, KB, D])
        rb1 = sb("rb1", [P, D])
        rb2 = sb("rb2", [P, D])
        rbl = sb("rbl", [P, F2W])
        rb6 = sb("rb6", [P, D])
        rb7 = sb("rb7", [P, D])
        rbp = sb("rbp", [P, D])
        gcn_const = sb("gcn_const", [P, D])
        t7_const = sb("t7_const", [P, 4, D])

        def running(name):
            return [Running(ctx.enter_context(nc.semaphore(f"{name}{i}"))) for i in range(2)]

        gathered_in = [running("gathered_a"), running("gathered_b")]
        scattered_out = running("scattered")

        class Phase:

            count = 0

            def __enter__(self):
                Phase.count += 1
                self.tag = f"_{Phase.count}"
                self.st = ExitStack()
                self.st.__enter__()
                self.sems = []
                self.passed = {e: self.sem("passed_" + e) for e in ("sp", "act", "pe", "dve", "pool")}
                return self

            def sem(self, name):
                s = self.st.enter_context(nc.semaphore(name + self.tag))
                self.sems.append(s)
                return s

            def slots(self, name, n):
                return [self.sem(f"{name}{k}") for k in range(n)]

            def sb(self, name, shape, dt=F32):
                return sb(name + self.tag, shape, dt, self.st)

            def ps(self, name, shape, dt=F32):
                return self.st.enter_context(nc.psum_tensor(name + self.tag, shape, dt))

            def __exit__(self, *err):
                if err[0] is None:
                    with nc.Block() as block:
                        @block.gpsimd
                        def _(pool):
                            for s in self.sems:
                                pool.sem_clear(s)
                return self.st.__exit__(*err)

        with Phase() as ph:
            NB = -(-T // P)
            raw = [ph.sb(f"raw{k}", [P, NB, P], I32) for k in range(3)]
            rows = [ph.sb(f"rows{k}", [P, NB, P]) for k in range(4)]
            src_col = ph.sb("src_col", [P, T])
            next_col = ph.sb("next_col", [P, T])
            tmp = ph.sb("tmp", [P, T])
            av = [ph.sb(f"av{k}", [P, D]) for k in range(6)]
            prod = ph.sb("prod", [P, KB, D])
            wraw = ph.sb("wraw", [P, KB, D])
            relu_b = ph.sb("relu_b", [P, D])
            relu_bt = ph.sb("relu_bt", [P, KB, P])
            ps_t = ph.ps("ps_t", [P, 512])
            ps_w = ph.ps("ps_w", [P, 4, P])
            ps_c = ph.ps("ps_c", [P, 512])
            cont = ph.sb("cont", [P, NB * P])
            s_pad, s_in, s_ids, s_id = ph.sem("s_pad"), ph.sem("s_in"), ph.sem("s_ids"), ph.sem("s_id")
            s_dr, s_drs, s_cont = ph.sem("s_dr"), ph.sem("s_drs"), ph.sem("s_cont")
            s_v, s_pe, s_ch = ph.sem("s_v"), ph.sem("s_pe"), ph.sem("s_ch")
            with nc.Block() as block:
                def load_rows(eng, to, flat, n):
                    full, count = n // P, 0
                    for b in range(NB):
                        r = min(full - b * P, P)
                        if r > 0:
                            eng.dma_start(to[0:r, b, :], flat[b * P * P:b * P * P + r * P]
                                          .rearrange("(t p) -> t p", p=P)).then_inc(s_ids, 16)
                            count += 1
                    if n % P:
                        q = full % P
                        eng.dma_start(to[q:q + 1, full // P, 0:n % P],
                                      flat[full * P:n].rearrange("(a n) -> a n", a=1)).then_inc(s_ids, 16)
                        count += 1
                    return count

                counted = {}

                @block.sync
                def _(sp):
                    n = 0
                    for w, t in ((W1, w1), (W2, w2)):
                        sp.dma_start(t[:, :, 0:D], w.rearrange("(k p) n -> p k n", p=P)).then_inc(s_in, 16)
                        n += 1
                    for w, t in ((Wq, wq), (W6, w6), (W7, w7), (Wp, wp), (WL, wraw)):
                        sp.dma_start(t[:, :, :], w.rearrange("(k p) n -> p k n", p=P)).then_inc(s_in, 16)
                        n += 1
                    sp.dma_start(wkv[:, :, 0:D], Wk.rearrange("(k p) n -> p k n", p=P)).then_inc(s_in, 16)
                    sp.dma_start(wkv[:, :, D:2 * D], Wv.rearrange("(k p) n -> p k n", p=P)).then_inc(s_in, 16)
                    with nc.allow_non_contiguous_dma(reason="one column of 256 elements"):
                        sp.dma_start(wl[:, :, 258:259], mag_w.rearrange("a (k p) -> p k a", p=P)).then_inc(s_in, 16)
                    n += 3
                    for v, t in ((b1, rb1), (b2, rb2), (b6, rb6), (b7, rb7), (bp, rbp)):
                        sp.dma_start(t[:, :], v.partition_broadcast(P)).then_inc(s_in, 16)
                        n += 1
                    sp.dma_start(rbl[:, 0:D], bL.partition_broadcast(P)).then_inc(s_in, 16)
                    sp.dma_start(rbl[:, 258:259], mag_b.partition_broadcast(P)).then_inc(s_in, 16)
                    for v, t in zip((a_src1, a_dst1, a_src2, a_dst2), av):
                        sp.dma_start(t[:, :], v.rearrange("h c -> (h c)").partition_broadcast(P)).then_inc(s_in, 16)
                    sp.dma_start(av[4][:, :], attn_w[0, 0:D].partition_broadcast(P)).then_inc(s_in, 16)
                    sp.dma_start(av[5][:, :], attn_w[0, D:2 * D].partition_broadcast(P)).then_inc(s_in, 16)
                    counted["in"] = 16 * (n + 8)
                    sp.wait_ge(s_pad, 8)
                    c = load_rows(sp, raw[0], src, E)
                    c += load_rows(sp, raw[1], dst, E)
                    c += load_rows(sp, raw[2], dst[1:E], E - 1)
                    c += load_rows(sp, rows[3], edge_weight, E)
                    counted["ids"] = 16 * c
                    sp.wait_ge(s_drs, 1)
                    for b in range(NB):
                        r = min(T - b * P, P)
                        sp.dma_start(DSTF[b * P:b * P + r, :], rows[1][0:r, b, :]).then_inc(s_dr, 16)
                    sp.wait_ge(s_cont, 1)
                    for b in range(NB):
                        r = min(T - b * P, P)
                        sp.dma_start(CONT[b * P:b * P + r, :], rows[0][0:r, b, :]).then_inc(s_dr, 16)
                    sp.wait_ge(s_dr, 32 * NB)

                @block.gpsimd
                def _(pool):
                    nc.gpsimd.memset(raw[0][:, :, :], 0).then_inc(s_pad, 1)
                    nc.gpsimd.memset(raw[1][:, :, :], OOB).then_inc(s_pad, 1)
                    nc.gpsimd.memset(raw[2][:, :, :], -1).then_inc(s_pad, 1)
                    nc.gpsimd.memset(rows[3][:, :, :], 0.0).then_inc(s_pad, 1)
                    nc.gpsimd.memset(w1[:, :, D:F2W], 0.0).then_inc(s_pad, 1)
                    nc.gpsimd.memset(w2[:, :, D:F2W], 0.0).then_inc(s_pad, 1)
                    nc.gpsimd.memset(wl[:, :, 259:F2W], 0.0).then_inc(s_pad, 1)
                    nc.gpsimd.memset(rbl[:, 259:F2W], 0.0).then_inc(s_pad, 1)
                    nc.gpsimd.memset(ident[:, :], 0.0).then_inc(s_id, 1)
                    nc.gpsimd.memset(last_row[:, :], 0.0).then_inc(s_id, 1)
                    pool.wait_ge(s_id, 2)
                    nc.gpsimd.affine_select(out=ident[:, :], in_=ident[:, :], compare_op=ALU.not_equal, fill=1.0,
                                            base=0, pattern=[[-1, P]], channel_multiplier=1).then_inc(s_id, 1)
                    nc.gpsimd.affine_select(out=last_row[:, :], in_=last_row[:, :], compare_op=ALU.not_equal,
                                            fill=1.0, base=-(P - 1), pattern=[[0, P]], channel_multiplier=1)\
                        .then_inc(s_id, 1)
                    pool.wait_ge(s_id, 4)

                @block.tensor
                def _(pe):
                    pe.wait_ge(s_id, 4)
                    for k in (0, 1, 2, 3):
                        pe.wait_ge(s_v, k + 1)
                        for b in range(NB):
                            last = nc.tensor.transpose(ps_t[:, b * P:(b + 1) * P], rows[k][:, b, :], ident[:, :])
                        last.then_inc(s_pe, 1)
                    pe.wait_ge(s_v, 5)
                    pe.wait_ge(s_in, counted["in"])
                    for i in range(KB):
                        for o in range(KB):
                            last = nc.tensor.transpose(ps_w[:, i * KB + o, :], wraw[:, o, i * P:(i + 1) * P],
                                                       ident[:, :])
                    last.then_inc(s_pe, 1)
                    for k, w in ((0, w7), (1, wp)):
                        pe.wait_ge(s_v, 6 + 2 * k)
                        for j in range(KB):
                            last = nc.tensor.transpose(ps_t[:, j * P:(j + 1) * P], relu_b[:, j * P:(j + 1) * P],
                                                       ident[:, :])
                        last.then_inc(s_pe, 1)
                        pe.wait_ge(s_v, 7 + 2 * k)
                        for j in range(KB):
                            last = nc.tensor.matmul(ps_t[:, 256:512], relu_bt[:, j, :], w[:, j, :],
                                                    start=(j == 0), stop=(j == KB - 1))
                        last.then_inc(s_pe, 1)
                    nc.tensor.matmul(ps_c[:, 0:T], last_row[:, :], dst_col[:, :], start=True, stop=True)\
                        .then_inc(s_pe, 1)
                    pe.wait_ge(s_v, 10)
                    for b in range(NB):
                        last = nc.tensor.transpose(ps_t[:, b * P:(b + 1) * P], cont[:, b * P:(b + 1) * P],
                                                   ident[:, :])
                    last.then_inc(s_pe, 1)

                @block.vector
                def _(dve):
                    link = Chain(dve, s_ch)
                    V = nc.vector
                    dve.wait_ge(s_ids, counted["ids"])
                    for k in range(3):
                        link(V.tensor_copy(rows[k][:, :, :], raw[k][:, :, :]))
                    dve.sem_inc(s_drs, 1)
                    dve.sem_inc(s_v, 1)
                    cols = (src_col, dst_col, next_col, ew)
                    for k in range(4):
                        dve.wait_ge(s_pe, k + 1)
                        link(V.tensor_copy(cols[k][:, :], ps_t[:, 0:T]))
                        dve.sem_inc(s_v, 1)
                    dve.wait_ge(s_in, counted["in"])
                    dve.wait_ge(s_pe, 5)
                    dve.wait_ge(s_pad, 8)
                    dve.wait_ge(s_id, 4)
                    for i in range(KB):
                        link(V.tensor_copy(wl[:, i, 0:D], ps_w[:, i * KB:(i + 1) * KB, :]
                                           .rearrange("p a b -> p (a b)")))
                    link(V.tensor_scalar(relu_b[:, :], rb6[:, :], 0.0, None, ALU.max))
                    dve.sem_inc(s_v, 1)
                    dve.wait_ge(s_pe, 6)
                    link(V.tensor_copy(relu_bt[:, :, :].rearrange("p a b -> p (a b)"), ps_t[:, 0:D]))
                    dve.sem_inc(s_v, 1)
                    dve.wait_ge(s_pe, 7)
                    for r in range(4):
                        link(V.tensor_copy(t7_const[:, r, :], ps_t[:, 256:512]))
                    link(V.tensor_scalar(relu_b[:, :], rb7[:, :], 0.0, None, ALU.max))
                    dve.sem_inc(s_v, 1)
                    dve.wait_ge(s_pe, 8)
                    link(V.tensor_copy(relu_bt[:, :, :].rearrange("p a b -> p (a b)"), ps_t[:, 0:D]))
                    dve.sem_inc(s_v, 1)
                    dve.wait_ge(s_pe, 9)
                    link(V.tensor_tensor(gcn_const[:, :], ps_t[:, 256:512], rbp[:, :], ALU.add))
                    for w, a, b in ((w1, av[0], av[1]), (w2, av[2], av[3])):
                        for off, vec in ((D, a), (D + 4, b)):
                            for k in range(KB):
                                link(V.tensor_tensor(prod[:, k, :], w[:, k, 0:D], vec[:, :], ALU.mult))
                                link(V.tensor_reduce(w[:, k, off:off + 4],
                                                     prod[:, k, :].rearrange("p (h c) -> p h c", h=4),
                                                     axis=AX.X, op=ALU.add))
                    for off, vec in ((D, av[4]), (D + 1, av[5])):
                        for k in range(KB):
                            link(V.tensor_tensor(prod[:, k, :], wl[:, k, 0:D], vec[:, :], ALU.mult))
                            link(V.tensor_reduce(wl[:, k, off:off + 1], prod[:, k, :], axis=AX.X, op=ALU.add))
                        link(V.tensor_tensor(prod[:, 0, :], rbl[:, 0:D], vec[:, :], ALU.mult))
                        link(V.tensor_reduce(rbl[:, off:off + 1], prod[:, 0, :], axis=AX.X, op=ALU.add))
                    link(V.tensor_copy(index[:, :, 0], src_col[:, :]))
                    link(V.tensor_scalar(index[:, :, 3], src_col[:, :], 17.0, 16.0, ALU.mult, ALU.add))
                    link(V.tensor_scalar(index[:, :, 5], src_col[:, :], 33.0, 32.0, ALU.mult, ALU.add))
                    link(V.tensor_scalar(tmp[:, :], dst_col[:, :], float(N - 1), None, ALU.min))
                    link(V.tensor_copy(index[:, :, 1], tmp[:, :]))
                    link(V.tensor_scalar(index[:, :, 4], tmp[:, :], 17.0, 16.0, ALU.mult, ALU.add))
                    link(V.tensor_scalar(index[:, :, 6], tmp[:, :], 33.0, 32.0, ALU.mult, ALU.add))
                    link(V.tensor_tensor(tmp[:, :], dst_col[:, :], next_col[:, :], ALU.is_equal))
                    link(V.scalar_tensor_tensor(index[:, :, 2], tmp[:, :], float(OOB), dst_col[:, :],
                                                ALU.mult, ALU.add))
                    link(V.memset(cont[:, :], 0.0))
                    dve.wait_ge(s_pe, 10)
                    link(V.tensor_copy(tmp[:, :], ps_c[:, 0:T]))
                    link(V.tensor_tensor(cont[:, 1:T], dst_col[:, 1:T], tmp[:, 0:T - 1], ALU.is_equal))
                    dve.sem_inc(s_v, 1)
                    dve.wait_ge(s_pe, 11)
                    link(V.tensor_copy(rows[0][:, :, :].rearrange("p b q -> p (b q)"), ps_t[:, 0:NB * P]))
                    dve.sem_inc(s_cont, 1)

        deg_stack = ExitStack()
        deg = sb("deg", [P, NCOL, 2], on=deg_stack)
        with Phase() as ph:
            iota_i = ph.sb("iota_i", [P, NCOL if NCOL > P else P], I32)
            iota_f = ph.sb("iota_f", [P, NCOL if NCOL > P else P])
            ids = ph.sb("ids", [P, T], I32)
            bits = ph.sb("bits", [P, T], I32)
            high = ph.sb("high", [P, T], I32)
            lo_f = [ph.sb(f"lo_f{k}", [P, T]) for k in range(2)]
            hi_f = [ph.sb(f"hi_f{k}", [P, T]) for k in range(2)]
            hot_lo = ph.sb("hot_lo", [P, 2, G, 2, P])
            hot_hi = ph.sb("hot_hi", [P, 2, G, 2, NCOL])
            ps_deg = [ph.ps(f"ps_deg{k}", [P, NCOL]) for k in range(2)]
            s_iota, s_ch = ph.sem("s_iota"), ph.sem("s_ch")
            hots_ready, hots_used = ph.sem("hots_ready"), ph.sem("hots_used")
            t7_out = ph.sem("t7_out")
            with nc.Block() as block:
                @block.sync
                def _(sp):
                    full = N // (G * P)
                    rest = N - full * G * P
                    with sp.Fori(0, full) as k:
                        sp.dma_start(T7[bass.ds(k * (G * P), G * P), :].rearrange("(p r) w -> p (r w)", r=G),
                                     t7_const[:, :, :].rearrange("p r w -> p (r w)")).then_inc(t7_out, 16)
                    if rest:
                        sp.dma_start(T7[full * G * P:N, :].rearrange("(p r) w -> p (r w)", r=G),
                                     t7_const[0:rest // G, :, :].rearrange("p r w -> p (r w)")).then_inc(t7_out, 16)
                    sp.wait_ge(t7_out, 16 * (full + (1 if rest else 0)))

                @block.gpsimd
                def _(pool):
                    nc.gpsimd.iota(iota_i[:, :], [[1, iota_i.shape[1]]], base=0, channel_multiplier=0)\
                        .then_inc(s_iota, 1)

                @block.vector
                def _(dve):
                    link = Chain(dve, s_ch)
                    V = nc.vector
                    dve.wait_ge(s_iota, 1)
                    link(V.tensor_copy(iota_f[:, :], iota_i[:, :]))
                    for k, nodes in ((0, 0), (1, 1)):
                        link(V.tensor_scalar(ids[:, :], index[:, :, nodes], 2, 127,
                                             ALU.logical_shift_right, ALU.bitwise_and))
                        link(V.tensor_copy(lo_f[k][:, :], ids[:, :]))
                        link(V.tensor_scalar(ids[:, :], index[:, :, nodes], 9, 2,
                                             ALU.logical_shift_right, ALU.logical_shift_left))
                        link(V.tensor_scalar(bits[:, :], index[:, :, nodes], 3, None, ALU.bitwise_and))
                        link(V.tensor_tensor(high[:, :], ids[:, :], bits[:, :], ALU.bitwise_or))
                        link(V.tensor_copy(hi_f[k][:, :], high[:, :]))

                    def group(at):
                        hold(dve, hots_used, at.n - 1, ph.passed["dve"])
                        for t in range(G):
                            col = bass.ds(at.n * G + t, 1)
                            for k in range(2):
                                V.tensor_scalar(hot_lo[:, at.slot, t, k, :], iota_f[:, 0:P], lo_f[k][:, col],
                                                ew[:, col], ALU.is_equal, ALU.mult)
                                last = V.tensor_scalar(hot_hi[:, at.slot, t, k, :], iota_f[:, 0:NCOL],
                                                       hi_f[k][:, col], None, ALU.is_equal)
                        last.then_inc(hots_ready, 1)
                    pipeline(dve, NG, 0, group)
                    dve.wait_ge(hots_used, NG)
                    for k in range(2):
                        link(V.tensor_copy(deg[:, :, k], ps_deg[k][:, :]))

                @block.tensor
                def _(pe):
                    def group(at):
                        hold(pe, hots_ready, at.n + 1, ph.passed["pe"])
                        for t in range(G):
                            first = type(at.n) is int and at.n + t == 0
                            end = type(at.n) is int and at.n * G + t == T - 1
                            for k in range(2):
                                last = nc.tensor.matmul(ps_deg[k][:, :], hot_lo[:, at.slot, t, k, :],
                                                        hot_hi[:, at.slot, t, k, :], start=first, stop=end)
                        last.then_inc(hots_used, 1)
                    pipeline(pe, NG, 0, group)

        with Phase() as ph:
            xin = ph.sb("xin", [P, 2, G, D])
            xb = ph.sb("xb", [P, 2, G, D])
            x1 = ph.sb("x1", [P, 2, G, D])
            h1 = ph.sb("h1", [P, G, D])
            h2 = ph.sb("h2", [P, 2, G, D])
            f1o = ph.sb("f1o", [P, 2, G, F1W])
            f2o = ph.sb("f2o", [P, 2, G, F2W])
            z = ph.sb("z", [P, G, D])
            zm = ph.sb("zm", [P, G, D])
            g = ph.sb("g", [P, G, D])
            tt = [ph.sb(f"tt{k}", [P, 2, 4, P]) for k in range(3)]
            hr = ph.sb("hr", [P, G, F2W])
            sq = ph.sb("sq", [P, G, D])
            ho = ph.sb("ho", [P, 2, G, F2W])
            x3o = ph.sb("x3o", [P, 2, G, D])
            oo = ph.sb("oo", [P, 2, G, D])
            st = ph.sb("st", [P, 2 * G, 6])
            mean, dm = ph.sb("mean", [P, 2 * G]), ph.sb("dm", [P, 2 * G])
            var, ra = ph.sb("var", [P, 3 * G]), ph.sb("ra", [P, 3 * G])
            rt, nm = ph.sb("rt", [P, 2, 3 * G]), ph.sb("nm", [P, 2, 2 * G])
            n2, em, th = ph.sb("n2", [P, G]), ph.sb("em", [P, G]), ph.sb("th", [P, G])
            fac, un, unc = ph.sb("fac", [P, G]), ph.sb("un", [P, G]), ph.sb("unc", [P, G])
            ga, gb, gc = ph.sb("ga", [P, G]), ph.sb("gb", [P, G]), ph.sb("gc", [P, G])
            warm = ph.sb("warm", [P, 1])
            tp = [ph.ps(f"tp{k}", [P, 4, P]) for k in range(2)]
            mm = [ph.ps(f"mm{k}", [P, 2, 512]) for k in range(3)]
            x_in = ph.slots("x_in", 2)
            f1_out, f2_out, h2_out = ph.slots("f1_out", 2), ph.slots("f2_out", 2), ph.slots("h2_out", 2)
            hl_out, x3_out, o_out = ph.slots("hl_out", 2), ph.slots("x3_out", 2), ph.slots("o_out", 2)
            s = {k: ph.sem(k) for k in (
                "ch", "xb", "deg", "stats", "h1_h", "h2", "zm", "exp", "g", "tp_h", "t_h", "mma_h", "mmb_h", "mmc_h",
                "f1_h", "f2_h", "hr_h", "em", "sq", "x1", "unc", "tanh", "x3", "ho", "oo", "warm", "pad")}

            def rows_of(table, at):
                if type(at.n) is not int:
                    return table[bass.ds(at.n * (G * P), G * P), :].rearrange("(p r) w -> p (r w)", r=G), P
                np_ = UPART if at.n == U - 1 else P
                return (table[at.n * G * P:at.n * G * P + G * np_, :].rearrange("(p r) w -> p (r w)", r=G), np_)

            def flat(t, slot, np_):
                return t[0:np_, slot, :, :].rearrange("p r w -> p (r w)")

            def wide(row, w, r):
                return row[:, 0:w].unsqueeze(1).to_broadcast([P, r, w])

            ORDER = "bac"
            LAG = {"b": 1, "a": 0, "c": 2}
            PAIR = {("b", 0): 0, ("b", 1): 1, ("a", 0): 2, ("a", 1): 0, ("c", 0): 1, ("c", 1): 2}
            READ = {"b": s["f2_h"], "a": s["f1_h"], "c": s["hr_h"]}

            def turns_before(at, stage):
                if type(at.n) is not int:
                    return at.n * 6 + (2 * ORDER.index(stage) - 6)
                stages = [(m, LAG[k]) for m in range(at.n) for k in ORDER]
                stages += [(at.n, LAG[k]) for k in ORDER[:ORDER.index(stage)]]
                return sum(2 for m, lag in stages if 0 <= m - lag < U)

            def bank_free(at, stage, q):
                where = [(o, k, h) for o in range(1, -1, -1) for k in ORDER for h in range(2)]
                for o, k, h in reversed(where[:where.index((0, stage, q))]):
                    n = at.back(o + LAG[k])
                    if PAIR[k, h] == PAIR[stage, q] and n.alive(U):
                        return READ[k], n.n * 2 + (h + 1)
                return READ[stage], 0

            with nc.Block() as block:
                @block.sync
                def _(sp):
                    ps = ph.passed["sp"]

                    def unit(at):
                        if at.alive(U):
                            hold(sp, s["stats"], at.n - 1, ps)
                            hold(sp, s["h1_h"], at.n * 2 - 2, ps)
                            hold(sp, s["xb"], at.n - 1, ps)
                            view, np_ = rows_of(x, at)
                            sp.dma_start(flat(xin, at.slot, np_), view).then_inc(x_in[at.slot], 16)
                        j = at.back(2)
                        if j.alive(U):
                            view, np_ = rows_of(F1, j)
                            hold(sp, s["f1_h"], j.n * 2 + 2, ps)
                            hold(sp, s["deg"], j.n + 1, ps)
                            sp.dma_start(view, flat(f1o, j.slot, np_)).then_inc(f1_out[j.slot], 16)
                        j = at.back(3)
                        if j.alive(U):
                            view, np_ = rows_of(F2, j)
                            hold(sp, s["f2_h"], j.n * 2 + 2, ps)
                            sp.dma_start(view, flat(f2o, j.slot, np_)).then_inc(f2_out[j.slot], 16)
                            view, np_ = rows_of(H2, j)
                            hold(sp, s["h2"], j.n + 1, ps)
                            sp.dma_start(view, flat(h2, j.slot, np_)).then_inc(h2_out[j.slot], 16)
                        j = at.back(4)
                        if j.alive(U):
                            view, np_ = rows_of(HL, j)
                            hold(sp, s["ho"], j.n + 1, ps)
                            sp.dma_start(view, flat(ho, j.slot, np_)).then_inc(hl_out[j.slot], 16)
                            view, np_ = rows_of(X3, j)
                            hold(sp, s["x3"], j.n + 1, ps)
                            sp.dma_start(view, flat(x3o, j.slot, np_)).then_inc(x3_out[j.slot], 16)
                            view, np_ = rows_of(out, j)
                            hold(sp, s["oo"], j.n + 1, ps)
                            sp.dma_start(view, flat(oo, j.slot, np_)).then_inc(o_out[j.slot], 16)
                    pipeline(sp, U, 4, unit)
                    for group in (f1_out, f2_out, h2_out, hl_out, x3_out, o_out):
                        for k in range(2):
                            sp.wait_ge(group[k], 16 * ((U + 1 - k) // 2))

                @block.gpsimd
                def _(pool):
                    pp = ph.passed["pool"]
                    nc.gpsimd.memset(f1o[:, :, :, :], 0.0)
                    nc.gpsimd.memset(warm[:, :], 0.0).then_inc(s["pad"], 1)
                    pool.wait_ge(s["pad"], 1)

                    def unit(at):
                        j = at.back(4)
                        if j.alive(U):
                            hold(pool, s["x3"], j.n + 1, pp)
                            hold(pool, o_out[j.slot], 16 * j.use, pp)
                            nc.gpsimd.tensor_tensor(oo[:, j.slot, :, :], x3o[:, j.slot, :, :],
                                                    wide(gcn_const, D, G), ALU.add).then_inc(s["oo"], 1)
                        if at.alive(U):
                            hold(pool, x_in[at.slot], 16 * (at.use + 1), pp)
                            hold(pool, s["x1"], at.n - 1, pp)
                            nc.gpsimd.tensor_tensor(xb[:, at.slot, :, :], xin[:, at.slot, :, :],
                                                    wide(rb2, D, G), ALU.add).then_inc(s["xb"], 1)
                            hold(pool, f1_out[at.slot], 16 * at.use, pp)
                            nc.gpsimd.tensor_copy(f1o[:, at.slot, :, 264:266], deg[:, bass.ds(at.n * G, G), :])\
                                .then_inc(s["deg"], 1)
                        b = at.back(1)
                        if b.alive(U):
                            hold(pool, s["xb"], b.n + 1, pp)
                            hold(pool, s["h2"], b.n - 1, pp)
                            hold(pool, s["x3"], b.n - 1, pp)
                            for q in range(2):
                                hold(pool, s["f2_h"], b.n * 2 + (q + 1), pp)
                                half = slice(2 * q, 2 * q + 2)
                                last = nc.gpsimd.tensor_tensor(x1[:, b.slot, half, :], xb[:, b.slot, half, :],
                                                               f2o[:, b.slot, half, 0:D], ALU.add)
                            last.then_inc(s["x1"], 1)
                    pipeline(pool, U, 4, unit)

                @block.tensor
                def _(pe):
                    pp = ph.passed["pe"]

                    def turn_half(rows_t, q, turns):
                        bank = tp[q]
                        hold(pe, s["t_h"], turns + (q - 1), pp)
                        for r in range(2):
                            for k in range(KB):
                                last = nc.tensor.transpose(bank[:, 2 * r + k, :],
                                                           rows_t[:, 2 * q + r, k * P:(k + 1) * P], ident[:, :])
                        last.then_inc(s["tp_h"], 1)

                    def multiply_half(at, stage, q, lhs, w, sem):
                        hold(pe, s["t_h"], turns_before(at, stage) + (q + 1), pp)
                        free, count = bank_free(at, stage, q)
                        hold(pe, free, count, pp)
                        for r in range(2):
                            for k in range(KB):
                                last = nc.tensor.matmul(mm[PAIR[stage, q]][:, r, 0:F2W], lhs[:, q, 2 * r + k, :],
                                                        w[:, k, :], start=(k == 0), stop=(k == KB - 1))
                        last.then_inc(sem, 1)

                    def unit(at):
                        a, b, c = at, at.back(1), at.back(2)
                        if b.alive(U):
                            hold(pe, s["g"], b.n + 1, pp)
                            for q in range(2):
                                turn_half(g, q, turns_before(at, "b"))
                            for q in range(2):
                                multiply_half(at, "b", q, tt[1], w2, s["mmb_h"])
                        if a.alive(U):
                            for q in range(2):
                                hold(pe, s["h1_h"], a.n * 2 + (q + 1), pp)
                                turn_half(h1, q, turns_before(at, "a"))
                            for q in range(2):
                                multiply_half(at, "a", q, tt[0], w1, s["mma_h"])
                        if c.alive(U):
                            hold(pe, s["h2"], c.n + 1, pp)
                            for q in range(2):
                                turn_half(h2[:, c.slot, :, :], q, turns_before(at, "c"))
                            for q in range(2):
                                multiply_half(at, "c", q, tt[2], wl, s["mmc_h"])
                    pipeline(pe, U, 2, unit)

                @block.scalar
                def _(act):
                    pa = ph.passed["act"]
                    act.wait_ge(s["pad"], 1)
                    nc.scalar.activation(warm[:, :], warm[:, :], ACT.Exp).then_inc(s["warm"], 1)
                    act.wait_ge(s["warm"], 1)

                    def copy_turned(at, stage, j, k, halves=(0, 1)):
                        hold(act, s[f"mm{stage}_h"], j.n * 2, pa)
                        for q in halves:
                            hold(act, s["tp_h"], turns_before(at, stage) + (q + 1), pa)
                            nc.scalar.activation(tt[k][:, q, :, :], tp[q][:, :, :], ACT.Copy).then_inc(s["t_h"], 1)

                    def copy_f2(b, q):
                        hold(act, s["mmb_h"], b.n * 2 + (q + 1), pa)
                        nc.scalar.activation(f2o[:, b.slot, 2 * q:2 * q + 2, :], mm[PAIR["b", q]][:, :, 0:F2W],
                                             ACT.Copy).then_inc(s["f2_h"], 1)

                    def unit(at):
                        a, b, c, d = at, at.back(1), at.back(2), at.back(3)
                        if b.alive(U):
                            hold(act, s["zm"], b.n + 1, pa)
                            nc.scalar.activation(zm[:, :, :], zm[:, :, :], ACT.Exp).then_inc(s["exp"], 1)
                        if b.alive(U):
                            copy_turned(at, "b", b, 1, (0,))
                        if d.alive(U):
                            hold(act, s["em"], d.n + 1, pa)
                            for r in range(G):
                                nc.scalar.activation(sq[:, r, :], hr[:, r, 0:D], ACT.Square,
                                                     accum_out=n2[:, r:r + 1])
                            nc.scalar.activation(em[:, :], em[:, :], ACT.Exp, scale=-1.0).then_inc(s["sq"], 1)
                            hold(act, s["sq"], d.n + 1, pa)
                        if b.alive(U):
                            copy_turned(at, "b", b, 1, (1,))
                        if b.alive(U):
                            hold(act, f2_out[b.slot], 16 * b.use, pa)
                            hold(act, s["x1"], b.n - 1, pa)
                            copy_f2(b, 0)
                        if a.alive(U) or c.alive(U):
                            hold(act, s["stats"], at.n + 1, pa)
                        if a.alive(U):
                            hold(act, s["tp_h"], turns_before(at.back(1), "c"), pa)
                        for r in range(G):
                            if a.alive(U):
                                relu = nc.scalar.activation(h1[:, r, :], xin[:, a.slot, r, :], ACT.Relu,
                                                            bias=nm[:, at.slot, r:r + 1],
                                                            scale=rt[:, at.slot, r:r + 1])
                                if r % 2:
                                    relu.then_inc(s["h1_h"], 1)
                            if d.alive(U) and r == 1:
                                hold(act, s["unc"], d.n + 1, pa)
                                nc.scalar.activation(th[:, :], unc[:, :], ACT.Tanh).then_inc(s["tanh"], 1)
                        if b.alive(U):
                            copy_f2(b, 1)
                        if a.alive(U):
                            copy_turned(at, "a", a, 0)
                        if c.alive(U):
                            hold(act, h2_out[c.slot], 16 * c.use, pa)
                            for r in range(G):
                                last = nc.scalar.activation(h2[:, c.slot, r, :], x1[:, c.slot, r, :], ACT.Relu,
                                                            bias=nm[:, at.slot, G + r:G + r + 1],
                                                            scale=rt[:, at.slot, G + r:G + r + 1])
                            last.then_inc(s["h2"], 1)
                        if a.alive(U):
                            hold(act, f1_out[a.slot], 16 * a.use, pa)
                            hold(act, s["zm"], a.n - 1, pa)
                            for q in range(2):
                                hold(act, s["mma_h"], a.n * 2 + (q + 1), pa)
                                nc.scalar.activation(f1o[:, a.slot, 2 * q:2 * q + 2, 0:F2W],
                                                     mm[PAIR["a", q]][:, :, 0:F2W], ACT.Copy)\
                                    .then_inc(s["f1_h"], 1)
                        if c.alive(U):
                            copy_turned(at, "c", c, 2)
                        if d.alive(U):
                            hold(act, hl_out[d.slot], 16 * d.use, pa)
                            for r in range(G):
                                last = nc.scalar.activation(ho[:, d.slot, r, :], hr[:, r, :], ACT.Copy,
                                                            scale=fac[:, r:r + 1])
                            last.then_inc(s["ho"], 1)
                    pipeline(act, U, 3, unit)

                @block.vector
                def _(dve):
                    pv = ph.passed["dve"]
                    V = nc.vector
                    link = Chain(dve, s["ch"])
                    link(V.memset(st[:, :, :], 1.0))
                    link(V.memset(var[:, :], 1.0))

                    def x_stats(a):
                        hold(dve, x_in[a.slot], 16 * (a.use + 1), pv)
                        for r in range(G):
                            V.bn_stats(st[:, r, :], xin[:, a.slot, r, :])

                    x_stats(At(0, 0, 0))

                    def unit(at):
                        a, b, c, d = at, at.back(1), at.back(2), at.back(3)
                        link.restart()
                        if b.alive(U):
                            for q in range(2):
                                half = slice(2 * q, 2 * q + 2)
                                hold(dve, s["f1_h"], b.n * 2 + (q + 1), pv)
                                nz = link.go(V.tensor_tensor(z[:, half, :], f1o[:, b.slot, half, 0:D],
                                                             wide(rb1, D, 2), ALU.add))
                            link.need(nz)
                            V.tensor_scalar(zm[:, :, :], z[:, :, :], 0.0, None, ALU.min).then_inc(s["zm"], 1)
                        if b.alive(U):
                            hold(dve, s["exp"], b.n + 1, pv)
                            hold(dve, s["tp_h"], turns_before(at.back(1), "a"), pv)
                            V.scalar_tensor_tensor(g[:, :, :], zm[:, :, :], -1.0, z[:, :, :], ALU.add, ALU.max)\
                                .then_inc(s["g"], 1)
                        if d.alive(U):
                            hold(dve, s["ho"], d.n, pv)
                            for q in range(2):
                                hold(dve, s["mmc_h"], d.n * 2 + (q + 1), pv)
                                V.tensor_tensor(hr[:, 2 * q:2 * q + 2, :], mm[PAIR["c", q]][:, :, 0:F2W],
                                                wide(rbl, F2W, 2), ALU.add).then_inc(s["hr_h"], 1)
                            hold(dve, s["hr_h"], d.n * 2 + 2, pv)
                            V.tensor_scalar(em[:, :], hr[:, :, 258], -87.0, None, ALU.max).then_inc(s["em"], 1)
                        take(layernorm_stats(nc, link, st, mean[:, :], dm[:, :], var[:, 0:2 * G]))
                        if d.alive(U):
                            hold(dve, s["sq"], d.n + 1, pv)
                            link(V.tensor_scalar(var[:, 2 * G:3 * G], n2[:, :], 1e-24, None, ALU.max))
                        hold(dve, s["h1_h"], min_int(a.n * 2 - 2, 2 * U), pv)
                        hold(dve, s["h2"], c.n - 1, pv)
                        rsq = rt[:, at.slot, :]
                        take(rsqrt(nc, link, rsq, var[:, :], ra[:, :]))
                        if a.alive(U) or c.alive(U):
                            V.scalar_tensor_tensor(nm[:, at.slot, :], mean[:, :], -0.5, rsq[:, 0:2 * G],
                                                   ALU.mult, ALU.mult).then_inc(s["stats"], 1)
                        steps = magnitude(nc, link, fac[:, :], em[:, :], rsq[:, 2 * G:3 * G], un[:, :], unc[:, :],
                                          n2[:, :])
                        if d.alive(U):
                            take(steps)
                            dve.sem_inc(s["unc"], 1)
                            hold(dve, s["tanh"], d.n + 1, pv)
                            take(expmap_scale(nc, link, ga[:, :], th[:, :], un[:, :], unc[:, :], gb[:, :], gc[:, :]))
                            link(V.tensor_tensor(ga[:, :], ga[:, :], fac[:, :], ALU.mult))
                            hold(dve, x3_out[d.slot], 16 * d.use, pv)
                            hold(dve, s["oo"], d.n - 1, pv)
                            for r in range(G):
                                last = V.scalar_tensor_tensor(x3o[:, d.slot, r, :], hr[:, r, 0:D], ga[:, r:r + 1],
                                                              x1[:, d.slot, r, :], ALU.mult, ALU.add)
                            last.then_inc(s["x3"], 1)
                        if at.back(-1).alive(U):
                            x_stats(at.back(-1))
                        if b.alive(U):
                            hold(dve, s["x1"], b.n + 1, pv)
                            for r in range(G):
                                V.bn_stats(st[:, G + r, :], x1[:, b.slot, r, :])
                    pipeline(dve, U, 3, unit)
        deg_stack.close()

        def softmax_weights(table, piece, width, col_src, col_dst, scores, first=False):
            gathered = ExitStack()
            raw_s = sb(f"raw_s{Phase.count}", [P, T, width], on=gathered)
            raw_d = sb(f"raw_d{Phase.count}", [P, T, width], on=gathered)
            with Phase() as ph:
                got = ph.sb("got", [P, 2, CH, 2, width])
                ix = ph.sb("ix", [P, 2, CH, 7], I32)
                got_in, taken, ix_ready = gathered_in[0], ph.sem("taken"), ph.sem("ix_ready")
                view = table.rearrange("n (q w) -> (n q) w", w=width)
                with nc.Block() as block:
                    @block.gpsimd
                    def _(pool):
                        pp = ph.passed["pool"]
                        bound = pool.to_reg(N * piece - 1)

                        def chunk(at):
                            sl = at.slot
                            hold(pool, taken, at.n - 1, pp)
                            nc.gpsimd.tensor_copy(ix[:, sl, :, :], index[:, bass.ds(at.n * CH, CH), :])\
                                .then_inc(ix_ready, 1)
                            hold(pool, ix_ready, at.n + 1, pp)
                            for r in range(CH):
                                for k, col in ((0, col_src), (1, col_dst)):
                                    nc.gpsimd.indirect_dma_start(
                                        out=got[:, sl, r, k, :], out_offset=None, in_=view,
                                        in_offset=bass.IndirectOffsetOnAxis(ap=ix[:, sl, r, col:col + 1], axis=0),
                                        bounds_check=bound, oob_is_err=False).then_inc(got_in[sl].sem, 16)
                        pipeline(pool, NC, 0, chunk)

                    @block.vector
                    def _(dve):
                        def chunk(at):
                            sl = at.slot
                            hold(dve, got_in[sl], 32 * CH * (at.use + 1), ph.passed["dve"])
                            nc.vector.tensor_copy(raw_s[:, bass.ds(at.n * CH, CH), :], got[:, sl, :, 0, :])
                            nc.vector.tensor_copy(raw_d[:, bass.ds(at.n * CH, CH), :], got[:, sl, :, 1, :])\
                                .then_inc(taken, 1)
                        pipeline(dve, NC, 0, chunk)
                for k in range(2):
                    got_in[k].base += 32 * CH * ((NC + 1 - k) // 2)

            def by_chunk(a):
                return a.rearrange("p (c r) h -> p r c h", r=CH)

            with Phase() as ph:
                logit = ph.sb("logit", [P, CH, P])
                own = ph.sb("own", [P, CH, P])
                key = ph.sb("key", [P, CH, P])
                lt = ph.sb("lt", [P, CE])
                kt = ph.sb("kt", [P, CE])
                fwd = ph.sb("fwd", [P, CE])
                bwd = ph.sb("bwd", [P, CE])
                pen_s = ph.sb("pen_s", [P, CE])
                pen_l = ph.sb("pen_l", [P, CE])
                diag = ph.sb("diag", [P, 4, P])
                ones = ph.sb("ones", [P, P])
                xr = ph.sb("xr", [P, 4, P])
                eq = ph.sb("eq", [P, 4, P])
                mx = ph.sb("mx", [P, 4])
                both_mx = ph.sb("both_mx", [P, 2])
                ps_l = ph.ps("ps_l", [P, 1024])
                ps_k = ph.ps("ps_k", [P, 1024])
                ps_x = ph.ps("ps_x", [P, 4, P])
                s_ch, s_v, s_pe, s_a = ph.sem("s_ch"), ph.sem("s_v"), ph.sem("s_pe"), ph.sem("s_a")
                with nc.Block() as block:
                    @block.tensor
                    def _(pe):
                        pe.wait_ge(s_v, 1)
                        for r in range(CH):
                            nc.tensor.transpose(ps_l[:, r * P:(r + 1) * P], logit[:, r, :], ident[:, :])
                            last = nc.tensor.transpose(ps_k[:, r * P:(r + 1) * P], key[:, r, :], ident[:, :])
                        last.then_inc(s_pe, 1)
                        pe.wait_ge(s_v, 2)
                        nc.tensor.matmul(ps_x[:, :, :], ones[:, :], diag[:, :, :], start=True, stop=True)\
                            .then_inc(s_pe, 1)
                        pe.wait_ge(s_v, 3)
                        for r in range(CH):
                            last = nc.tensor.transpose(ps_l[:, r * P:(r + 1) * P], bwd[:, r * P:(r + 1) * P],
                                                       ident[:, :])
                        last.then_inc(s_pe, 1)

                    @block.scalar
                    def _(act):
                        act.wait_ge(s_v, 4)
                        nc.scalar.activation(w_edge[:, :, :], w_edge[:, :, :], ACT.Exp)
                        nc.scalar.activation(w_self[:, :, :], w_self[:, :, :], ACT.Exp).then_inc(s_a, 1)
                        act.wait_ge(s_a, 1)

                    @block.vector
                    def _(dve):
                        link = Chain(dve, s_ch)
                        V = nc.vector
                        link(V.memset(logit[:, :, :], -BIG))
                        link(V.memset(own[:, :, :], 0.0))
                        link(V.memset(key[:, :, :], -1.0))
                        link(V.memset(ones[:, :], 1.0))

                        def heads(a):
                            return a[:, :, 0:CQ].rearrange("p r (c h) -> p r c h", h=HQ)
                        dst_rc = dst_col[:, :].rearrange("p (c r) -> p r c", r=CH)
                        for h in range(HQ):
                            link(V.tensor_scalar(heads(key)[:, :, :, h], dst_rc, float(HQ), float(h),
                                                 ALU.mult, ALU.add))
                        if scores == "gat":
                            link(V.tensor_tensor(heads(logit), by_chunk(raw_s[:, :, 0:HQ]),
                                                 by_chunk(raw_d[:, :, HQ:2 * HQ]), ALU.add))
                            link(V.tensor_tensor(heads(own), by_chunk(raw_d[:, :, 0:HQ]),
                                                 by_chunk(raw_d[:, :, HQ:2 * HQ]), ALU.add))
                            for a in (logit, own):
                                link(V.scalar_tensor_tensor(a[:, :, 0:CQ], a[:, :, 0:CQ], 0.2, a[:, :, 0:CQ],
                                                            ALU.mult, ALU.max))
                        else:
                            for h in range(HQ):
                                link(V.tensor_tensor(heads(logit)[:, :, :, h],
                                                     raw_s[:, :, 0].rearrange("p (c r) -> p r c", r=CH),
                                                     raw_d[:, :, 1].rearrange("p (c r) -> p r c", r=CH), ALU.add))
                        if first:
                            link(V.tensor_tensor(norm[:, :], raw_s[:, :, 8], raw_d[:, :, 9], ALU.mult))
                            link(V.tensor_scalar(norm[:, :], norm[:, :], 1e-12, None, ALU.add))
                            take(rsqrt(nc, link, fwd[:, 0:T], norm[:, :], bwd[:, 0:T]))
                            link(V.tensor_tensor(norm[:, :], fwd[:, 0:T], ew[:, :], ALU.mult))
                        dve.sem_inc(s_v, 1)
                        dve.wait_ge(s_pe, 1)
                        link(V.tensor_copy(lt[:, :], ps_l[:, 0:CE]))
                        link(V.tensor_copy(kt[:, :], ps_k[:, 0:CE]))
                        link(V.memset(pen_s[:, 0:1], 0.0))
                        link(V.memset(pen_l[:, CE - 1:CE], 0.0))
                        link(V.tensor_tensor(fwd[:, 1:CE], kt[:, 1:CE], kt[:, 0:CE - 1], ALU.is_equal))
                        link(V.tensor_scalar(pen_s[:, 1:CE], fwd[:, 1:CE], -1.0, BIG, ALU.add, ALU.mult))
                        link(V.tensor_copy(pen_l[:, 0:CE - 1], pen_s[:, 1:CE]))
                        link(V.tensor_tensor_scan(fwd[:, :], pen_s[:, :], lt[:, :], -BIG, ALU.add, ALU.max))
                        link(V.tensor_tensor_scan(bwd[:, ::-1], pen_l[:, ::-1], fwd[:, ::-1], -BIG,
                                                  ALU.add, ALU.max))
                        ends = (bwd[:, 0:1], bwd[:, CE - 1:CE], kt[:, 0:1], kt[:, CE - 1:CE])
                        for k, e in enumerate(ends):
                            link(V.tensor_scalar(diag[:, k, :], ident[:, :], e, None, ALU.mult))
                        dve.sem_inc(s_v, 1)
                        dve.wait_ge(s_pe, 2)
                        link(V.tensor_copy(xr[:, :, :], ps_x[:, :, :]))
                        for k in range(2):
                            for m in range(2):
                                link(V.tensor_scalar(eq[:, 2 * k + m, :], xr[:, 2 + m, :], ends[2 + k], -1.0,
                                                     ALU.is_equal, ALU.add))
                                link(V.scalar_tensor_tensor(eq[:, 2 * k + m, :], eq[:, 2 * k + m, :], BIG,
                                                            xr[:, m, :], ALU.mult, ALU.add))
                        link(V.tensor_reduce(both_mx[:, :], eq[:, :, :].rearrange("p (k m) q -> p k (m q)", k=2),
                                             axis=AX.X, op=ALU.max))
                        for k in range(2):
                            link(V.tensor_scalar(lt[:, :], kt[:, :], ends[2 + k], -1.0, ALU.is_equal, ALU.add))
                            link(V.tensor_scalar(lt[:, :], lt[:, :], BIG, both_mx[:, k:k + 1], ALU.mult, ALU.add))
                            link(V.tensor_tensor(bwd[:, :], bwd[:, :], lt[:, :], ALU.max))
                        dve.sem_inc(s_v, 1)
                        dve.wait_ge(s_pe, 3)
                        top = fwd[:, :].rearrange("p (r q) -> p r q", r=CH)
                        link(V.tensor_copy(fwd[:, :], ps_l[:, 0:CE]))
                        if scores == "gat":
                            link(V.tensor_tensor(top[:, :, 0:CQ], top[:, :, 0:CQ], own[:, :, 0:CQ], ALU.max))
                        else:
                            link(V.tensor_scalar(fwd[:, :], fwd[:, :], -1e9, None, ALU.max))
                        for a, w in ((logit, w_edge), (own, w_self)):
                            link(V.tensor_tensor(a[:, :, 0:CQ], a[:, :, 0:CQ], top[:, :, 0:CQ], ALU.subtract))
                            link(V.tensor_copy(by_chunk(w[:, :, :]), heads(a)))
                        dve.sem_inc(s_v, 1)
            gathered.close()

        class EdgePass(Phase):

            def __init__(self, width, gathers, scatter):
                self.width, self.gathers, self.scatter = width, gathers, scatter

            def __enter__(self):
                Phase.__enter__(self)
                self.drow = self.sb("drow", [P, 2, G * P])
                self.sel = self.sb("sel", [P, 2, G, P])
                self.carry = self.sb("carry", [P, 2, G * P])
                self.msg = self.sb("msg", [P, 2, G, self.width])
                self.rows = self.sb("rows", [P, 2, G, self.width])
                self.ix = [self.sb(f"ix{k}", [P, 2, G], I32) for k in range(len(self.gathers))]
                self.ix_put = self.sb("ix_put", [P, 2, G], I32)
                self.got = [self.sb(f"got{k}", [P, 2, G, t.shape[1]]) for k, (t, c) in enumerate(self.gathers)]
                self.put = self.sb("put", [P, 2, G, self.scatter.shape[1]])
                self.warm = self.sb("warm", [P, 1])
                self.acc = [self.ps(f"acc{k}", [P, 512]) for k in range(2)]
                self.got_in = [gathered_in[k] for k in range(len(self.gathers))]
                self.put_out = scattered_out
                self.ctl_in = self.slots("ctl_in", 2)
                self.done = {k: self.sem(k) for k in ("ix0", "ix1", "msg", "acc", "rows", "used", "put", "start",
                                                      "ix_put", "warm", "ch")}
                return self

            def step(self, *names):
                for k in names:
                    self.done[k] = self.sem(k)

            def start_pool(self, pool):
                nc.gpsimd.memset(self.rows[:, :, :, :], 0.0)
                nc.gpsimd.memset(self.put[:, :, :, :], 0.0)
                nc.gpsimd.memset(self.carry[:, :, :], 0.0)
                nc.gpsimd.memset(self.warm[:, :], 0.0).then_inc(self.done["start"], 1)
                pool.wait_ge(self.done["start"], 1)

            def start_act(self, act):
                act.wait_ge(self.done["start"], 1)
                nc.scalar.activation(self.warm[:, :], self.warm[:, :], ACT.Exp).then_inc(self.done["warm"], 1)
                act.wait_ge(self.done["warm"], 1)

            def control(self, sp, at):
                ps = self.passed["sp"]
                if type(at.n) is int and at.n == 0:
                    sp.wait_ge(self.done["start"], 1)
                hold(sp, self.done["msg"], at.n - 1, ps)
                hold(sp, self.done["acc"], at.n * G - G, ps)
                group = bass.ds(at.n * G, G)
                sp.dma_start(self.drow[:, at.slot, :], DSTF[group, :].rearrange("t p -> (t p)")
                             .partition_broadcast(P)).then_inc(self.ctl_in[at.slot], 16)
                sp.dma_start(self.carry[P - 1:P, at.slot, :], CONT[group, :].rearrange("(a t) p -> a (t p)", a=1))\
                    .then_inc(self.ctl_in[at.slot], 16)

            def gather(self, pool, at, k, bound, free, count):
                pp, (table, col), done = self.passed["pool"], self.gathers[k], self.done[f"ix{k}"]
                hold(pool, free, count, pp)
                nc.gpsimd.tensor_copy(self.ix[k][:, at.slot, :], index[:, bass.ds(at.n * G, G), col])\
                    .then_inc(done, 1)
                hold(pool, done, at.n + 1, pp)
                for t in range(G):
                    nc.gpsimd.indirect_dma_start(
                        out=self.got[k][:, at.slot, t, :], out_offset=None, in_=table,
                        in_offset=bass.IndirectOffsetOnAxis(ap=self.ix[k][:, at.slot, t:t + 1], axis=0),
                        bounds_check=bound, oob_is_err=False).then_inc(self.got_in[k][at.slot].sem, 16)

            def gathered(self, eng, at, k, passed):
                hold(eng, self.got_in[k][at.slot], 16 * G * (at.use + 1), passed)

            def scatter_rows(self, pool, at, bound):
                d, pp = self.done, self.passed["pool"]
                hold(pool, self.put_out[at.slot], 16 * G * at.use, pp)
                nc.gpsimd.tensor_copy(self.ix_put[:, at.slot, :], index[:, bass.ds(at.n * G, G), 2])\
                    .then_inc(d["ix_put"], 1)
                hold(pool, d["ix_put"], at.n + 1, pp)
                hold(pool, d["put"], (at.n + 1) * self.puts, pp)
                for t in range(G):
                    nc.gpsimd.indirect_dma_start(
                        out=self.scatter, in_=self.put[:, at.slot, t, :], in_offset=None,
                        out_offset=bass.IndirectOffsetOnAxis(ap=self.ix_put[:, at.slot, t:t + 1], axis=0),
                        bounds_check=bound, oob_is_err=False).then_inc(self.put_out[at.slot].sem, 16)

            puts = 1

            def free_put(self, eng, at, passed):
                hold(eng, self.put_out[at.slot], 16 * G * at.use, passed)

            def end_pool(self, pool):
                for k in range(2):
                    hold(pool, self.put_out[k], 16 * G * ((NG + 1 - k) // 2), None)

            def __exit__(self, *err):
                for pair in (*self.got_in, self.put_out):
                    for k in range(2):
                        pair[k].base += 16 * G * ((NG + 1 - k) // 2)
                return Phase.__exit__(self, *err)

            def select(self, dve, at):
                hold(dve, self.ctl_in[at.slot], 32 * (at.use + 1), self.passed["dve"])
                nc.vector.tensor_tensor(self.sel[:, at.slot, :, :],
                                        self.drow[:, at.slot, :].rearrange("p (t q) -> p t q", t=G),
                                        dst_col[:, bass.ds(at.n * G, G)].unsqueeze(2).to_broadcast([P, G, P]),
                                        ALU.is_equal).then_inc(self.done["msg"], 1)

            def accumulate(self, pe, at, t):
                d, pp, sl = self.done, self.passed["pe"], at.slot
                tile = at.n * G + t
                if t == 0:
                    hold(pe, d["msg"], at.n + 1, pp)
                    hold(pe, self.ctl_in[sl], 32 * (at.use + 1), pp)
                hold(pe, d["rows"], tile - 1, pp)
                acc = self.acc[t % 2][:, 0:self.width]
                nc.tensor.matmul(acc, self.sel[:, sl, t, :], self.msg[:, sl, t, :], start=True, stop=False)
                if type(at.n) is int and tile == 0:
                    pe.wait_ge(d["start"], 1)
                hold(pe, d["rows"], tile, pp)
                before = self.rows[:, sl, t - 1, :] if t else self.rows[:, 1 - sl, G - 1, :]
                nc.tensor.matmul(acc, self.carry[:, sl, t * P:(t + 1) * P], before, start=False,
                                 stop=True).then_inc(d["acc"], 1)

            def take_rows(self, act, at, t):
                d, pa = self.done, self.passed["act"]
                hold(act, d["acc"], at.n * G + (t + 1), pa)
                nc.scalar.activation(self.rows[:, at.slot, t, :], self.acc[t % 2][:, 0:self.width],
                                     ACT.Copy).then_inc(d["rows"], 1)

        def turn(nc, rows2, bank):
            for k in range(KB):
                last = nc.tensor.transpose(bank[:, k, :], rows2[:, k * P:(k + 1) * P], ident[:, :])
            return last

        def product(acc, lhs, w):
            for k in range(KB):
                last = nc.tensor.matmul(acc, lhs[:, k, :], w[:, k, :], start=(k == 0), stop=(k == KB - 1))
            return last

        def heads(a, h):
            return a.rearrange("p t (h c) -> p t h c", h=h)

        def per_head(w, c):
            return w.unsqueeze(3).to_broadcast([P, G, w.shape[2], c])

        def of_group(w, at):
            return w[:, bass.ds(at.n * G, G), :]

        def on_tiles(row):
            return row[:, 0:D].unsqueeze(1).to_broadcast([P, G, D])

        def edge_rows(table, at):
            return table[bass.ds(at.n * (G * P), G * P), :].rearrange("(t p) w -> p t w", p=P)

        def gat_message(dve, ph, at):
            pv = ph.passed["dve"]
            ph.gathered(dve, at, 0, pv)
            hold(dve, ph.done["acc"], at.n * G - G, pv)
            w = of_group(w_edge, at)
            nc.vector.tensor_tensor(heads(ph.msg[:, at.slot, :, 0:D], HQ), heads(ph.got[0][:, at.slot, :, 0:D], HQ),
                                    per_head(w, D // HQ), ALU.mult)
            nc.vector.tensor_copy(ph.msg[:, at.slot, :, D:D + HQ], w)
            ph.select(dve, at)

        def gat_output(link, ph, at, o, own, den):
            V, rows = nc.vector, ph.rows[:, at.slot, :, :]
            no = link.go(V.tensor_tensor(heads(o, HQ), heads(own, HQ), per_head(of_group(w_self, at), D // HQ),
                                         ALU.mult))
            nd = link.go(V.scalar_tensor_tensor(den, rows[:, :, D:D + HQ], 1e-16, of_group(w_self, at),
                                                ALU.add, ALU.add))
            link.need(no)
            no = link.go(V.tensor_tensor(o, o, rows[:, :, 0:D], ALU.add))
            link.need(nd)
            nd = link.go(V.reciprocal(den, den))
            link.need(no)
            link.need(nd)
            link(V.tensor_tensor(heads(o, HQ), heads(o, HQ), per_head(den, D // HQ), ALU.mult))

        softmax_weights(F1, 17, 16, 3, 4, "gat", first=True)
        with EdgePass(D + HQ, [(F1, 0), (F1, 1)], F2) as ph:
            ph.step("zm", "exp", "g", "tp", "gt", "mm", "fe")
            ph.puts = G
            d = ph.done
            o = ph.sb("o", [P, G, D])
            zm = ph.sb("zm", [P, G, D])
            den = ph.sb("den", [P, G, HQ])
            g = ph.sb("g", [P, 2, G, D])
            gt = ph.sb("gt", [P, KB, P])
            tp = ph.ps("tp", [P, KB, P])
            mm = ph.ps("mm", [P, 512])
            fe_out = ph.slots("fe_out", 2)
            with nc.Block() as block:
                @block.gpsimd
                def _(pool):
                    ph.start_pool(pool)
                    bound = pool.to_reg(N - 1)

                    def group(at):
                        b, j = at.back(1), at.back(4)
                        if at.alive(NG):
                            ph.gather(pool, at, 0, bound, d["msg"], at.n - 1)
                        if b.alive(NG):
                            ph.gather(pool, b, 1, bound, d["used"], b.n - 1)
                        if j.alive(NG):
                            ph.scatter_rows(pool, j, bound)
                    pipeline(pool, NG, 4, group)
                    ph.end_pool(pool)

                @block.sync
                def _(sp):
                    def group(at):
                        if at.alive(NG):
                            ph.control(sp, at)
                        j = at.back(3)
                        if j.alive(NG):
                            hold(sp, d["put"], (j.n + 1) * G, ph.passed["sp"])
                            sp.dma_start(edge_rows(FE2, j), ph.put[:, j.slot, :, :]).then_inc(fe_out[j.slot], 16)
                    pipeline(sp, NG, 3, group)
                    for k in range(2):
                        sp.wait_ge(fe_out[k], 16 * ((NG + 1 - k) // 2))

                @block.vector
                def _(dve):
                    link = Chain(dve, d["ch"])
                    pv = ph.passed["dve"]
                    V = nc.vector

                    def group(at):
                        link.restart()
                        b = at.back(1)
                        if at.alive(NG):
                            gat_message(dve, ph, at)
                        if b.alive(NG):
                            hold(dve, d["rows"], (b.n + 1) * G, pv)
                            ph.gathered(dve, b, 1, pv)
                            gat_output(link, ph, b, o[:, :, :], ph.got[1][:, b.slot, :, 0:D], den[:, :, :])
                            link(V.tensor_tensor(o[:, :, :], o[:, :, :], on_tiles(rb1), ALU.add))
                            V.tensor_scalar(zm[:, :, :], o[:, :, :], 0.0, None, ALU.min).then_inc(d["zm"], 1)
                            dve.sem_inc(d["used"], 1)
                            hold(dve, d["exp"], b.n + 1, pv)
                            hold(dve, d["tp"], b.n * G - G, pv)
                            V.scalar_tensor_tensor(g[:, b.slot, :, :], zm[:, :, :], -1.0, o[:, :, :], ALU.add, ALU.max)\
                                .then_inc(d["g"], 1)
                    pipeline(dve, NG, 1, group)

                @block.tensor
                def _(pe):
                    pp = ph.passed["pe"]

                    def group(at):
                        c = at.back(2)
                        for t in range(G):
                            if at.alive(NG):
                                ph.accumulate(pe, at, t)
                            if c.alive(NG):
                                if t == 0:
                                    hold(pe, d["g"], c.n + 1, pp)
                                hold(pe, d["gt"], c.n * G + t, pp)
                                turn(nc, g[:, c.slot, t, :], tp).then_inc(d["tp"], 1)
                                hold(pe, d["gt"], c.n * G + (t + 1), pp)
                                hold(pe, d["put"], c.n * G + t, pp)
                                product(mm[:, 0:F2W], gt, w2).then_inc(d["mm"], 1)
                    pipeline(pe, NG, 2, group)

                @block.scalar
                def _(act):
                    pa = ph.passed["act"]
                    ph.start_act(act)

                    def group(at):
                        b, c = at.back(1), at.back(2)
                        if at.alive(NG):
                            hold(act, d["used"], at.n - 1, pa)
                        if c.alive(NG):
                            ph.free_put(act, c, pa)
                            hold(act, fe_out[c.slot], 16 * c.use, pa)
                        for t in range(G):
                            if at.alive(NG):
                                ph.take_rows(act, at, t)
                            if c.alive(NG):
                                hold(act, d["tp"], c.n * G + (t + 1), pa)
                                hold(act, d["mm"], c.n * G + t, pa)
                                nc.scalar.activation(gt[:, :, :], tp[:, :, :], ACT.Copy).then_inc(d["gt"], 1)
                                hold(act, d["mm"], c.n * G + (t + 1), pa)
                                nc.scalar.activation(ph.put[:, c.slot, t, :], mm[:, 0:F2W], ACT.Copy)\
                                    .then_inc(d["put"], 1)
                            if b.alive(NG) and t == 1:
                                hold(act, d["zm"], b.n + 1, pa)
                                nc.scalar.activation(zm[:, :, :], zm[:, :, :], ACT.Exp).then_inc(d["exp"], 1)
                    pipeline(act, NG, 2, group)

        softmax_weights(F2, 33, 8, 5, 6, "gat")
        with EdgePass(D + HQ, [(F2, 0), (x, 1)], H2) as ph:
            ph.step("x1", "stats")
            d = ph.done
            fe = ph.sb("fe", [P, 2, G, F2W])
            o = ph.sb("o", [P, G, D])
            x1 = ph.sb("x1", [P, 2, G, D])
            den = ph.sb("den", [P, G, HQ])
            st, mean, dm = ph.sb("st", [P, G, 6]), ph.sb("mean", [P, G]), ph.sb("dm", [P, G])
            var, ra = ph.sb("var", [P, G]), ph.sb("ra", [P, G])
            rt, nm = ph.sb("rt", [P, 2, G]), ph.sb("nm", [P, 2, G])
            fe_in, x1_out = ph.slots("fe_in", 2), ph.slots("x1_out", 2)
            with nc.Block() as block:
                @block.gpsimd
                def _(pool):
                    ph.start_pool(pool)
                    bound = pool.to_reg(N - 1)

                    def group(at):
                        b, j = at.back(1), at.back(3)
                        if at.alive(NG):
                            ph.gather(pool, at, 0, bound, d["msg"], at.n - 1)
                        if b.alive(NG):
                            ph.gather(pool, b, 1, bound, d["used"], b.n - 1)
                        if j.alive(NG):
                            ph.scatter_rows(pool, j, bound)
                    pipeline(pool, NG, 3, group)
                    ph.end_pool(pool)

                @block.sync
                def _(sp):
                    ps = ph.passed["sp"]

                    def group(at):
                        b, j = at.back(1), at.back(2)
                        if at.alive(NG):
                            ph.control(sp, at)
                        if b.alive(NG):
                            hold(sp, d["used"], b.n - 1, ps)
                            sp.dma_start(fe[:, b.slot, :, :], edge_rows(FE2, b)).then_inc(fe_in[b.slot], 16)
                        if j.alive(NG):
                            hold(sp, d["x1"], j.n + 1, ps)
                            sp.dma_start(edge_rows(XE1, j), x1[:, j.slot, :, :]).then_inc(x1_out[j.slot], 16)
                    pipeline(sp, NG, 2, group)
                    for k in range(2):
                        sp.wait_ge(x1_out[k], 16 * ((NG + 1 - k) // 2))

                @block.vector
                def _(dve):
                    link = Chain(dve, d["ch"])
                    pv = ph.passed["dve"]
                    V = nc.vector

                    def group(at):
                        link.restart()
                        b = at.back(1)
                        if at.alive(NG):
                            gat_message(dve, ph, at)
                        if b.alive(NG):
                            sl = b.slot
                            hold(dve, d["rows"], (b.n + 1) * G, pv)
                            hold(dve, fe_in[sl], 16 * (b.use + 1), pv)
                            ph.gathered(dve, b, 1, pv)
                            gat_output(link, ph, b, o[:, :, :], fe[:, sl, :, 0:D], den[:, :, :])
                            link(V.tensor_tensor(o[:, :, :], o[:, :, :], on_tiles(rb2), ALU.add))
                            hold(dve, x1_out[sl], 16 * b.use, pv)
                            hold(dve, d["put"], b.n - 1, pv)
                            V.tensor_tensor(x1[:, sl, :, :], o[:, :, :], ph.got[1][:, sl, :, :], ALU.add)\
                                .then_inc(d["x1"], 1)
                            hold(dve, d["x1"], b.n + 1, pv)
                            dve.sem_inc(d["used"], 1)
                            for t in range(G):
                                last = V.bn_stats(st[:, t, :], x1[:, sl, t, :])
                            link(last)
                            take(layernorm_stats(nc, link, st, mean[:, :], dm[:, :], var[:, :]))
                            take(rsqrt(nc, link, rt[:, sl, :], var[:, :], ra[:, :]))
                            V.scalar_tensor_tensor(nm[:, sl, :], mean[:, :], -0.5, rt[:, sl, :],
                                                   ALU.mult, ALU.mult).then_inc(d["stats"], 1)
                    pipeline(dve, NG, 1, group)

                @block.tensor
                def _(pe):
                    def group(at):
                        for t in range(G):
                            ph.accumulate(pe, at, t)
                    pipeline(pe, NG, 0, group)

                @block.scalar
                def _(act):
                    pa = ph.passed["act"]
                    ph.start_act(act)

                    def group(at):
                        if at.alive(NG):
                            hold(act, d["used"], at.n - 1, pa)
                            for t in range(G):
                                ph.take_rows(act, at, t)
                        b = at.back(1)
                        if b.alive(NG):
                            hold(act, d["stats"], b.n + 1, pa)
                            ph.free_put(act, b, pa)
                            sl = b.slot
                            for t in range(G):
                                last = nc.scalar.activation(ph.put[:, sl, t, :], x1[:, sl, t, :], ACT.Relu,
                                                            bias=nm[:, sl, t:t + 1], scale=rt[:, sl, t:t + 1])
                            last.then_inc(d["put"], 1)
                    pipeline(act, NG, 1, group)

        NH = 8
        with EdgePass(D + NH, [(H2, 0), (H2, 1)], HL) as ph:
            ph.step("tp", "ht", "kvm", "qm", "kv", "q", "score", "exp", "x2", "stats", "h", "tp3", "h3", "mm", "raw",
                    "hr", "sq", "xl")
            d = ph.done
            xe = ph.sb("xe", [P, 2, G, D])
            ht = ph.sb("ht", [P, 2, 4, P])
            kvs = ph.sb("kvs", [P, 2, G, 2 * D])
            qs = ph.sb("qs", [P, 2, G, D])
            pr = ph.sb("pr", [P, G, D])
            sc = ph.sb("sc", [P, G, NH])
            o = ph.sb("o", [P, G, D])
            x2 = ph.sb("x2", [P, 2, G, D])
            den = ph.sb("den", [P, G, NH])
            h = ph.sb("h", [P, 2, G, D])
            h3 = ph.sb("h3", [P, KB, P])
            raw = ph.sb("raw", [P, G, F2W])
            hr = ph.sb("hr", [P, G, F2W])
            sq = ph.sb("sq", [P, G, D])
            em, n2, fac = ph.sb("em", [P, G]), ph.sb("n2", [P, G]), ph.sb("fac", [P, G])
            st, mean, dm = ph.sb("st", [P, G, 6]), ph.sb("mean", [P, G]), ph.sb("dm", [P, G])
            var, ra = ph.sb("var", [P, 2 * G]), ph.sb("ra", [P, 2 * G])
            rt, nm = ph.sb("rt", [P, 2, 2 * G]), ph.sb("nm", [P, 2, G])
            tp = ph.ps("tp", [P, 4, P])
            kv = [ph.ps(f"kv{k}", [P, 2 * D]) for k in range(2)]
            qp = ph.ps("qp", [P, D])
            tp3 = ph.ps("tp3", [P, KB, P])
            mm = ph.ps("mm", [P, 512])
            xe_in, x2_out, he_out = ph.slots("xe_in", 2), ph.slots("x2_out", 2), ph.slots("he_out", 2)
            with nc.Block() as block:
                @block.gpsimd
                def _(pool):
                    ph.start_pool(pool)
                    bound = pool.to_reg(N - 1)

                    def group(at):
                        j = at.back(7)
                        if at.alive(NG):
                            for k in range(2):
                                ph.gather(pool, at, k, bound, d["tp"], at.n * G - G)
                        if j.alive(NG):
                            ph.scatter_rows(pool, j, bound)
                    pipeline(pool, NG, 7, group)
                    ph.end_pool(pool)

                @block.sync
                def _(sp):
                    ps = ph.passed["sp"]

                    def group(at):
                        b, e, f = at.back(1), at.back(4), at.back(5)
                        if b.alive(NG):
                            ph.control(sp, b)
                        c = at.back(2)
                        if c.alive(NG):
                            hold(sp, d["xl"], c.n - 1, ps)
                            sp.dma_start(xe[:, c.slot, :, :], edge_rows(XE1, c)).then_inc(xe_in[c.slot], 16)
                        if e.alive(NG):
                            hold(sp, d["x2"], e.n + 1, ps)
                            sp.dma_start(edge_rows(XE2, e), x2[:, e.slot, :, :]).then_inc(x2_out[e.slot], 16)
                        j = at.back(6)
                        if j.alive(NG):
                            hold(sp, d["put"], j.n + 1, ps)
                            sp.dma_start(edge_rows(HE2, j), ph.put[:, j.slot, :, 0:D]).then_inc(he_out[j.slot], 16)
                    pipeline(sp, NG, 6, group)
                    for k in range(2):
                        sp.wait_ge(x2_out[k], 16 * ((NG + 1 - k) // 2))
                        sp.wait_ge(he_out[k], 16 * ((NG + 1 - k) // 2))

                @block.tensor
                def _(pe):
                    pp = ph.passed["pe"]

                    def group(at):
                        c, e = at.back(2), at.back(4)
                        if at.alive(NG):
                            for k in range(2):
                                ph.gathered(pe, at, k, pp)
                        for t in range(G):
                            n = at.n * G + t
                            if at.alive(NG):
                                hold(pe, d["ht"], n, pp)
                                turn(nc, ph.got[0][:, at.slot, t, :], tp[:, 0:2, :])
                                turn(nc, ph.got[1][:, at.slot, t, :], tp[:, 2:4, :]).then_inc(d["tp"], 1)
                            if c.alive(NG):
                                ph.accumulate(pe, c, t)
                            if e.alive(NG):
                                if t == 0:
                                    hold(pe, d["h"], e.n + 1, pp)
                                hold(pe, d["h3"], e.n * G + t, pp)
                                turn(nc, h[:, e.slot, t, :], tp3).then_inc(d["tp3"], 1)
                            if at.alive(NG):
                                hold(pe, d["ht"], n + 1, pp)
                                hold(pe, d["kv"], n - 1, pp)
                                product(kv[t % 2][:, :], ht[:, t % 2, 0:2, :], wkv).then_inc(d["kvm"], 1)
                                hold(pe, d["q"], n, pp)
                                product(qp[:, :], ht[:, t % 2, 2:4, :], wq).then_inc(d["qm"], 1)
                            if e.alive(NG):
                                hold(pe, d["h3"], e.n * G + (t + 1), pp)
                                hold(pe, d["raw"], e.n * G + t, pp)
                                product(mm[:, 0:F2W], h3, wl).then_inc(d["mm"], 1)
                    pipeline(pe, NG, 4, group)

                @block.vector
                def _(dve):
                    link = Chain(dve, d["ch"])
                    pv = ph.passed["dve"]
                    V = nc.vector
                    link(V.memset(var[:, :], 1.0))

                    def group(at):
                        link.restart()
                        b, v, f = at.back(1), at.back(3), at.back(5)
                        if b.alive(NG):
                            hold(dve, d["kv"], (b.n + 1) * G, pv)
                            hold(dve, d["q"], (b.n + 1) * G, pv)
                            link(V.tensor_tensor(pr[:, :, :], kvs[:, b.slot, :, 0:D], qs[:, b.slot, :, :], ALU.mult))
                            link(V.tensor_reduce(sc[:, :, :], heads(pr[:, :, :], NH), axis=AX.X, op=ALU.add))
                            link(V.tensor_scalar(sc[:, :, :], sc[:, :, :], float((D // NH) ** -0.5), 5.0,
                                                 ALU.mult, ALU.min))
                            V.tensor_scalar(sc[:, :, :], sc[:, :, :], -5.0, None, ALU.max).then_inc(d["score"], 1)
                        if f.alive(NG):
                            hold(dve, d["raw"], (f.n + 1) * G, pv)
                            link(V.tensor_tensor(hr[:, :, :], raw[:, :, :],
                                                 rbl[:, :].unsqueeze(1).to_broadcast([P, G, F2W]), ALU.add))
                            V.tensor_scalar(em[:, :], hr[:, :, 258], -87.0, None, ALU.max).then_inc(d["hr"], 1)
                        if v.alive(NG):
                            hold(dve, d["rows"], (v.n + 1) * G, pv)
                            hold(dve, xe_in[v.slot], 16 * (v.use + 1), pv)
                            rows = ph.rows[:, v.slot, :, :]
                            nd = link.go(V.tensor_scalar(den[:, :, :], rows[:, :, D:D + NH], 1e-9, None, ALU.add))
                            link.need(nd)
                            link(V.reciprocal(den[:, :, :], den[:, :, :]))
                            link(V.tensor_tensor(heads(o[:, :, :], NH), heads(rows[:, :, 0:D], NH),
                                                 per_head(den[:, :, :], D // NH), ALU.mult))
                            dve.sem_inc(d["used"], 1)
                            hold(dve, x2_out[v.slot], 16 * v.use, pv)
                            hold(dve, d["h"], v.n - 1, pv)
                            V.tensor_tensor(x2[:, v.slot, :, :], o[:, :, :], xe[:, v.slot, :, :], ALU.add)\
                                .then_inc(d["x2"], 1)
                            hold(dve, d["x2"], v.n + 1, pv)
                            dve.sem_inc(d["xl"], 1)
                            for t in range(G):
                                last = V.bn_stats(st[:, t, :], x2[:, v.slot, t, :])
                            link(last)
                            take(layernorm_stats(nc, link, st, mean[:, :], dm[:, :], var[:, 0:G]))
                        if b.alive(NG):
                            hold(dve, d["exp"], b.n + 1, pv)
                            hold(dve, d["acc"], b.n * G - G, pv)
                            V.tensor_tensor(heads(ph.msg[:, b.slot, :, 0:D], NH), heads(kvs[:, b.slot, :, D:2 * D], NH),
                                            per_head(sc[:, :, :], D // NH), ALU.mult)
                            V.tensor_copy(ph.msg[:, b.slot, :, D:D + NH], sc[:, :, :])
                            ph.select(dve, b)
                        if f.alive(NG):
                            hold(dve, d["sq"], f.n + 1, pv)
                            link(V.tensor_scalar(var[:, G:2 * G], n2[:, :], 1e-24, None, ALU.max))
                        if v.alive(NG) or f.alive(NG):
                            rsq = rt[:, v.slot, :]
                            take(rsqrt(nc, link, rsq, var[:, :], ra[:, :]))
                        if v.alive(NG):
                            V.scalar_tensor_tensor(nm[:, v.slot, :], mean[:, :], -0.5, rsq[:, 0:G],
                                                   ALU.mult, ALU.mult).then_inc(d["stats"], 1)
                        if f.alive(NG):
                            take(magnitude(nc, link, fac[:, :], em[:, :], rsq[:, G:2 * G], None, None, None))
                            ph.free_put(dve, f, pv)
                            hold(dve, he_out[f.slot], 16 * f.use, pv)
                            for t in range(G):
                                last = V.tensor_scalar(ph.put[:, f.slot, t, :], hr[:, t, :], fac[:, t:t + 1], None,
                                                       ALU.mult)
                            last.then_inc(d["put"], 1)
                    pipeline(dve, NG, 5, group)

                @block.scalar
                def _(act):
                    pa = ph.passed["act"]
                    ph.start_act(act)

                    def group(at):
                        b, c, v, e, f = (at.back(k) for k in range(1, 6))
                        if c.alive(NG):
                            hold(act, d["used"], c.n - 1, pa)
                        if at.alive(NG):
                            hold(act, d["msg"], at.n - 1, pa)
                        for t in range(G):
                            n = at.n * G + t
                            if at.alive(NG):
                                hold(act, d["tp"], n + 1, pa)
                                hold(act, d["qm"], n - 1, pa)
                                nc.scalar.activation(ht[:, t % 2, :, :], tp[:, :, :], ACT.Copy).then_inc(d["ht"], 1)
                            if c.alive(NG):
                                ph.take_rows(act, c, t)
                            if e.alive(NG):
                                hold(act, d["tp3"], e.n * G + (t + 1), pa)
                                hold(act, d["mm"], e.n * G + t, pa)
                                nc.scalar.activation(h3[:, :, :], tp3[:, :, :], ACT.Copy).then_inc(d["h3"], 1)
                            if at.alive(NG):
                                hold(act, d["kvm"], n + 1, pa)
                                nc.scalar.activation(kvs[:, at.slot, t, :], kv[t % 2][:, :], ACT.Copy)\
                                    .then_inc(d["kv"], 1)
                                hold(act, d["qm"], n + 1, pa)
                                nc.scalar.activation(qs[:, at.slot, t, :], qp[:, :], ACT.Copy).then_inc(d["q"], 1)
                            if e.alive(NG):
                                hold(act, d["mm"], e.n * G + (t + 1), pa)
                                if t == 0:
                                    hold(act, d["hr"], e.n, pa)
                                nc.scalar.activation(raw[:, t, :], mm[:, 0:F2W], ACT.Copy).then_inc(d["raw"], 1)
                            if b.alive(NG) and t == 0:
                                hold(act, d["score"], b.n + 1, pa)
                                nc.scalar.activation(sc[:, :, :], sc[:, :, :], ACT.Exp).then_inc(d["exp"], 1)
                            if f.alive(NG) and t == 0:
                                hold(act, d["hr"], f.n + 1, pa)
                                nc.scalar.activation(em[:, :], em[:, :], ACT.Exp, scale=-1.0)
                                for r in range(G):
                                    last = nc.scalar.activation(sq[:, r, :], hr[:, r, 0:D], ACT.Square,
                                                                accum_out=n2[:, r:r + 1])
                                last.then_inc(d["sq"], 1)
                            if v.alive(NG) and t == 2:
                                hold(act, d["stats"], v.n + 1, pa)
                                hold(act, d["tp3"], v.n * G - G, pa)
                                for r in range(G):
                                    last = nc.scalar.activation(h[:, v.slot, r, :], x2[:, v.slot, r, :], ACT.Relu,
                                                                bias=nm[:, v.slot, r:r + 1], scale=rt[:, v.slot, r:r + 1])
                                last.then_inc(d["h"], 1)
                    pipeline(act, NG, 5, group)

        softmax_weights(HL, 33, 8, 5, 6, "hyperbolic")
        with EdgePass(D + 2, [(HL, 0)], X3) as ph:
            ph.step("hc", "sq", "unc", "tanh")
            d = ph.done
            xe = ph.sb("xe", [P, 2, G, D])
            he = ph.sb("he", [P, 2, G, D])
            hc = ph.sb("hc", [P, 2, G, D])
            sq = ph.sb("sq", [P, G, D])
            den, n2, th = ph.sb("den", [P, G]), ph.sb("n2", [P, 2, G]), ph.sb("th", [P, G])
            var, ra, rt = ph.sb("var", [P, G]), ph.sb("ra", [P, G]), ph.sb("rt", [P, G])
            un, unc = ph.sb("un", [P, G]), ph.sb("unc", [P, G])
            ga, gb, gc = ph.sb("ga", [P, G]), ph.sb("gb", [P, G]), ph.sb("gc", [P, G])
            he_in, xe_in, x3_out = ph.slots("he_in", 2), ph.slots("xe_in", 2), ph.slots("x3_out", 2)
            with nc.Block() as block:
                @block.gpsimd
                def _(pool):
                    ph.start_pool(pool)
                    bound = pool.to_reg(N - 1)

                    def group(at):
                        j = at.back(4)
                        if at.alive(NG):
                            ph.gather(pool, at, 0, bound, d["msg"], at.n - 1)
                        if j.alive(NG):
                            ph.scatter_rows(pool, j, bound)
                    pipeline(pool, NG, 4, group)
                    ph.end_pool(pool)

                @block.sync
                def _(sp):
                    ps = ph.passed["sp"]

                    def group(at):
                        b, j = at.back(1), at.back(3)
                        if at.alive(NG):
                            ph.control(sp, at)
                            hold(sp, d["hc"], at.n - 1, ps)
                            sp.dma_start(he[:, at.slot, :, :], edge_rows(HE2, at)).then_inc(he_in[at.slot], 16)
                        if b.alive(NG):
                            hold(sp, d["put"], b.n - 1, ps)
                            sp.dma_start(xe[:, b.slot, :, :], edge_rows(XE2, b)).then_inc(xe_in[b.slot], 16)
                        if j.alive(NG):
                            hold(sp, d["put"], j.n + 1, ps)
                            sp.dma_start(edge_rows(XE3, j), ph.put[:, j.slot, :, :]).then_inc(x3_out[j.slot], 16)
                    pipeline(sp, NG, 3, group)
                    for k in range(2):
                        sp.wait_ge(x3_out[k], 16 * ((NG + 1 - k) // 2))

                @block.vector
                def _(dve):
                    link = Chain(dve, d["ch"])
                    pv = ph.passed["dve"]
                    V = nc.vector

                    def group(at):
                        link.restart()
                        b, c = at.back(1), at.back(2)
                        if at.alive(NG):
                            ph.gathered(dve, at, 0, pv)
                            hold(dve, d["acc"], at.n * G - G, pv)
                            w = of_group(w_edge, at)
                            V.tensor_tensor(ph.msg[:, at.slot, :, 0:D], ph.got[0][:, at.slot, :, 0:D],
                                            w[:, :, 0:1].to_broadcast([P, G, D]), ALU.mult)
                            V.tensor_copy(ph.msg[:, at.slot, :, D:D + 2], w[:, :, 0:2])
                            ph.select(dve, at)
                        if c.alive(NG):
                            hold(dve, d["sq"], c.n + 1, pv)
                            link(V.tensor_scalar(var[:, :], n2[:, c.slot, :], 1e-36, None, ALU.max))
                            take(rsqrt(nc, link, rt[:, :], var[:, :], ra[:, :]))
                            link(V.tensor_tensor(un[:, :], n2[:, c.slot, :], rt[:, :], ALU.mult))
                            V.tensor_scalar(unc[:, :], un[:, :], 1e-15, None, ALU.max).then_inc(d["unc"], 1)
                        if b.alive(NG):
                            hold(dve, d["rows"], (b.n + 1) * G, pv)
                            hold(dve, he_in[b.slot], 16 * (b.use + 1), pv)
                            hold(dve, d["sq"], b.n - 1, pv)
                            link(V.tensor_scalar(den[:, :], ph.rows[:, b.slot, :, D], 1e-10, None, ALU.add))
                            link(V.reciprocal(den[:, :], den[:, :]))
                            for t in range(G):
                                last = V.scalar_tensor_tensor(hc[:, b.slot, t, :], ph.rows[:, b.slot, t, 0:D],
                                                              den[:, t:t + 1], he[:, b.slot, t, :],
                                                              ALU.mult, ALU.add)
                            last.then_inc(d["hc"], 1)
                        if c.alive(NG):
                            hold(dve, d["tanh"], c.n + 1, pv)
                            hold(dve, d["unc"], c.n + 1, pv)
                            take(expmap_scale(nc, link, ga[:, :], th[:, :], un[:, :], unc[:, :], gb[:, :], gc[:, :]))
                            ph.free_put(dve, c, pv)
                            hold(dve, x3_out[c.slot], 16 * c.use, pv)
                            hold(dve, xe_in[c.slot], 16 * (c.use + 1), pv)
                            for t in range(G):
                                last = V.scalar_tensor_tensor(ph.put[:, c.slot, t, :], hc[:, c.slot, t, :],
                                                              ga[:, t:t + 1], xe[:, c.slot, t, :],
                                                              ALU.mult, ALU.add)
                            last.then_inc(d["put"], 1)
                    pipeline(dve, NG, 2, group)

                @block.tensor
                def _(pe):
                    def group(at):
                        for t in range(G):
                            ph.accumulate(pe, at, t)
                    pipeline(pe, NG, 0, group)

                @block.scalar
                def _(act):
                    pa = ph.passed["act"]
                    ph.start_act(act)

                    def group(at):
                        b, c = at.back(1), at.back(2)
                        if at.alive(NG):
                            hold(act, d["hc"], at.n - 1, pa)
                        for t in range(G):
                            if at.alive(NG):
                                ph.take_rows(act, at, t)
                            if c.alive(NG) and t == 0:
                                hold(act, d["unc"], c.n + 1, pa)
                                nc.scalar.activation(th[:, :], unc[:, :], ACT.Tanh).then_inc(d["tanh"], 1)
                        if b.alive(NG):
                            hold(act, d["hc"], b.n + 1, pa)
                            hold(act, d["sq"], b.n, pa)
                            hold(act, d["unc"], b.n - 1, pa)
                            for t in range(G):
                                last = nc.scalar.activation(sq[:, t, :], hc[:, b.slot, t, :], ACT.Square,
                                                            accum_out=n2[:, b.slot, t:t + 1])
                            last.then_inc(d["sq"], 1)
                    pipeline(act, NG, 2, group)

        with EdgePass(D, [(X3, 0)], T7) as ph:
            ph.step("stats", "h", "tp", "at", "m6", "raw", "z", "tpz", "zt", "m7")
            ph.puts = G
            d = ph.done
            h = ph.sb("h", [P, 2, G, D])
            rowt = ph.sb("rowt", [P, KB, P])
            raw = ph.sb("raw", [P, 2, G, D])
            z = ph.sb("z", [P, 2, G, D])
            zt = ph.sb("zt", [P, KB, P])
            st, mean, dm = ph.sb("st", [P, G, 6]), ph.sb("mean", [P, G]), ph.sb("dm", [P, G])
            var, ra = ph.sb("var", [P, G]), ph.sb("ra", [P, G])
            rt, nm = ph.sb("rt", [P, 2, G]), ph.sb("nm", [P, 2, G])
            tp = ph.ps("tp", [P, KB, P])
            tpz = ph.ps("tpz", [P, KB, P])
            m6 = ph.ps("m6", [P, D])
            m7 = ph.ps("m7", [P, D])
            with nc.Block() as block:
                @block.gpsimd
                def _(pool):
                    ph.start_pool(pool)
                    bound = pool.to_reg(N - 1)

                    def group(at):
                        j = at.back(5)
                        if at.alive(NG):
                            ph.gather(pool, at, 0, bound, d["h"], at.n - 1)
                        if j.alive(NG):
                            ph.scatter_rows(pool, j, bound)
                    pipeline(pool, NG, 5, group)
                    ph.end_pool(pool)

                @block.sync
                def _(sp):
                    pipeline(sp, NG, 0, lambda at: ph.control(sp, at))

                @block.vector
                def _(dve):
                    link = Chain(dve, d["ch"])
                    pv = ph.passed["dve"]
                    V = nc.vector

                    def group(at):
                        link.restart()
                        b, e = at.back(1), at.back(3)
                        if b.alive(NG):
                            hold(dve, d["h"], b.n + 1, pv)
                            hold(dve, d["acc"], b.n * G - G, pv)
                            V.tensor_tensor(ph.msg[:, b.slot, :, :], h[:, b.slot, :, :],
                                            norm[:, bass.ds(b.n * G, G)].unsqueeze(2).to_broadcast([P, G, D]),
                                            ALU.mult)
                            ph.select(dve, b)
                        if e.alive(NG):
                            hold(dve, d["raw"], (e.n + 1) * G, pv)
                            hold(dve, d["tpz"], e.n * G - G, pv)
                            V.tensor_tensor(z[:, e.slot, :, :], raw[:, e.slot, :, :], on_tiles(rb6), ALU.add)\
                                .then_inc(d["z"], 1)
                        if at.alive(NG):
                            sl = at.slot
                            ph.gathered(dve, at, 0, pv)
                            hold(dve, d["h"], at.n - 1, pv)
                            for t in range(G):
                                last = V.bn_stats(st[:, t, :], ph.got[0][:, sl, t, :])
                            link(last)
                            take(layernorm_stats(nc, link, st, mean[:, :], dm[:, :], var[:, :]))
                            take(rsqrt(nc, link, rt[:, sl, :], var[:, :], ra[:, :]))
                            V.scalar_tensor_tensor(nm[:, sl, :], mean[:, :], -0.5, rt[:, sl, :],
                                                   ALU.mult, ALU.mult).then_inc(d["stats"], 1)
                    pipeline(dve, NG, 3, group)

                @block.tensor
                def _(pe):
                    pp = ph.passed["pe"]

                    def group(at):
                        b, c, e = at.back(1), at.back(2), at.back(3)
                        for t in range(G):
                            n, m = c.n * G + t, e.n * G + t
                            if b.alive(NG):
                                ph.accumulate(pe, b, t)
                            if c.alive(NG):
                                if t == 0:
                                    hold(pe, d["rows"], (c.n + 1) * G, pp)
                                hold(pe, d["at"], n, pp)
                                turn(nc, ph.rows[:, c.slot, t, :], tp).then_inc(d["tp"], 1)
                            if e.alive(NG):
                                hold(pe, d["z"], e.n + 1, pp)
                                hold(pe, d["zt"], m, pp)
                                turn(nc, z[:, e.slot, t, :], tpz).then_inc(d["tpz"], 1)
                            if c.alive(NG):
                                hold(pe, d["at"], n + 1, pp)
                                hold(pe, d["raw"], n, pp)
                                product(m6[:, :], rowt, w6).then_inc(d["m6"], 1)
                            if e.alive(NG):
                                hold(pe, d["zt"], m + 1, pp)
                                hold(pe, d["put"], m, pp)
                                product(m7[:, :], zt, w7).then_inc(d["m7"], 1)
                    pipeline(pe, NG, 3, group)

                @block.scalar
                def _(act):
                    pa = ph.passed["act"]
                    ph.start_act(act)

                    def group(at):
                        b, c, e = at.back(1), at.back(2), at.back(3)
                        if b.alive(NG):
                            hold(act, d["tp"], b.n * G - G, pa)
                        if c.alive(NG):
                            hold(act, d["z"], c.n - 1, pa)
                        if e.alive(NG):
                            ph.free_put(act, e, pa)
                        for t in range(G):
                            n, m = c.n * G + t, e.n * G + t
                            if b.alive(NG):
                                ph.take_rows(act, b, t)
                            if c.alive(NG):
                                hold(act, d["tp"], n + 1, pa)
                                hold(act, d["m6"], n, pa)
                                nc.scalar.activation(rowt[:, :, :], tp[:, :, :], ACT.Copy).then_inc(d["at"], 1)
                            if e.alive(NG):
                                hold(act, d["tpz"], m + 1, pa)
                                hold(act, d["m7"], m, pa)
                                nc.scalar.activation(zt[:, :, :], tpz[:, :, :], ACT.Relu).then_inc(d["zt"], 1)
                            if c.alive(NG):
                                hold(act, d["m6"], n + 1, pa)
                                nc.scalar.activation(raw[:, c.slot, t, :], m6[:, :], ACT.Copy).then_inc(d["raw"], 1)
                            if e.alive(NG):
                                hold(act, d["m7"], m + 1, pa)
                                nc.scalar.activation(ph.put[:, e.slot, t, :], m7[:, :], ACT.Copy)\
                                    .then_inc(d["put"], 1)
                            if at.alive(NG) and t == 2:
                                sl = at.slot
                                hold(act, d["stats"], at.n + 1, pa)
                                hold(act, d["msg"], at.n - 1, pa)
                                for r in range(G):
                                    last = nc.scalar.activation(h[:, sl, r, :], ph.got[0][:, sl, r, :], ACT.Relu,
                                                                bias=nm[:, sl, r:r + 1], scale=rt[:, sl, r:r + 1])
                                last.then_inc(d["h"], 1)
                    pipeline(act, NG, 3, group)

        with EdgePass(D, [(T7, 0)], out) as ph:
            ph.step("y", "tp", "yt", "mm", "raw", "xb")
            d = ph.done
            xe = ph.sb("xe", [P, 2, G, D])
            y = ph.sb("y", [P, 2, G, D])
            yt = ph.sb("yt", [P, KB, P])
            raw = ph.sb("raw", [P, 2, G, D])
            xb = ph.sb("xb", [P, G, D])
            tp = ph.ps("tp", [P, KB, P])
            mm = ph.ps("mm", [P, D])
            e_in = ph.slots("e_in", 2)
            with nc.Block() as block:
                @block.gpsimd
                def _(pool):
                    ph.start_pool(pool)
                    bound = pool.to_reg(N - 1)

                    def group(at):
                        j = at.back(5)
                        if at.alive(NG):
                            ph.gather(pool, at, 0, bound, d["msg"], at.n - 1)
                        if j.alive(NG):
                            ph.scatter_rows(pool, j, bound)
                    pipeline(pool, NG, 5, group)
                    ph.end_pool(pool)

                @block.sync
                def _(sp):
                    def group(at):
                        if at.alive(NG):
                            ph.control(sp, at)
                        c = at.back(2)
                        if c.alive(NG):
                            hold(sp, d["xb"], c.n - 1, ph.passed["sp"])
                            sp.dma_start(xe[:, c.slot, :, :], edge_rows(XE3, c)).then_inc(e_in[c.slot], 16)
                    pipeline(sp, NG, 2, group)

                @block.vector
                def _(dve):
                    pv = ph.passed["dve"]
                    V = nc.vector

                    def group(at):
                        b, e = at.back(1), at.back(3)
                        if at.alive(NG):
                            ph.gathered(dve, at, 0, pv)
                            hold(dve, d["acc"], at.n * G - G, pv)
                            V.tensor_tensor(ph.msg[:, at.slot, :, :], ph.got[0][:, at.slot, :, :],
                                            norm[:, bass.ds(at.n * G, G)].unsqueeze(2).to_broadcast([P, G, D]),
                                            ALU.mult)
                            ph.select(dve, at)
                        if b.alive(NG):
                            hold(dve, d["rows"], (b.n + 1) * G, pv)
                            hold(dve, d["tp"], b.n * G - G, pv)
                            V.tensor_tensor(y[:, b.slot, :, :], ph.rows[:, b.slot, :, :], on_tiles(rb7), ALU.add)\
                                .then_inc(d["y"], 1)
                        if e.alive(NG):
                            hold(dve, e_in[e.slot], 16 * (e.use + 1), pv)
                            hold(dve, d["put"], e.n, pv)
                            V.tensor_tensor(xb[:, :, :], xe[:, e.slot, :, :], on_tiles(rbp), ALU.add)\
                                .then_inc(d["xb"], 1)
                            hold(dve, d["xb"], e.n + 1, pv)
                            hold(dve, d["raw"], (e.n + 1) * G, pv)
                            ph.free_put(dve, e, pv)
                            V.tensor_tensor(ph.put[:, e.slot, :, :], raw[:, e.slot, :, :], xb[:, :, :], ALU.add)\
                                .then_inc(d["put"], 1)
                    pipeline(dve, NG, 3, group)

                @block.tensor
                def _(pe):
                    pp = ph.passed["pe"]

                    def group(at):
                        c = at.back(2)
                        for t in range(G):
                            n = c.n * G + t
                            if at.alive(NG):
                                ph.accumulate(pe, at, t)
                            if c.alive(NG):
                                hold(pe, d["y"], c.n + 1, pp)
                                hold(pe, d["yt"], n, pp)
                                turn(nc, y[:, c.slot, t, :], tp).then_inc(d["tp"], 1)
                                hold(pe, d["yt"], n + 1, pp)
                                hold(pe, d["raw"], n, pp)
                                product(mm[:, :], yt, wp).then_inc(d["mm"], 1)
                    pipeline(pe, NG, 2, group)

                @block.scalar
                def _(act):
                    pa = ph.passed["act"]
                    ph.start_act(act)

                    def group(at):
                        c = at.back(2)
                        if at.alive(NG):
                            hold(act, d["y"], at.n - 1, pa)
                        if c.alive(NG):
                            hold(act, d["put"], c.n - 1, pa)
                        for t in range(G):
                            n = c.n * G + t
                            if at.alive(NG):
                                ph.take_rows(act, at, t)
                            if c.alive(NG):
                                hold(act, d["tp"], n + 1, pa)
                                hold(act, d["mm"], n, pa)
                                nc.scalar.activation(yt[:, :, :], tp[:, :, :], ACT.Relu).then_inc(d["yt"], 1)
                                hold(act, d["mm"], n + 1, pa)
                                nc.scalar.activation(raw[:, c.slot, t, :], mm[:, :], ACT.Copy).then_inc(d["raw"], 1)
                    pipeline(act, NG, 2, group)


NAMES = ['x', 'src', 'dst', 'edge_weight', 'L0_gnn_W1', 'L0_gnn_a_src1', 'L0_gnn_a_dst1', 'L0_gnn_b1', 'L0_gnn_W2',
         'L0_gnn_a_src2', 'L0_gnn_a_dst2', 'L0_gnn_b2', 'L1_gnn_Wq', 'L1_gnn_Wk', 'L1_gnn_Wv', 'L2_gnn_W',
         'L2_gnn_b', 'L2_gnn_mag_w', 'L2_gnn_mag_b', 'L2_gnn_attn_w', 'L3_gnn_W6', 'L3_gnn_b6', 'L3_gnn_W7',
         'L3_gnn_b7', 'L3_gnn_Wp', 'L3_gnn_bp']


def kernel(**inputs):
    import numpy as np
    import concourse.bacc as bacc
    from concourse.bass_utils import run_bass_kernel_spmd

    nc = bacc.Bacc("TRN2", target_bir_lowering=False, num_devices=1)
    arrays, args = {}, []
    for name in NAMES:
        a = np.ascontiguousarray(inputs[name])
        arrays[f"in_{name}_dram"] = a
        args.append(nc.dram_tensor(f"in_{name}_dram", a.shape, mybir.dt.from_np(a.dtype), kind="ExternalInput").ap())
    shape = tuple(inputs["x"].shape)
    args.append(nc.dram_tensor("out_0_dram", shape, F32, kind="ExternalOutput").ap())
    gnn_program(nc, *args)
    r = run_bass_kernel_spmd(nc, [arrays], core_ids=[0])
    return r.results[0]["out_0_dram"]
```
